# Optimizing a Trainium2 kernel written in Bass

```python
import numpy as np
import jax
import jax.numpy as jnp

def _softmax(x, axis=-1):
    return jax.nn.softmax(x, axis=axis)

def _gelu(x):
    return jax.nn.gelu(x, approximate=True)

def _silu(x):
    return jax.nn.silu(x)

def _sigmoid(x):
    return jax.nn.sigmoid(x)

def _layernorm(x, axis=-1, eps=1e-05):
    m = jnp.mean(x, axis=axis, keepdims=True)
    v = jnp.var(x, axis=axis, keepdims=True)
    return (x - m) / jnp.sqrt(v + eps)

def _scatter_add(tgt, idx, src, axis=0):
    return tgt.at[idx].add(src)

def _segment_sum(src, seg, n):
    return jax.ops.segment_sum(src, seg, n)
kernel_name = 'mk_gps_d2_gnn_r8_f0ffe3'

def setup_inputs(seed: int=0):
    np.random.seed(seed)
    _w = jnp.asarray

    def _rec_inputs():
        import jax
        import jax.numpy as jnp
        _gk = jax.random.key(seed)
        x = -0.0003713 + 1 * jax.random.normal(jax.random.fold_in(_gk, 1), (3125, 512), jnp.float32)
        _s = jax.random.randint(jax.random.fold_in(_gk, 2), (25000,), 0, 3125, jnp.int32)
        _d = jax.random.randint(jax.random.fold_in(_gk, 3), (25000,), 0, 3125, jnp.int32)
        _loop = jnp.arange(3125, dtype=jnp.int32)
        src = jnp.concatenate([_s, _d, _loop])
        dst = jnp.concatenate([_d, _s, _loop])
        _o = jnp.argsort(dst, stable=True)
        src = src[_o]
        dst = dst[_o]
        edge_attr_32 = jax.random.uniform(jax.random.fold_in(_gk, 11), (53125, 32), jnp.float32, 0.0, 1)
        edge_attr_4 = 0.000937891 + 0.999965 * jax.random.normal(jax.random.fold_in(_gk, 12), (53125, 4), jnp.float32)
        return (x, src, dst, edge_attr_32, edge_attr_4)
    x, src, dst, edge_attr_32, edge_attr_4 = _rec_inputs()

    def _L0_gnn_setup():
        import jax, jax.numpy as jnp
        import numpy as np
        N = 3125
        M = 18750
        D = 512
        H = 8
        DK = 64
        DV = 64
        key = jax.random.key(seed)
        ks = jax.random.split(key, 8)
        x = jax.random.normal(ks[0], (N, D), jnp.float32)
        edge_index = jax.random.randint(ks[1], (2, M), 0, N).astype(jnp.int32)
        s_in = 1.0 / np.sqrt(D).astype(np.float32)
        s_ff = 1.0 / np.sqrt(H * DV).astype(np.float32)
        Wk = jax.random.normal(ks[2], (D, H * DK), jnp.float32) * s_in
        Wq = jax.random.normal(ks[3], (D, H * DK), jnp.float32) * s_in
        Wv = jax.random.normal(ks[4], (D, H * DV), jnp.float32) * s_in
        Wff = jax.random.normal(ks[5], (H * DV, D), jnp.float32) * s_ff
        bk = jnp.zeros((H * DK,), jnp.float32)
        bq = jnp.zeros((H * DK,), jnp.float32)
        bv = jnp.zeros((H * DV,), jnp.float32)
        bff = jnp.zeros((D,), jnp.float32)
        return {'x': x, 'edge_index': edge_index, 'Wk': Wk, 'bk': bk, 'Wq': Wq, 'bq': bq, 'Wv': Wv, 'bv': bv, 'Wff': Wff, 'bff': bff}
    _L0_gnn_all = _L0_gnn_setup()
    _L0_gnn_in = {k: v for k, v in _L0_gnn_all.items() if k in ('Wk', 'bk', 'Wq', 'bq', 'Wv', 'bv', 'Wff', 'bff')}
    del _L0_gnn_all

    def _L0_mix_setup():
        import jax, jax.numpy as jnp
        import numpy as np
        HEADS = 8
        EPS_LN = 1e-05
        EPS_NORM = 1e-08
        key = jax.random.key(seed)
        ks = jax.random.split(key, 3)
        B, N, C = (4, 1024, 512)
        x = jax.random.normal(ks[0], (B, N, C), dtype=jnp.float32)
        qkv_w = jax.random.normal(ks[1], (3 * C, C), dtype=jnp.float32) / np.sqrt(C)
        qkv_b = jnp.zeros((3 * C,), dtype=jnp.float32)
        out_w = jax.random.normal(ks[2], (C, C), dtype=jnp.float32) / np.sqrt(C)
        out_b = jnp.zeros((C,), dtype=jnp.float32)
        ln_gamma = jnp.ones((C,), dtype=jnp.float32)
        ln_beta = jnp.zeros((C,), dtype=jnp.float32)
        return {'x': x, 'qkv_w': qkv_w, 'qkv_b': qkv_b, 'out_w': out_w, 'out_b': out_b, 'ln_gamma': ln_gamma, 'ln_beta': ln_beta}
    _L0_mix_all = _L0_mix_setup()
    _L0_mix_in = {k: v for k, v in _L0_mix_all.items() if k in ('qkv_w', 'qkv_b', 'out_w', 'out_b', 'ln_gamma', 'ln_beta')}
    del _L0_mix_all

    def _L0_ffn_setup():
        import jax, jax.numpy as jnp
        import numpy as np
        NUM_EXPERTS = 8
        TOP_K = 2
        HIDDEN = 512
        INTERMEDIATE = 256
        BATCH, SEQ = (8, 256)
        key = jax.random.key(seed)
        ks = jax.random.split(key, 7)
        s_in = 1.0 / np.sqrt(HIDDEN)
        s_mid = 1.0 / np.sqrt(INTERMEDIATE)
        return {'x': jax.random.normal(ks[0], (BATCH, SEQ, HIDDEN), jnp.float32), 'Wg': jax.random.normal(ks[1], (HIDDEN, NUM_EXPERTS), jnp.float32) * s_in, 'bg': jnp.zeros((NUM_EXPERTS,), jnp.float32), 'W1': jax.random.normal(ks[2], (NUM_EXPERTS, HIDDEN, INTERMEDIATE), jnp.float32) * s_in, 'b1': jnp.zeros((NUM_EXPERTS, INTERMEDIATE), jnp.float32), 'W2': jax.random.normal(ks[3], (NUM_EXPERTS, INTERMEDIATE, HIDDEN), jnp.float32) * s_mid, 'b2': jnp.zeros((NUM_EXPERTS, HIDDEN), jnp.float32)}
    _L0_ffn_all = _L0_ffn_setup()
    _L0_ffn_in = {k: v for k, v in _L0_ffn_all.items() if k in ('Wg', 'bg', 'W1', 'b1', 'W2', 'b2')}
    del _L0_ffn_all

    def _L1_gnn_setup():
        import jax, jax.numpy as jnp
        import numpy as np
        import math
        N, E = (2500, 25000)
        MUL = 128
        D = MUL + 3 * MUL
        EDGE_ATTR = 32
        HID = 32
        LOG2 = math.log(2.0)

        def ssp(x):
            return jax.nn.softplus(x) - LOG2

        def split_irreps(x):
            return (x[:, :MUL], x[:, MUL:].reshape(x.shape[0], MUL, 3))

        def merge_irreps(x0, x1):
            return jnp.concatenate([x0, x1.reshape(x1.shape[0], MUL * 3)], axis=-1)

        def irrep_linear(x, W0, b0, W1):
            x0, x1 = split_irreps(x)
            y0 = x0 @ W0 + b0
            y1 = jnp.einsum('nuc,uv->nvc', x1, W1)
            return merge_irreps(y0, y1)
        key = jax.random.key(seed)
        ks = iter(jax.random.split(key, 32))

        def randn(shape, scale=1.0):
            return (scale * jax.random.normal(next(ks), shape)).astype(jnp.float32)
        inp = {'x': randn((N, D)), 'edge_sh': randn((E, 4)), 'edge_attr': jax.random.uniform(next(ks), (E, EDGE_ATTR), dtype=jnp.float32), 'edge_index': jax.random.randint(next(ks), (2, E), 0, N, dtype=jnp.int32), 'W_pre0': randn((MUL, MUL), MUL ** (-0.5)), 'b_pre0': jnp.zeros((MUL,), jnp.float32), 'W_pre1': randn((MUL, MUL), MUL ** (-0.5)), 'W_nd0': randn((MUL, MUL), MUL ** (-0.5)), 'b_nd0': jnp.zeros((MUL,), jnp.float32), 'W_nd1': randn((MUL, MUL), MUL ** (-0.5)), 'W_g1': randn((2 * MUL, 2 * MUL), (2 * MUL) ** (-0.5)), 'b_g1': jnp.zeros((2 * MUL,), jnp.float32), 'W_g2': randn((2 * MUL, 2 * MUL), (2 * MUL) ** (-0.5)), 'b_g2': jnp.zeros((2 * MUL,), jnp.float32), 'W_f1': randn((EDGE_ATTR, HID), EDGE_ATTR ** (-0.5)), 'W_f2': randn((HID, 4 * MUL), HID ** (-0.5)), 'W_s1': randn((3 * MUL, HID), (3 * MUL) ** (-0.5)), 'W_s2': randn((HID, 4 * MUL), HID ** (-0.5)), 'W_o0': randn((MUL, MUL), MUL ** (-0.5)), 'b_o0': jnp.zeros((MUL,), jnp.float32), 'W_o1': randn((MUL, MUL), MUL ** (-0.5))}
        return inp
    _L1_gnn_all = _L1_gnn_setup()
    _L1_gnn_in = {k: v for k, v in _L1_gnn_all.items() if k in ('W_pre0', 'b_pre0', 'W_pre1', 'W_nd0', 'b_nd0', 'W_nd1', 'W_g1', 'b_g1', 'W_g2', 'b_g2', 'W_f1', 'W_f2', 'W_s1', 'W_s2', 'W_o0', 'b_o0', 'W_o1')}
    del _L1_gnn_all

    def _L1_mix_setup():
        import jax, jax.numpy as jnp
        import numpy as np
        NUM_HEADS = 8
        EPS = 1e-06
        key = jax.random.key(seed)
        k1, k2, k3, k4 = jax.random.split(key, 4)
        B, N, C = (16, 512, 512)
        x = jax.random.normal(k1, (B, N, C), dtype=jnp.float32)
        W_qkv = jax.random.normal(k2, (3 * C, C), dtype=jnp.float32) * C ** (-0.5)
        W_proj = jax.random.normal(k3, (C, C), dtype=jnp.float32) * C ** (-0.5)
        b_proj = jax.random.normal(k4, (C,), dtype=jnp.float32) * 0.02
        return {'x': x, 'W_qkv': W_qkv, 'W_proj': W_proj, 'b_proj': b_proj}
    _L1_mix_all = _L1_mix_setup()
    _L1_mix_in = {k: v for k, v in _L1_mix_all.items() if k in ('W_qkv', 'W_proj', 'b_proj')}
    del _L1_mix_all

    def _L1_ffn_setup():
        import jax, jax.numpy as jnp
        import numpy as np
        B, S, D, E, O = (1024, 256, 512, 16, 512)
        key = jax.random.key(seed)
        k_x, k_wg, k_bg, k_we, k_be = jax.random.split(key, 5)
        scale_g = 1.0 / np.sqrt(D)
        scale_e = 1.0 / np.sqrt(D)
        return {'x': jax.random.normal(k_x, (B, S, D), dtype=jnp.float32), 'Wg': jax.random.uniform(k_wg, (D, E), jnp.float32, -scale_g, scale_g), 'bg': jax.random.uniform(k_bg, (E,), jnp.float32, -scale_g, scale_g), 'We': jax.random.uniform(k_we, (E, D, O), jnp.float32, -scale_e, scale_e), 'be': jax.random.uniform(k_be, (E, O), jnp.float32, -scale_e, scale_e)}
    _L1_ffn_all = _L1_ffn_setup()
    _L1_ffn_in = {k: v for k, v in _L1_ffn_all.items() if k in ('Wg', 'bg', 'We', 'be')}
    del _L1_ffn_all
    return {'x': x, 'src': src, 'dst': dst, 'edge_attr_32': edge_attr_32, 'edge_attr_4': edge_attr_4, 'L0_gnn_Wk': _L0_gnn_in['Wk'], 'L0_gnn_bk': _L0_gnn_in['bk'], 'L0_gnn_Wq': _L0_gnn_in['Wq'], 'L0_gnn_bq': _L0_gnn_in['bq'], 'L0_gnn_Wv': _L0_gnn_in['Wv'], 'L0_gnn_bv': _L0_gnn_in['bv'], 'L0_gnn_Wff': _L0_gnn_in['Wff'], 'L0_gnn_bff': _L0_gnn_in['bff'], 'L0_mix_qkv_w': _L0_mix_in['qkv_w'], 'L0_mix_qkv_b': _L0_mix_in['qkv_b'], 'L0_mix_out_w': _L0_mix_in['out_w'], 'L0_mix_out_b': _L0_mix_in['out_b'], 'L0_mix_ln_gamma': _L0_mix_in['ln_gamma'], 'L0_mix_ln_beta': _L0_mix_in['ln_beta'], 'L0_ffn_Wg': _L0_ffn_in['Wg'], 'L0_ffn_bg': _L0_ffn_in['bg'], 'L0_ffn_W1': _L0_ffn_in['W1'], 'L0_ffn_b1': _L0_ffn_in['b1'], 'L0_ffn_W2': _L0_ffn_in['W2'], 'L0_ffn_b2': _L0_ffn_in['b2'], 'L1_gnn_W_pre0': _L1_gnn_in['W_pre0'], 'L1_gnn_b_pre0': _L1_gnn_in['b_pre0'], 'L1_gnn_W_pre1': _L1_gnn_in['W_pre1'], 'L1_gnn_W_nd0': _L1_gnn_in['W_nd0'], 'L1_gnn_b_nd0': _L1_gnn_in['b_nd0'], 'L1_gnn_W_nd1': _L1_gnn_in['W_nd1'], 'L1_gnn_W_g1': _L1_gnn_in['W_g1'], 'L1_gnn_b_g1': _L1_gnn_in['b_g1'], 'L1_gnn_W_g2': _L1_gnn_in['W_g2'], 'L1_gnn_b_g2': _L1_gnn_in['b_g2'], 'L1_gnn_W_f1': _L1_gnn_in['W_f1'], 'L1_gnn_W_f2': _L1_gnn_in['W_f2'], 'L1_gnn_W_s1': _L1_gnn_in['W_s1'], 'L1_gnn_W_s2': _L1_gnn_in['W_s2'], 'L1_gnn_W_o0': _L1_gnn_in['W_o0'], 'L1_gnn_b_o0': _L1_gnn_in['b_o0'], 'L1_gnn_W_o1': _L1_gnn_in['W_o1'], 'L1_mix_W_qkv': _L1_mix_in['W_qkv'], 'L1_mix_W_proj': _L1_mix_in['W_proj'], 'L1_mix_b_proj': _L1_mix_in['b_proj'], 'L1_ffn_Wg': _L1_ffn_in['Wg'], 'L1_ffn_bg': _L1_ffn_in['bg'], 'L1_ffn_We': _L1_ffn_in['We'], 'L1_ffn_be': _L1_ffn_in['be']}

def reference(x, src, dst, edge_attr_32, edge_attr_4, L0_gnn_Wk, L0_gnn_bk, L0_gnn_Wq, L0_gnn_bq, L0_gnn_Wv, L0_gnn_bv, L0_gnn_Wff, L0_gnn_bff, L0_mix_qkv_w, L0_mix_qkv_b, L0_mix_out_w, L0_mix_out_b, L0_mix_ln_gamma, L0_mix_ln_beta, L0_ffn_Wg, L0_ffn_bg, L0_ffn_W1, L0_ffn_b1, L0_ffn_W2, L0_ffn_b2, L1_gnn_W_pre0, L1_gnn_b_pre0, L1_gnn_W_pre1, L1_gnn_W_nd0, L1_gnn_b_nd0, L1_gnn_W_nd1, L1_gnn_W_g1, L1_gnn_b_g1, L1_gnn_W_g2, L1_gnn_b_g2, L1_gnn_W_f1, L1_gnn_W_f2, L1_gnn_W_s1, L1_gnn_W_s2, L1_gnn_W_o0, L1_gnn_b_o0, L1_gnn_W_o1, L1_mix_W_qkv, L1_mix_W_proj, L1_mix_b_proj, L1_ffn_Wg, L1_ffn_bg, L1_ffn_We, L1_ffn_be):
    import jax
    import jax.numpy as jnp

    def _L0_gnn_ref(x, edge_index, Wk, bk, Wq, bq, Wv, bv, Wff, bff):
        import jax, jax.numpy as jnp
        import numpy as np
        N = 3125
        M = 18750
        D = 512
        H = 8
        DK = 64
        DV = 64
        K = (x @ Wk + bk).reshape(-1, H, DK)
        Q = (x @ Wq + bq).reshape(-1, H, DK)
        V = (x @ Wv + bv).reshape(-1, H, DV)
        senders, receivers = (edge_index[0], edge_index[1])
        att = jnp.einsum('mhd,mhd->mh', Q[receivers], K[senders]) / np.sqrt(DK).astype(np.float32)
        att = jnp.exp(att + 3.0 - att.max())
        ssum = jax.ops.segment_sum(att, receivers, num_segments=N)
        denom = ssum[receivers]
        att = jnp.where(denom == 0, 0.0, att / jnp.where(denom == 0, 1.0, denom))
        msg = att[..., None] * V[senders]
        agg = jax.ops.segment_sum(msg, receivers, num_segments=N)
        return agg.reshape(-1, H * DV) @ Wff + bff

    def _L0_mix_ref(x, qkv_w, qkv_b, out_w, out_b, ln_gamma, ln_beta):
        import jax, jax.numpy as jnp
        import numpy as np
        HEADS = 8
        EPS_LN = 1e-05
        EPS_NORM = 1e-08
        B, N, C = x.shape
        h = HEADS
        d = C // h
        residual = x
        mu = jnp.mean(x, axis=-1, keepdims=True)
        var = jnp.var(x, axis=-1, keepdims=True)
        xn = (x - mu) / jnp.sqrt(var + EPS_LN) * ln_gamma + ln_beta
        qkv = xn @ qkv_w.T + qkv_b
        qkv = qkv.reshape(B, N, 3, h, d).transpose(2, 0, 3, 1, 4)
        q, k, v = (qkv[0], qkv[1], qkv[2])
        q = jax.nn.elu(q) + 1.0
        k = jax.nn.elu(k) + 1.0
        kv = jnp.einsum('bhnd,bhne->bhde', k, v)
        k_sum = jnp.sum(k, axis=2)
        out = jnp.einsum('bhnd,bhde->bhne', q, kv)
        normalizer = jnp.einsum('bhnd,bhd->bhn', q, k_sum)
        out = out / (normalizer[..., None] + EPS_NORM)
        out = out.transpose(0, 2, 1, 3).reshape(B, N, C)
        out = out @ out_w.T + out_b
        return out + residual

    def _L0_ffn_ref(x, Wg, bg, W1, b1, W2, b2):
        import jax, jax.numpy as jnp
        import numpy as np
        NUM_EXPERTS = 8
        TOP_K = 2
        HIDDEN = 512
        INTERMEDIATE = 256
        BATCH, SEQ = (8, 256)
        B, S, H = x.shape
        xf = x.reshape(B * S, H)
        logits = xf @ Wg + bg
        probs = jax.nn.softmax(logits, axis=-1)
        _, top_idx = jax.lax.top_k(probs, TOP_K)
        mask = jnp.any(top_idx[:, :, None] == jnp.arange(NUM_EXPERTS)[None, None, :], axis=1)
        comb = probs * mask.astype(probs.dtype)
        out = jnp.zeros_like(xf)
        for e in range(NUM_EXPERTS):
            h = jax.nn.gelu(xf @ W1[e] + b1[e])
            y = h @ W2[e] + b2[e]
            out = out + comb[:, e:e + 1] * y
        return out.reshape(B, S, H)

    def _L1_gnn_ref(x, edge_sh, edge_attr, edge_index, W_pre0, b_pre0, W_pre1, W_nd0, b_nd0, W_nd1, W_g1, b_g1, W_g2, b_g2, W_f1, W_f2, W_s1, W_s2, W_o0, b_o0, W_o1):
        import jax, jax.numpy as jnp
        import numpy as np
        import math
        N, E = (2500, 25000)
        MUL = 128
        D = MUL + 3 * MUL
        EDGE_ATTR = 32
        HID = 32
        LOG2 = math.log(2.0)

        def ssp(x):
            return jax.nn.softplus(x) - LOG2

        def split_irreps(x):
            return (x[:, :MUL], x[:, MUL:].reshape(x.shape[0], MUL, 3))

        def merge_irreps(x0, x1):
            return jnp.concatenate([x0, x1.reshape(x1.shape[0], MUL * 3)], axis=-1)

        def irrep_linear(x, W0, b0, W1):
            x0, x1 = split_irreps(x)
            y0 = x0 @ W0 + b0
            y1 = jnp.einsum('nuc,uv->nvc', x1, W1)
            return merge_irreps(y0, y1)
        edge_dst, edge_src = (edge_index[0], edge_index[1])
        old_x = x
        pre = irrep_linear(x, W_pre0, b_pre0, W_pre1)
        p0, p1 = split_irreps(pre)
        pd0 = p0[edge_dst]
        ip1 = jnp.einsum('eum,eum->eu', p1[edge_dst], p1[edge_src]) / 3.0
        s0 = jnp.concatenate([pd0, pd0, ip1], axis=-1)
        x0, x1 = split_irreps(x)
        n1 = jnp.sqrt(jnp.sum(x1 * x1, axis=-1) / 3.0)
        g = jax.nn.silu(jnp.concatenate([x0, n1], -1) @ W_g1 + b_g1) @ W_g2 + b_g2
        xg = merge_irreps(g[:, :MUL], x1 * g[:, MUL:, None])
        x = irrep_linear(xg, W_nd0, b_nd0, W_nd1)
        self_x = x
        w = ssp(edge_attr @ W_f1) @ W_f2 * (ssp(s0 @ W_s1) @ W_s2)
        w1, w2, w3, w4 = jnp.split(w, 4, axis=-1)
        x0e, x1e = split_irreps(x[edge_src])
        sh0, sh1 = (edge_sh[:, 0], edge_sh[:, 1:4])
        out0 = w1 * x0e * sh0[:, None] + w4 * (jnp.einsum('eum,em->eu', x1e, sh1) / jnp.sqrt(3.0))
        out1 = w2[:, :, None] * x0e[:, :, None] * sh1[:, None, :] + w3[:, :, None] * x1e * sh0[:, None, None]
        edge_feat = merge_irreps(out0, out1)
        out = jax.ops.segment_sum(edge_feat, edge_dst, num_segments=old_x.shape[0])
        out = out + self_x
        out = irrep_linear(out, W_o0, b_o0, W_o1)
        return out + old_x

    def _L1_mix_ref(x, W_qkv, W_proj, b_proj):
        import jax, jax.numpy as jnp
        import numpy as np
        NUM_HEADS = 8
        EPS = 1e-06
        B, N, C = x.shape
        H = NUM_HEADS
        E = C // H
        scale = E ** (-0.5)
        qkv = (x @ W_qkv.T).reshape(B, N, 3, H, E)
        q, k, v = (qkv[:, :, 0], qkv[:, :, 1], qkv[:, :, 2])
        q_ = jax.nn.relu(q) + scale
        k_ = jax.nn.relu(k) + scale
        kv = jnp.einsum('bnhe,bnhf->bhef', k_, v)
        k_sum = jnp.sum(k_, axis=1)
        z = 1.0 / (jnp.einsum('bnhe,bhe->bnh', q_, k_sum) + EPS)
        out = jnp.einsum('bnhe,bhef->bnhf', q_, kv) * z[..., None]
        out = out.reshape(B, N, C)
        return out @ W_proj.T + b_proj

    def _L1_ffn_ref(x, Wg, bg, We, be):
        import jax, jax.numpy as jnp
        import numpy as np
        B, S, D, E, O = (1024, 256, 512, 16, 512)
        scores = jax.nn.softmax(jnp.mean(x, axis=1) @ Wg + bg, axis=-1)
        idx = jnp.argmax(scores, axis=-1)
        gate = jnp.take_along_axis(scores, idx[:, None], axis=-1)
        W_sel = We[idx]
        b_sel = be[idx]
        y = jnp.einsum('bsd,bdo->bso', x, W_sel) + b_sel[:, None, :]
        return gate[:, :, None] * y
    edge_index = jnp.stack([src, dst])
    xn = _layernorm(x, axis=-1)
    x = x + _L0_gnn_ref(xn, edge_index, L0_gnn_Wk, L0_gnn_bk, L0_gnn_Wq, L0_gnn_bq, L0_gnn_Wv, L0_gnn_bv, L0_gnn_Wff, L0_gnn_bff) + _L0_mix_ref(xn[None], L0_mix_qkv_w, L0_mix_qkv_b, L0_mix_out_w, L0_mix_out_b, L0_mix_ln_gamma, L0_mix_ln_beta)[0]
    x = x + _L0_ffn_ref(_layernorm(x, axis=-1)[None], L0_ffn_Wg, L0_ffn_bg, L0_ffn_W1, L0_ffn_b1, L0_ffn_W2, L0_ffn_b2)[0]
    xn = _layernorm(x, axis=-1)
    x = x + _L1_gnn_ref(xn, edge_attr_4, edge_attr_32, edge_index, L1_gnn_W_pre0, L1_gnn_b_pre0, L1_gnn_W_pre1, L1_gnn_W_nd0, L1_gnn_b_nd0, L1_gnn_W_nd1, L1_gnn_W_g1, L1_gnn_b_g1, L1_gnn_W_g2, L1_gnn_b_g2, L1_gnn_W_f1, L1_gnn_W_f2, L1_gnn_W_s1, L1_gnn_W_s2, L1_gnn_W_o0, L1_gnn_b_o0, L1_gnn_W_o1) + _L1_mix_ref(xn[None], L1_mix_W_qkv, L1_mix_W_proj, L1_mix_b_proj)[0]
    x = x + _L1_ffn_ref(_layernorm(x, axis=-1)[None], L1_ffn_Wg, L1_ffn_bg, L1_ffn_We, L1_ffn_be)[0]
    return x

_drawn_inputs = setup_inputs


def setup_inputs(seed=0):
    import zlib

    import numpy as np

    out = dict(_drawn_inputs(seed))
    spreads = {'L0_gnn_bk': (0.0, 2.0),
     'L0_gnn_bq': (0.0, 0.428),
     'L0_gnn_bv': (0.0, 0.1),
     'L0_gnn_bff': (0.0, 0.1),
     'L0_mix_qkv_b': (0.0, 0.1),
     'L0_mix_out_b': (0.0, 0.1),
     'L0_mix_ln_gamma': (1.0, 0.6),
     'L0_mix_ln_beta': (0.0, 0.1),
     'L0_ffn_bg': (0.0, 0.302),
     'L0_ffn_b1': (0.0, 0.545),
     'L0_ffn_b2': (0.0, 0.362),
     'L1_gnn_b_pre0': (0.0, 0.567),
     'L1_gnn_b_nd0': (0.0, 0.3),
     'L1_gnn_b_g1': (0.0, 0.328),
     'L1_gnn_b_g2': (0.0, 0.1),
     'L1_gnn_b_o0': (0.0, 0.546)}
    factors = {'L1_mix_b_proj': 8.0,
     'L1_ffn_Wg': 4.399,
     'L1_ffn_bg': 8.0,
     'L1_ffn_We': 4.496,
     'L1_ffn_be': 63.429}
    for name, (base, spread) in spreads.items():
        noise = np.random.default_rng([zlib.crc32(name.encode()), seed]).standard_normal(out[name].shape)
        drawn = base * np.exp(spread * noise) if base else spread * noise
        out[name] = jnp.asarray(drawn.astype(out[name].dtype))
    for name, factor in factors.items():
        out[name] = (out[name] * factor).astype(out[name].dtype)
    return out
```

```python
from contextlib import ExitStack

import concourse.bass as bass
from concourse import mybir

F32 = mybir.dt.float32
I32 = mybir.dt.int32
BF16 = mybir.dt.bfloat16
ALU = mybir.AluOpType
ACT = mybir.ActivationFunctionType
AX = mybir.AxisListType.X
RMAX = bass.bass_isa.ReduceOp.max

P = 128
N = 3125
D = 512
NT = -(-N // P)
NP = NT * P
E = 53125
EU = 16
ET = -(-E // (P * EU)) * EU
EB = ET // EU
EH = EU // 2
U = 5
NB = NT // U
H = 8
DH = D // H
KC = D // P
ACCW = D + H
SPARE = NP
ACCR = NP + P
NACC = 2
QF = 256
NX0 = 8
NX1 = 16
HID = 32
STATS = 7
LEAD_STEPS = 5
DW = 3 * P + HID
SW = 3 * P + D


def need(eng, sem, value):
    if isinstance(value, int) and value <= 0:
        return
    eng.wait_ge(sem, value)


def last_tile(n):
    return isinstance(n, int) and n == NT - 1


def last_pass(b):
    return isinstance(b, int) and b == EB - 1


def passes(eng, count, body):
    body(0)
    if count > 2:
        with eng.Fori(1, count - 1) as i:
            body(i)
    body(count - 1)


class Stage:

    def __init__(self, nc, name):
        self.nc, self.name, self.ctx, self.sems = nc, name, ExitStack(), []

    def __enter__(self):
        self.ctx.__enter__()
        return self

    def __exit__(self, *a):
        if self.sems:
            self.nc.clear_and_free_semaphores(self.sems)
            self.nc.all_engine_barrier()
        return self.ctx.__exit__(*a)

    def sb(self, name, shape, dt=F32):
        return self.ctx.enter_context(self.nc.sbuf_tensor(f"{self.name}_{name}", shape, dt))

    def ps(self, name, shape, dt=F32):
        return self.ctx.enter_context(self.nc.psum_tensor(f"{self.name}_{name}", shape, dt))

    def sem(self, name):
        self.sems.append(self.nc.alloc_semaphore(name=f"{self.name}_{name}"))
        return self.sems[-1]


class Steps:

    def __init__(self, eng, sem, per_pass):
        self.eng, self.sem, self.per_pass, self.base, self.k = eng, sem, per_pass, 0, 0

    def begin(self, i):
        self.base, self.k = i * self.per_pass, 0

    def did(self, ins):
        self.k += 1
        ins.then_inc(self.sem, 1)

    def wait(self):
        self.eng.wait_ge(self.sem, self.base + self.k)

    def end(self):
        assert self.k == self.per_pass, (self.k, self.per_pass)


def norm_factors(vec, s_step, at, keep, tmp, eps=1e-5):
    even, odd = keep.stats[:, :, 1], keep.stats[:, :, 4]
    vec.tensor_tensor(keep.mean[:], even, odd, ALU.add).then_inc(s_step, 1)
    vec.tensor_tensor(tmp[:, 0, :], even, odd, ALU.subtract).then_inc(s_step, 1)
    vec.tensor_tensor(tmp[:, 1, :], keep.stats[:, :, 2], keep.stats[:, :, 5], ALU.add).then_inc(s_step, 1)
    vec.wait_ge(s_step, at + 3)
    vec.tensor_scalar(keep.mean[:], keep.mean[:], 0.5, None, ALU.mult).then_inc(s_step, 1)
    vec.scalar_tensor_tensor(tmp[:, 0, :], tmp[:, 0, :], 0.25, tmp[:, 0, :], ALU.mult, ALU.mult).then_inc(s_step, 1)
    vec.tensor_scalar(tmp[:, 1, :], tmp[:, 1, :], 1.0 / D, eps, ALU.mult, ALU.add).then_inc(s_step, 1)
    vec.wait_ge(s_step, at + 6)
    vec.tensor_tensor(keep.rstd[:], tmp[:, 0, :], tmp[:, 1, :], ALU.add).then_inc(s_step, 1)
    return at + STATS


def lead_rows(vec, s_t, node, count, spare, go, ints):
    vec.tensor_scalar(go[:, 0, :], count[:], 1.0, None, ALU.min).then_inc(s_t, 1)
    vec.tensor_scalar(go[:, 1, :], node[:], -1.0, spare[:], ALU.mult, ALU.add).then_inc(s_t, 1)
    vec.wait_ge(s_t, 2)
    vec.tensor_tensor(go[:, 0, :], go[:, 0, :], go[:, 1, :], ALU.mult).then_inc(s_t, 1)
    vec.wait_ge(s_t, 3)
    vec.tensor_tensor(go[:, 0, :], go[:, 0, :], node[:], ALU.add).then_inc(s_t, 1)
    vec.wait_ge(s_t, 4)
    vec.tensor_copy(ints[:], go[:, 0, :]).then_inc(s_t, 1)


def clear_sums(act, s_z, zero, acc, width):
    for rows in acc:
        rows = rows.rearrange("(p r) w -> p (r w)", p=P)
        for r in range(0, ACCR // P, 2):
            act.dma_start(rows[:, r * width:(r + 2) * width], zero[:, 0:2 * width]).then_inc(s_z, 16)
    return 16 * NACC * (ACCR // P // 2)


def load_consts(nc, io, keep):
    with Stage(nc, "consts") as s:
        ints = s.sb("ints", [P, 4, ET], I32)
        digits, lines = s.sb("digits", [P, 2, 2, ET], I32), s.sb("lines", [P, 2, 2, ET], BF16)
        tmp = s.sb("tmp", [P, 2, NT])
        s_c, s_i, s_f, s_w, s_st, s_v, s_r = (s.sem(n) for n in (
            "consts", "ints", "floats", "row_out", "stats", "steps", "powers"))
        s_x = [s.sem(f"x{b}") for b in range(NB)]
        with nc.Block() as block:
            @block.sync
            def _(sp):
                sp.dma_start(keep.ident[:], io["ident"][:, :]).then_inc(s_c, 16)
                sp.dma_start(keep.valid[:], io["valid"][:, :]).then_inc(s_c, 16)
                for k, ends in enumerate((io["dst_rows"], io["src_rows"], io["dst_cols"], io["src_cols"])):
                    sp.dma_start(ints[:, k, :], ends[:, :]).then_inc(s_i, 16)
                xv = io["x"].rearrange("(t p) f -> p t f", p=P)
                for b in range(NB):
                    sp.dma_start(keep.X[:, U * b:U * (b + 1), :], xv[:, U * b:U * (b + 1), :]).then_inc(s_x[b], 16)
                sp.wait_ge(s_f, 3)
                sp.dma_start(io["dst_l"].rearrange("k p t -> p k t"), lines[:, 0]).then_inc(s_w, 16)
                sp.dma_start(io["src_l"].rearrange("k p t -> p k t"), lines[:, 1]).then_inc(s_w, 16)
                sp.wait_ge(s_c, 32)
                sp.wait_ge(s_w, 32)

            @block.vector
            def _(vec):
                vec.wait_ge(s_i, 64)
                vec.tensor_scalar(digits[:, :, 0, :], ints[:, 0:2, :], -P, None, ALU.bitwise_and).then_inc(s_f, 1)
                vec.tensor_scalar(digits[:, :, 1, :], ints[:, 0:2, :], P - 1, None, ALU.bitwise_and).then_inc(s_f, 1)
                vec.wait_ge(s_f, 2)
                vec.tensor_copy(lines[:], digits[:]).then_inc(s_f, 1)
                vec.tensor_copy(keep.dst[:], ints[:, 2, :])
                vec.tensor_copy(keep.src[:], ints[:, 3, :])
                for n in range(NT):
                    vec.wait_ge(s_x[n // U], 16)
                    ins = vec.bn_stats(keep.stats[:, n, :], keep.X[:, n, :])
                ins.then_inc(s_st, 1)
                vec.wait_ge(s_st, 1)
                at = norm_factors(vec, s_v, 0, keep, tmp)
                vec.wait_ge(s_v, at)
                vec.tensor_scalar(tmp[:, 1, :], keep.rstd[:], 1e-5, None, ALU.subtract).then_inc(s_v, 1)
                vec.wait_ge(s_r, 1)
                vec.reciprocal(keep.rstd[:], keep.rstd[:]).then_inc(s_v, 1)
                vec.wait_ge(s_v, at + 2)
                vec.tensor_tensor(tmp[:, 1, :], tmp[:, 1, :], keep.rstd[:], ALU.mult).then_inc(s_v, 1)
                vec.wait_ge(s_v, at + 3)
                vec.tensor_tensor(tmp[:, 1, :], tmp[:, 1, :], keep.rstd[:], ALU.mult).then_inc(s_v, 1)
                vec.wait_ge(s_v, at + 4)
                vec.tensor_scalar(keep.rstd2[:], tmp[:, 1, :], 1e-5, None, ALU.add).then_inc(s_v, 1)
                vec.wait_ge(s_r, 2)
                vec.reciprocal(keep.rstd2[:], keep.rstd2[:]).then_inc(s_v, 1)

            @block.scalar
            def _(act):
                act.wait_ge(s_v, STATS + 1)
                act.activation(keep.rstd[:], keep.rstd[:], ACT.Sqrt).then_inc(s_r, 1)
                act.wait_ge(s_v, STATS + 5)
                act.activation(keep.rstd2[:], keep.rstd2[:], ACT.Sqrt).then_inc(s_r, 1)


def tables0(nc, io, keep):
    with Stage(nc, "t0") as s:
        W = s.sb("w", [P, KC, 3 * D])
        bias = s.sb("bias", [P, 3, D])
        extra = s.sb("extra", [P, 2, D])
        gamma, beta = s.sb("gamma", [P, KC]), s.sb("beta", [P, KC])
        xn, xh = s.sb("xn", [P, U, D]), s.sb("xh", [P, U, D])
        xnT, xhT = s.sb("xnT", [P, U, D]), s.sb("xhT", [P, U, D])
        rows = s.sb("rows", [P, U, D])
        tpn, tph = s.ps("tpn", [P, D]), s.ps("tph", [P, D])
        acc = [s.ps(f"acc{k}", [P, D]) for k in range(5)]
        s_w, s_b = s.sem("weights"), s.sem("biases")
        s_bias = s.sem("bias_sum")
        zero = s.sb("zero", [P, 2 * ACCW])
        s_zero, s_z = s.sem("zero"), s.sem("sums_cleared")
        s_go = s.sem("go")
        s_xn, s_xh, s_res, s_tp, s_xT, s_xhT, s_mm, s_rows = (s.sem(n) for n in ("normed", "normed_twice", "residual", "transposed", "xT", "xhT", "products", "rows"))
        s_store = [s.sem(f"rows_out{k}") for k in range(U)]
        s_hstore = [s.sem(f"xhT_out{k}") for k in range(U)]
        with nc.Block() as block:
            @block.sync
            def _(sp):
                for k in range(3):
                    sp.dma_start(W[:, :, D * k:D * (k + 1)], io["w_att"][k].rearrange("(c p) n -> p c n", p=P)).then_inc(s_w, 16)
                sp.dma_start(bias[:], io["b_att"].rearrange("p (k n) -> p k n", k=3)).then_inc(s_b, 16)
                sp.dma_start(gamma[:], io["gamma"][:, :]).then_inc(s_b, 16)
                sp.dma_start(beta[:], io["beta"][:, :]).then_inc(s_b, 16)
                sp.dma_start(extra[:, 0, :], io["b_res"][:, :]).then_inc(s_b, 16)
                sp.dma_start(extra[:, 1, :], io["b_res2"][:, :]).then_inc(s_b, 16)

                def body(i):
                    for j in range(U):
                        n = U * i + j
                        sp.wait_ge(s_xhT, n + 1)
                        sp.dma_start(io["xhT"][n], xhT[:, j, :]).then_inc(s_hstore[j], 16)
                        for w in range(3):
                            m, k = 3 * n + w, (3 * j + w) % 5
                            sp.wait_ge(s_rows, m + 1)
                            sp.dma_start(io["att_rows"][w][bass.ds(n * P, P), :], rows[:, k, :]).then_inc(s_store[k], 16)
                passes(sp, NB, body)
                for k in range(U):
                    sp.wait_ge(s_store[k], 16 * 3 * NB)
                    sp.wait_ge(s_hstore[k], 16 * NB)

            @block.vector
            def _(vec):
                vec.wait_ge(s_b, 80)

                def norms(n, j):
                    need(vec, s_tp, 2 * (n - U) + 2)
                    need(vec, s_res, n - U + 1)
                    vec.tensor_scalar(xn[:, j, :], keep.X[:, n, :], keep.mean[:, bass.ds(n, 1)],
                                      keep.rstd[:, bass.ds(n, 1)], ALU.subtract, ALU.mult).then_inc(s_xn, 1)
                    vec.wait_ge(s_xn, n + 1)
                    vec.tensor_scalar(xh[:, j, :], xn[:, j, :], keep.rstd2[:, bass.ds(n, 1)], None,
                                      ALU.mult).then_inc(s_xh, 1)

                norms(0, 0)

                def body(i):
                    for j in range(U):
                        if not last_tile(U * i + j):
                            norms(U * i + j + 1, (j + 1) % U)
                        for w in range(3):
                            m, k = 3 * (U * i + j) + w, (3 * j + w) % 5
                            vec.wait_ge(s_mm, m + 1)
                            need(vec, s_store[k], 16 * (3 * i + (3 * j + w) // 5))
                            vec.tensor_tensor(rows[:, k, :], acc[k][:], bias[:, w, :], ALU.add).then_inc(s_rows, 1)
                passes(vec, NB, body)

            @block.gpsimd
            def _(pool):
                pool.memset(zero[:], 0.0).then_inc(s_zero, 1)
                pool.wait_ge(s_b, 80)
                pool.tensor_tensor(extra[:, 0, :], extra[:, 0, :], extra[:, 1, :], ALU.add).then_inc(s_bias, 1)
                pool.wait_ge(s_bias, 1)

                def body(i):
                    for j in range(U):
                        n = U * i + j
                        pool.wait_ge(s_xn, n + 1)
                        pool.tensor_tensor(keep.X[:, n, :], keep.X[:, n, :], xn[:, j, :], ALU.add).then_inc(s_res, 1)
                        pool.wait_ge(s_res, n + 1)
                        pool.sem_inc(s_go, 1)
                        pool.tensor_tensor(keep.X[:, n, :], keep.X[:, n, :], extra[:, 0, :], ALU.add)
                passes(pool, NB, body)

            @block.scalar
            def _(act):
                act.wait_ge(s_b, 80)
                act.wait_ge(s_zero, 1)
                cleared = clear_sums(act, s_z, zero, io["acc0"], ACCW)

                def body(i):
                    for j in range(U):
                        n = U * i + j
                        act.wait_ge(s_tp, 2 * n + 1)
                        need(act, s_mm, 3 * (n - U) + 3)
                        act.activation(xnT[:, j, :], tpn[:], ACT.Copy).then_inc(s_xT, 1)
                        act.wait_ge(s_tp, 2 * n + 2)
                        need(act, s_hstore[j], 16 * i)
                        for c in range(KC):
                            cols = slice(P * c, P * (c + 1))
                            ins = act.activation(xhT[:, j, cols], tph[:, cols], ACT.Identity,
                                                 bias=beta[:, c:c + 1], scale=gamma[:, c:c + 1])
                        ins.then_inc(s_xhT, 1)
                passes(act, NB, body)
                act.wait_ge(s_z, cleared)

            @block.tensor
            def _(pe):
                def transposes(n, j):
                    pe.wait_ge(s_xn, n + 1)
                    need(pe, s_xT, n)
                    for c in range(KC):
                        cols = slice(P * c, P * (c + 1))
                        ins = pe.transpose(tpn[:, cols], xn[:, j, cols], keep.ident[:])
                    ins.then_inc(s_tp, 1)
                    pe.wait_ge(s_xh, n + 1)
                    need(pe, s_xhT, n)
                    for c in range(KC):
                        cols = slice(P * c, P * (c + 1))
                        ins = pe.transpose(tph[:, cols], xh[:, j, cols], keep.ident[:])
                    ins.then_inc(s_tp, 1)

                pe.wait_ge(s_w, 48)
                transposes(0, 0)

                def body(i):
                    for j in range(U):
                        n = U * i + j
                        if not last_tile(n):
                            transposes(n + 1, (j + 1) % U)
                        pe.wait_ge(s_xT, n + 1)
                        for w in range(3):
                            m, k = 3 * n + w, (3 * j + w) % 5
                            need(pe, s_rows, m - 5 + 1)
                            for c in range(KC):
                                ins = pe.matmul(acc[k][:], xnT[:, j, P * c:P * (c + 1)], W[:, c, D * w:D * (w + 1)],
                                                start=c == 0, stop=c == KC - 1)
                            ins.then_inc(s_mm, 1)
                passes(pe, NB, body)


def scores0(nc, io, keep):
    with Stage(nc, "s0") as s:
        S = EH
        W = s.sb("w", [P, KC, 3 * D])
        bq, bkv = s.sb("bq", [P, KC]), s.sb("bkv", [P, 2, D])
        half, lower = s.sb("half", [P, 2]), s.sb("lower", [P, P])
        ones, zeros = s.sb("ones", [P, P]), s.sb("zeros", [P, D])
        ix = s.sb("ix", [P, 2, 2, EH], I32)
        qrow, krow = s.sb("qrow", [P, S, D]), s.sb("krow", [P, S, D])
        line, ones2 = s.sb("line", [2, 2, EH * P], BF16), s.sb("ones2", [2, P], BF16)
        junk = s.sb("junk", [P, P])
        xhT = s.sb("xhT", [P, D])
        y, e, el, v = s.sb("y", [P, 2, D]), s.sb("e", [P, 2, D]), s.sb("el", [P, 2, D]), s.sb("v", [P, D])
        pq, pk, pv, pkv, pks = (s.ps(n, [P, D]) for n in ("pq", "pk", "pv", "pkv", "pks"))
        pd = [s.ps(f"pd{k}", [P, D]) for k in range(2)]
        s_w, s_b, s_const = s.sem("weights"), s.sem("biases"), s.sem("constants")
        s_ix = [s.sem(f"indices{h}") for h in range(2)]
        s_line = [s.sem(f"line{h}") for h in range(2)]
        s_g = [s.sem(f"gathered{k}") for k in range(S)]
        s_prod, s_att, s_cnt, s_bc = s.sem("edge_products"), s.sem("scores"), s.sem("counts"), s.sem("destinations")
        s_x, s_mm, s_y, s_e, s_el, s_v, s_kv, s_q = (s.sem(n) for n in (
            "xhT_in", "products", "sums", "exps", "elu", "values", "kv", "q_out"))
        s_end = s.sem("blocks")
        s_go = s.sem("go")
        with nc.Block() as block:
            @block.sync
            def _(sp):
                for k in range(3):
                    sp.dma_start(W[:, :, D * k:D * (k + 1)],
                                 io["w_mix0"][:, D * k:D * (k + 1)].rearrange("(c p) n -> p c n", p=P)).then_inc(s_w, 16)
                sp.dma_start(bq[:], io["bq_mix0"][:, :]).then_inc(s_b, 16)
                sp.dma_start(bkv[:], io["bkv_mix0"].rearrange("p (k n) -> p k n", k=2)).then_inc(s_b, 16)
                sp.dma_start(half[:], io["half"][:, :]).then_inc(s_b, 16)
                sp.dma_start(lower[:], io["lower"][:, :]).then_inc(s_b, 16)
                lines = io["dst_l"].rearrange("k p t -> k (p t)")

                def body(b):
                    if not last_pass(b):
                        need(sp, s_mm, 3 * b)
                        sp.dma_start(xhT[:], io["xhT"][b]).then_inc(s_x, 16)
                    for h in range(2):
                        need(sp, s_att, EU * (b - 1) + EH * (h + 1))
                        sp.dma_start(ix[:, h, 0, :], io["dst_ix"][b, :, EH * h:EH * (h + 1)]).then_inc(s_ix[h], 16)
                        sp.dma_start(ix[:, h, 1, :], io["src_ix"][b, :, EH * h:EH * (h + 1)]).then_inc(s_ix[h], 16)
                        need(sp, s_bc, 4 * (b - 1) + 2 * (h + 1))
                        sp.dma_start(line[:, h, :], lines[:, bass.ds((2 * b + h) * EH * P, EH * P)]).then_inc(s_line[h], 16)
                passes(sp, EB, body)

            @block.gpsimd
            def _(pool):
                def body(b):
                    for k in range(EU):
                        t = EU * b + k
                        if k % EH == 0:
                            pool.wait_ge(s_ix[k // EH], 32 * (b + 1))
                        need(pool, s_att, t - S + 1)
                        pool.sem_inc(s_go, 1)
                        for w, rows in ((0, qrow), (1, krow)):
                            pool.indirect_dma_start(
                                rows[:, k % S, :], None, io["att_rows"][w],
                                bass.IndirectOffsetOnAxis(ap=ix[:, k // EH, w, k % EH:k % EH + 1], axis=0),
                            ).then_inc(s_g[k % S], 16)
                passes(pool, EB, body)

            @block.vector
            def _(vec):
                vec.memset(ones[:], 1.0).then_inc(s_const, 1)
                vec.memset(ones2[:], 1.0).then_inc(s_const, 1)
                vec.memset(zeros[:], 0.0).then_inc(s_const, 1)
                vec.wait_ge(s_b, 64)

                def edge(b, k):
                    t = EU * b + k
                    vec.wait_ge(s_g[k % S], 32 * (2 * b + k // S + 1))
                    vec.tensor_tensor(qrow[:, k % S, :], qrow[:, k % S, :], krow[:, k % S, :], ALU.mult).then_inc(s_prod, 1)
                    if k % 4 == 0:
                        vec.wait_ge(s_bc, 4 * b + k // 4 + 1)
                    need(vec, s_cnt, t)
                    vec.scalar_tensor_tensor(junk[:], pd[k // 4 % 2][:, P * (k % 4):P * (k % 4 + 1)],
                                             keep.dst[:, bass.ds(t, 1)], lower[:], ALU.is_equal, ALU.mult,
                                             accum_out=keep.count[:, bass.ds(t, 1)]).then_inc(s_cnt, 1)
                    vec.wait_ge(s_prod, t + 1)
                    vec.tensor_reduce(keep.att[:, t, :], qrow[:, k % S, :].rearrange("p (h d) -> p h d", h=H),
                                      AX, ALU.add).then_inc(s_att, 1)

                def mix_sums(b):
                    vec.wait_ge(s_mm, 3 * b + 1)
                    need(vec, s_el, 2 * b - 1)
                    vec.tensor_tensor(y[:, 0, :].rearrange("p (c n) -> p c n", c=KC),
                                      pq[:].rearrange("p (c n) -> p c n", c=KC),
                                      bq[:].unsqueeze(2).broadcast_to([P, KC, P]), ALU.add).then_inc(s_y, 1)
                    vec.wait_ge(s_mm, 3 * b + 2)
                    vec.tensor_tensor(y[:, 1, :], pk[:], bkv[:, 0, :], ALU.add).then_inc(s_y, 1)
                    vec.wait_ge(s_mm, 3 * b + 3)
                    need(vec, s_kv, b)
                    vec.tensor_tensor(v[:], pv[:], bkv[:, 1, :], ALU.add).then_inc(s_v, 1)

                def mix_elu(b, last):
                    vec.wait_ge(s_e, 4 * b + 2)
                    need(vec, s_q, 16 * b)
                    vec.scalar_tensor_tensor(el[:, 0, :], y[:, 0, :], 0.0, e[:, 0, :], ALU.max, ALU.add).then_inc(s_el, 1)
                    vec.wait_ge(s_e, 4 * b + 4)
                    ins = vec.scalar_tensor_tensor(el[:, 1, :], y[:, 1, :], 0.0, e[:, 1, :], ALU.max, ALU.add)
                    if last:
                        ins.then_inc(s_end, 1)
                        vec.wait_ge(s_end, 1)
                        ins = vec.tensor_scalar(el[:, 1, :], el[:, 1, :], keep.valid[:, NT - 1:NT], None, ALU.mult)
                    ins.then_inc(s_el, 1)

                def body(b):
                    last = isinstance(b, int) and b == NT - 1
                    for k in range(EU):
                        if k == 4 and not last_pass(b):
                            mix_sums(b)
                        if k == 8 and not last_pass(b):
                            mix_elu(b, last)
                        edge(b, k)
                body(0)
                with vec.Fori(1, NT - 1) as b:
                    body(b)
                body(NT - 1)
                body(EB - 1)
                vec.wait_ge(s_kv, NT)
                for c in range(KC):
                    vec.tensor_tensor(keep.kv[:, c, :].rearrange("p (h d) -> p h d", h=2),
                                      pkv[:, P * c:P * (c + 1)].rearrange("p (h d) -> p h d", h=2),
                                      half[:].unsqueeze(2).broadcast_to([P, 2, DH]), ALU.mult)
                vec.tensor_tensor(keep.ksum[:], pks[:, 0:KC].unsqueeze(2).broadcast_to([P, KC, 2]),
                                  half[:].unsqueeze(1).broadcast_to([P, KC, 2]), ALU.mult).then_inc(s_end, 1)
                vec.wait_ge(s_end, 2)

            @block.scalar
            def _(act):
                def body(b):
                    for k in range(2):
                        act.wait_ge(s_y, 2 * b + k + 1)
                        need(act, s_el, 2 * (b - 1) + k + 1)
                        act.activation(e[:, k, :], y[:, k, :], ACT.Relu, scale=-1.0).then_inc(s_e, 1)
                        act.wait_ge(s_e, 4 * b + 2 * k + 1)
                        act.activation(e[:, k, :], e[:, k, :], ACT.Exp, scale=-1.0).then_inc(s_e, 1)
                    act.wait_ge(s_el, 2 * b + 1)
                    act.dma_start(io["qT"][b], el[:, 0, :]).then_inc(s_q, 16)
                passes(act, NT, body)
                act.wait_ge(s_q, 16 * NT)

            @block.tensor
            def _(pe):
                pe.wait_ge(s_const, 3)
                pe.wait_ge(s_w, 48)
                pe.matmul(pkv[:], zeros[:, 0:P], zeros[:], start=True, stop=False, skip_group_check=True)
                pe.matmul(pks[:, 0:KC], zeros[:, 0:P], zeros[:, 0:KC], start=True, stop=False, skip_group_check=True)

                def spread(b, q):
                    pe.wait_ge(s_line[q // 2], 16 * (b + 1))
                    need(pe, s_cnt, EU * b + 4 * (q - 2) + 4)
                    pe.matmul(pd[q % 2][:], ones2[:], line[:, q // 2, D * (q % 2):D * (q % 2 + 1)],
                              start=True, stop=True).then_inc(s_bc, 1)

                def mix(b):
                    pe.wait_ge(s_x, 16 * (b + 1))
                    need(pe, s_y, 2 * b - 1)
                    for f in range(KC):
                        for c in range(KC):
                            ins = pe.matmul(pq[:, P * f:P * (f + 1)], W[:, c, P * f:P * (f + 1)],
                                            xhT[:, P * c:P * (c + 1)], start=c == 0, stop=c == KC - 1)
                    ins.then_inc(s_mm, 1)
                    for w, acc, sem, count in ((1, pk, s_y, 2 * b), (2, pv, s_v, b)):
                        need(pe, sem, count)
                        for c in range(KC):
                            ins = pe.matmul(acc[:], xhT[:, P * c:P * (c + 1)], W[:, c, D * w:D * (w + 1)],
                                            start=c == 0, stop=c == KC - 1)
                        ins.then_inc(s_mm, 1)

                def sums(b, last):
                    pe.wait_ge(s_v, b + 1)
                    pe.wait_ge(s_el, 2 * b + 2)
                    for c in range(KC):
                        cols = slice(P * c, P * (c + 1))
                        pe.matmul(pkv[:, cols], el[:, 1, cols], v[:, cols], start=False, stop=last and c == KC - 1,
                                  skip_group_check=True)
                        ins = pe.matmul(pks[:, c:c + 1], el[:, 1, cols], ones[:, 0:1], start=False,
                                        stop=last and c == KC - 1, skip_group_check=True)
                    ins.then_inc(s_kv, 1)

                def body(b):
                    last = isinstance(b, int) and b == NT - 1
                    spread(b, 0)
                    spread(b, 1)
                    if not last_pass(b):
                        mix(b)
                    spread(b, 2)
                    if not last_pass(b):
                        sums(b, last)
                    spread(b, 3)
                body(0)
                with pe.Fori(1, NT - 1) as b:
                    body(b)
                body(NT - 1)
                body(EB - 1)


def weights0(nc, io, keep):
    with Stage(nc, "w0") as s:
        m = s.sb("m", [P, 3])
        spare = s.sb("spare", [P, 1])
        go = s.sb("go", [P, 2, ET])
        ints = s.sb("ints", [P, ET], I32)
        s_in, s_m, s_all, s_b, s_exp, s_t, s_out = (s.sem(n) for n in ("spare", "max", "max_all", "shift", "exps", "steps", "out"))
        with nc.Block() as block:
            @block.sync
            def _(sp):
                sp.dma_start(spare[:], io["spare"][:, :]).then_inc(s_in, 16)
                sp.wait_ge(s_t, LEAD_STEPS)
                sp.dma_start(io["lead_ix0"][:, :], ints[:]).then_inc(s_out, 16)
                sp.wait_ge(s_out, 16)

            @block.gpsimd
            def _(pool):
                pool.wait_ge(s_m, 1)
                pool.partition_all_reduce(m[:, 1:2], m[:, 0:1], P, RMAX).then_inc(s_all, 1)

            @block.scalar
            def _(act):
                act.wait_ge(s_b, 1)
                flat = keep.att[:].rearrange("p t h -> p (t h)")
                act.activation(flat, flat, ACT.Exp, bias=m[:, 2:3], scale=DH ** -0.5).then_inc(s_exp, 1)

            @block.vector
            def _(vec):
                vec.reduce_max(m[:, 0:1], keep.att[:].rearrange("p t h -> p (t h)"), AX).then_inc(s_m, 1)
                vec.wait_ge(s_in, 16)
                lead_rows(vec, s_t, keep.dst, keep.count, spare, go, ints)
                vec.wait_ge(s_all, 1)
                vec.tensor_scalar(m[:, 2:3], m[:, 1:2], -DH ** -0.5, 3.0, ALU.mult, ALU.add).then_inc(s_b, 1)


def messages0(nc, io, keep):
    with Stage(nc, "m0") as s:
        S, LEAD, R = EH, 6, 4
        ones = s.sb("ones", [2, P], BF16)
        ix = s.sb("ix", [P, 2, 2, EH], I32)
        vrow = s.sb("vrow", [P, S, D])
        line, sline = s.sb("line", [2, 2, EH * P], BF16), s.sb("sline", [2, 2, EH * P], BF16)
        lower, junk = s.sb("lower", [P, P]), s.sb("junk", [P, P])
        same = s.sb("same", [P, R, P])
        out = s.sb("out", [P, R, ACCW])
        pd = [s.ps(f"pd{k}", [P, D]) for k in range(2)]
        pm = [s.ps(f"pm{k}", [P, D]) for k in range(2)]
        pw = [s.ps(f"pw{k}", [P, H]) for k in range(2)]
        psrc = [s.ps(f"psrc{k}", [P, D]) for k in range(2)]
        s_const, s_low, s_cnt, s_bs = s.sem("constants"), s.sem("lower"), s.sem("counts"), s.sem("sources")
        s_go = s.sem("go")
        s_ix = [s.sem(f"indices{h}") for h in range(2)]
        s_line = [s.sem(f"line{h}") for h in range(2)]
        s_g = [s.sem(f"gathered{k}") for k in range(S)]
        s_add = [s.sem(f"added{k}") for k in range(R)]
        s_msg, s_same, s_bc, s_mm, s_row = (s.sem(n) for n in ("messages", "same", "destinations", "products", "rows"))
        with nc.Block() as block:
            @block.sync
            def _(sp):
                lines = io["dst_l"].rearrange("k p t -> k (p t)")
                slines = io["src_l"].rearrange("k p t -> k (p t)")
                sp.dma_start(lower[:], io["lower"][:, :]).then_inc(s_low, 16)

                def body(b):
                    for h in range(2):
                        need(sp, s_bs, 4 * (b - 1) + 2 * (h + 1))
                        cols = bass.ds((2 * b + h) * EH * P, EH * P)
                        sp.dma_start(line[:, h, :], lines[:, cols]).then_inc(s_line[h], 16)
                        sp.dma_start(sline[:, h, :], slines[:, cols]).then_inc(s_line[h], 16)
                        for r in range(R):
                            need(sp, s_add[r], 16 * ((EU * (b - 1) + EH * (h + 1)) // R) if isinstance(b, int)
                                 else 16 * (EU // R * (b - 1) + EH // R * (h + 1)))
                        sp.dma_start(ix[:, h, 0, :], io["lead_ix0"][:, bass.ds(EU * b + EH * h, EH)]).then_inc(s_ix[h], 16)
                        sp.dma_start(ix[:, h, 1, :], io["src_ix"][b, :, EH * h:EH * (h + 1)]).then_inc(s_ix[h], 16)
                passes(sp, EB, body)

            @block.gpsimd
            def _(pool):
                def gather(b, k):
                    b, k = b + k // EU, k % EU
                    t = EU * b + k
                    if k % EH == 0:
                        pool.wait_ge(s_ix[k // EH], 32 * (b + 1))
                    need(pool, s_mm, t - S + 1)
                    pool.sem_inc(s_go, 1)
                    pool.indirect_dma_start(
                        vrow[:, k % S, :], None, io["att_rows"][2],
                        bass.IndirectOffsetOnAxis(ap=ix[:, k // EH, 1, k % EH:k % EH + 1], axis=0),
                    ).then_inc(s_g[k % S], 16)

                def body(b):
                    for k in range(EU):
                        t = EU * b + k
                        if not (last_pass(b) and k + LEAD >= EU):
                            gather(b, k + LEAD)
                        pool.wait_ge(s_row, t + 1)
                        prev = k - NACC
                        at = EU // R * b + prev // R
                        need(pool, s_add[prev % R], 16 * (at + 1))
                        pool.sem_inc(s_go, 1)
                        pool.indirect_dma_start(
                            io["acc0"][k % NACC], bass.IndirectOffsetOnAxis(ap=ix[:, k // EH, 0, k % EH:k % EH + 1], axis=0),
                            out[:, k % R, :], None, compute_op=ALU.add,
                        ).then_inc(s_add[k % R], 16)
                for k in range(LEAD):
                    gather(0, k)
                passes(pool, EB, body)
                for r in range(R):
                    pool.wait_ge(s_add[r], 16 * (ET // R))

            @block.vector
            def _(vec):
                vec.memset(ones[:], 1.0).then_inc(s_const, 1)
                vec.wait_ge(s_low, 16)

                def body(b):
                    for k in range(EU):
                        t = EU * b + k
                        if k % 4 == 0:
                            vec.wait_ge(s_bc, 4 * b + k // 4 + 1)
                        need(vec, s_mm, t - R + 1)
                        vec.tensor_scalar(same[:, k % R, :], pd[k // 4 % 2][:, P * (k % 4):P * (k % 4 + 1)],
                                          keep.dst[:, bass.ds(t, 1)], None, ALU.is_equal).then_inc(s_same, 1)
                        if k % 4 == 0:
                            vec.wait_ge(s_bs, 4 * b + k // 4 + 1)
                        need(vec, s_cnt, t)
                        vec.scalar_tensor_tensor(junk[:], psrc[k // 4 % 2][:, P * (k % 4):P * (k % 4 + 1)],
                                                 keep.src[:, bass.ds(t, 1)], lower[:], ALU.is_equal, ALU.mult,
                                                 accum_out=keep.count[:, bass.ds(t, 1)]).then_inc(s_cnt, 1)
                        vec.wait_ge(s_g[k % S], 16 * (2 * b + k // S + 1))
                        rows = vrow[:, k % S, :].rearrange("p (h d) -> p h d", h=H)
                        vec.tensor_tensor(rows, rows, keep.att[:, t, :].unsqueeze(2).broadcast_to([P, H, DH]),
                                          ALU.mult).then_inc(s_msg, 1)
                passes(vec, EB, body)

            @block.tensor
            def _(pe):
                pe.wait_ge(s_const, 1)

                def spread(b, q):
                    pe.wait_ge(s_line[q // 2], 32 * (b + 1))
                    need(pe, s_same, EU * b + 4 * (q - 2) + 4)
                    pe.matmul(pd[q % 2][:], ones[:], line[:, q // 2, D * (q % 2):D * (q % 2 + 1)],
                              start=True, stop=True).then_inc(s_bc, 1)
                    need(pe, s_cnt, EU * b + 4 * (q - 2) + 4)
                    pe.matmul(psrc[q % 2][:], ones[:], sline[:, q // 2, D * (q % 2):D * (q % 2 + 1)],
                              start=True, stop=True).then_inc(s_bs, 1)

                spread(0, 0)

                def body(b):
                    for k in range(EU):
                        t = EU * b + k
                        if k % 4 == 0 and not (last_pass(b) and k + 4 == EU):
                            spread(b + (k + 4) // EU, (k // 4 + 1) % 4)
                        pe.wait_ge(s_msg, t + 1)
                        need(pe, s_row, t - 1)
                        pe.matmul(pm[k % 2][:], same[:, k % R, :], vrow[:, k % S, :], start=True, stop=True)
                        pe.matmul(pw[k % 2][:], same[:, k % R, :], keep.att[:, t, :], start=True, stop=True).then_inc(s_mm, 1)
                passes(pe, EB, body)

            @block.scalar
            def _(act):
                def body(b):
                    for k in range(EU):
                        t = EU * b + k
                        act.wait_ge(s_mm, t + 1)
                        need(act, s_add[k % R], 16 * (EU // R * b + k // R))
                        act.activation(out[:, k % R, 0:D], pm[k % 2][:], ACT.Copy)
                        act.activation(out[:, k % R, D:ACCW], pw[k % 2][:], ACT.Copy).then_inc(s_row, 1)
                passes(act, EB, body)


def leads1(nc, io, keep):
    with Stage(nc, "w1") as s:
        spare = s.sb("spare", [P, 1])
        go = s.sb("go", [P, 2, ET])
        ints = s.sb("ints", [P, ET], I32)
        s_in, s_t, s_out = s.sem("spare"), s.sem("steps"), s.sem("out")
        with nc.Block() as block:
            @block.sync
            def _(sp):
                sp.dma_start(spare[:], io["spare"][:, :]).then_inc(s_in, 16)
                sp.wait_ge(s_t, LEAD_STEPS)
                sp.dma_start(io["lead_ix1"][:, :], ints[:]).then_inc(s_out, 16)
                sp.wait_ge(s_out, 16)

            @block.vector
            def _(vec):
                vec.wait_ge(s_in, 16)
                lead_rows(vec, s_t, keep.src, keep.count, spare, go, ints)


def attend(pe, q, kv, ksum, po, pn):
    for c in range(KC):
        cols = slice(P * c, P * (c + 1))
        pe.matmul(po[:, cols], q[:, cols], kv[:, c, :], start=True, stop=True)
    for c in range(KC):
        ins = pe.matmul(pn[:, 2 * c:2 * c + 2], q[:, P * c:P * (c + 1)], ksum[:, c, :], start=True, stop=True)
    return ins


def by_head(x):
    return x.rearrange("p (h d) -> p h d", h=H)


def over_head(x):
    return x.unsqueeze(2).broadcast_to([P, H, DH])


def merge0(nc, io, keep):
    with Stage(nc, "g0") as s:
        W = s.sb("w", [P, 2, KC, D])
        a0, a1 = s.sb("a0", [P, U, ACCW]), s.sb("a1", [P, U, ACCW])
        q = s.sb("q", [P, U, D])
        o, aT, oT = s.sb("o", [P, U, D]), s.sb("aT", [P, U, D]), s.sb("oT", [P, U, D])
        z, zo = s.sb("z", [P, 2, H]), s.sb("zo", [P, H])
        po, pn, tpa, tpo = s.ps("po", [P, D]), s.ps("pn", [P, H]), s.ps("tpa", [P, D]), s.ps("tpo", [P, D])
        pout = [s.ps(f"pout{k}", [P, D]) for k in range(2)]
        s_w = s.sem("weights")
        s_in = [s.sem(f"in{j}") for j in range(U)]
        s_st, s_agg, s_o, s_po, s_ta, s_to, s_aT, s_oT, s_mm, s_x = (s.sem(n) for n in (
            "steps", "edges", "mixed", "attended", "edgesT", "mixedT", "aT", "oT", "products", "x"))
        with nc.Block() as block:
            @block.sync
            def _(sp):
                sp.dma_start(W[:, 0], io["w_ff"].rearrange("(c p) n -> p c n", p=P)).then_inc(s_w, 16)
                sp.dma_start(W[:, 1], io["w_out0"].rearrange("(c p) n -> p c n", p=P)).then_inc(s_w, 16)

                def body(i):
                    for j in range(U):
                        n = U * i + j
                        need(sp, s_ta, n - U + 1)
                        need(sp, s_po, n - U + 1)
                        rows = bass.ds(n * P, P)
                        sp.dma_start(a0[:, j, :], io["acc0"][0][rows, :]).then_inc(s_in[j], 16)
                        sp.dma_start(a1[:, j, :], io["acc0"][1][rows, :]).then_inc(s_in[j], 16)
                        sp.dma_start(q[:, j, :], io["qT"][n]).then_inc(s_in[j], 16)
                passes(sp, NB, body)

            @block.vector
            def _(vec):
                st = Steps(vec, s_st, 5)

                def norm_edges(i, j):
                    n = U * i + j
                    st.begin(n)
                    vec.wait_ge(s_in[j], 48 * (i + 1))
                    st.did(vec.tensor_tensor(a0[:, j, :], a0[:, j, :], a1[:, j, :], ALU.add))
                    st.wait()
                    den = a0[:, j, D:ACCW]
                    st.did(vec.scalar_tensor_tensor(z[:, 0, :], den, 0.0, den, ALU.is_equal, ALU.add))
                    st.wait()
                    st.did(vec.reciprocal(z[:, 1, :], z[:, 0, :]))
                    st.wait()
                    vec.tensor_tensor(by_head(a0[:, j, 0:D]), by_head(a0[:, j, 0:D]), over_head(z[:, 1, :]),
                                      ALU.mult).then_inc(s_agg, 1)

                def norm_mixed(i, j):
                    n = U * i + j
                    vec.wait_ge(s_po, n + 1)
                    st.did(vec.tensor_scalar(zo[:], pn[:], 1e-8, None, ALU.add))
                    st.wait()
                    st.did(vec.reciprocal(zo[:], zo[:]))
                    st.wait()
                    need(vec, s_to, n - U + 1)
                    vec.tensor_tensor(by_head(o[:, j, :]), by_head(po[:]), over_head(zo[:]), ALU.mult).then_inc(s_o, 1)

                def add(i, j):
                    n = U * i + j
                    vec.wait_ge(s_mm, n + 1)
                    vec.tensor_tensor(keep.X[:, n, :], keep.X[:, n, :], pout[j % 2][:], ALU.add).then_inc(s_x, 1)
                    vec.wait_ge(s_x, n + 1)
                    vec.bn_stats(keep.stats[:, n, :], keep.X[:, n, :])

                def ahead(i, j):
                    norm_edges(i, j)
                    norm_mixed(i, j)

                ahead(0, 0)

                def body(i):
                    for j in range(U):
                        if not last_tile(U * i + j):
                            ahead(i + (j + 1) // U, (j + 1) % U)
                        add(i, j)
                passes(vec, NB, body)

            @block.scalar
            def _(act):
                def turn(i, j):
                    n = U * i + j
                    act.wait_ge(s_ta, n + 1)
                    need(act, s_mm, n - U + 1)
                    act.activation(aT[:, j, :], tpa[:], ACT.Copy).then_inc(s_aT, 1)
                    act.wait_ge(s_to, n + 1)
                    act.activation(oT[:, j, :], tpo[:], ACT.Copy).then_inc(s_oT, 1)

                def body(i):
                    for j in range(U):
                        turn(i, j)
                passes(act, NB, body)

            @block.tensor
            def _(pe):
                def edges(i, j):
                    n = U * i + j
                    pe.wait_ge(s_in[j], 48 * (i + 1))
                    need(pe, s_o, n)
                    attend(pe, q[:, j, :], keep.kv, keep.ksum, po, pn).then_inc(s_po, 1)
                    pe.wait_ge(s_agg, n + 1)
                    need(pe, s_aT, n)
                    for c in range(KC):
                        cols = slice(P * c, P * (c + 1))
                        ins = pe.transpose(tpa[:, cols], a0[:, j, cols], keep.ident[:])
                    ins.then_inc(s_ta, 1)

                def mixed(i, j):
                    n = U * i + j
                    pe.wait_ge(s_o, n + 1)
                    need(pe, s_oT, n)
                    for c in range(KC):
                        cols = slice(P * c, P * (c + 1))
                        ins = pe.transpose(tpo[:, cols], o[:, j, cols], keep.ident[:])
                    ins.then_inc(s_to, 1)

                pe.wait_ge(s_w, 32)
                edges(0, 0)
                mixed(0, 0)

                def body(i):
                    for j in range(U):
                        n = U * i + j
                        nxt = (i + (j + 1) // U, (j + 1) % U)
                        pe.wait_ge(s_aT, n + 1)
                        need(pe, s_x, n if j == 0 else n - 1)
                        for c in range(KC):
                            pe.matmul(pout[j % 2][:], aT[:, j, P * c:P * (c + 1)], W[:, 0, c, :], start=c == 0, stop=False)
                        if not last_tile(n):
                            edges(*nxt)
                        pe.wait_ge(s_oT, n + 1)
                        for c in range(KC):
                            ins = pe.matmul(pout[j % 2][:], oT[:, j, P * c:P * (c + 1)], W[:, 1, c, :], start=False, stop=c == KC - 1)
                        ins.then_inc(s_mm, 1)
                        if not last_tile(n):
                            mixed(*nxt)
                passes(pe, NB, body)


def norm_rows(nc, io, keep, name, stats):
    with Stage(nc, name) as s:
        tmp = s.sb("tmp", [P, 2, NT])
        s_st, s_v, s_r = s.sem("stats"), s.sem("steps"), s.sem("roots")
        with nc.Block() as block:
            @block.vector
            def _(vec):
                if stats:
                    with vec.Fori(0, NT) as n:
                        vec.bn_stats(keep.stats[:, n, :], keep.X[:, n, :]).then_inc(s_st, 1)
                    vec.wait_ge(s_st, NT)
                at = norm_factors(vec, s_v, 0, keep, tmp)
                vec.wait_ge(s_r, 1)
                vec.reciprocal(keep.rstd[:], keep.rstd[:]).then_inc(s_v, 1)
                vec.wait_ge(s_v, at + 1)

            @block.scalar
            def _(act):
                act.wait_ge(s_v, STATS)
                act.activation(keep.rstd[:], keep.rstd[:], ACT.Sqrt).then_inc(s_r, 1)


def gates0(nc, io, keep):
    with Stage(nc, "r0") as s:
        xn = s.sb("xn", [P, U, D])
        wg, bg, lower8 = s.sb("wg", [P, KC, NX0]), s.sb("bg", [NX0, 1]), s.sb("lower8", [P, NX0 * NX0])
        lgT = s.sb("lgT", [NX0, NP])
        g = s.sb("g", [P, NT, NX0])
        m = s.sb("m", [P, NT])
        rank, eq = s.sb("rank", [P, NT, NX0 * NX0]), s.sb("eq", [P, NT, NX0 * NX0])
        tp = [s.ps(f"tp{k}", [P, D]) for k in range(5)]
        pl = s.ps("pl", [NX0, D])
        pg = s.ps("pg", [P, NT * NX0])
        GW = 640 // 2
        s_w, s_xn, s_tp, s_xT, s_l, s_lT, s_g, s_e, s_v = (s.sem(n) for n in (
            "weights", "normed", "transposed", "xT", "logits", "logitsT", "turned", "exps", "steps"))
        s_go = s.sem("go")
        with nc.Block() as block:
            @block.sync
            def _(sp):
                sp.dma_start(wg[:], io["wg0"].rearrange("(c p) n -> p c n", p=P)).then_inc(s_w, 16)
                sp.dma_start(bg[:], io["bg0"][:, :]).then_inc(s_w, 16)
                sp.dma_start(lower8[:], io["lower8"][:, :]).then_inc(s_w, 16)
                sp.wait_ge(s_w, 48)

            @block.vector
            def _(vec):
                def body(i):
                    for j in range(U):
                        n = U * i + j
                        need(vec, s_tp, n - U + 1)
                        vec.tensor_scalar(xn[:, j, :], keep.X[:, n, :], keep.mean[:, bass.ds(n, 1)],
                                          keep.rstd[:, bass.ds(n, 1)], ALU.subtract, ALU.mult).then_inc(s_xn, 1)
                passes(vec, NB, body)
                st = Steps(vec, s_v, 0)
                st.begin(0)

                def over(x):
                    return x.unsqueeze(2).broadcast_to([P, NT, NX0])
                vec.wait_ge(s_w, 48)
                vec.wait_ge(s_g, 1)
                logits = pg[:].rearrange("p (t e) -> p t e", e=NX0)
                st.did(vec.tensor_reduce(m[:], logits, AX, ALU.max))
                st.wait()
                st.did(vec.tensor_tensor(g[:], logits, over(m[:]), ALU.subtract))
                vec.wait_ge(s_e, 1)
                st.did(vec.tensor_reduce(m[:], g[:], AX, ALU.add))
                st.wait()
                st.did(vec.reciprocal(m[:], m[:]))
                st.wait()
                st.did(vec.tensor_tensor(g[:], g[:], over(m[:]), ALU.mult))
                st.wait()
                wide = [P, NT, NX0, NX0]
                r4, e4 = (x[:].rearrange("p t (a b) -> p t a b", b=NX0) for x in (rank, eq))
                mine, other = g[:].unsqueeze(3).broadcast_to(wide), g[:].unsqueeze(2).broadcast_to(wide)
                st.did(vec.tensor_tensor(r4, other, mine, ALU.is_gt))
                st.did(vec.tensor_tensor(e4, other, mine, ALU.is_equal))
                st.wait()
                st.did(vec.tensor_tensor(eq[:], eq[:], lower8[:].unsqueeze(1).broadcast_to([P, NT, NX0 * NX0]), ALU.mult))
                st.wait()
                st.did(vec.tensor_tensor(rank[:], rank[:], eq[:], ALU.add))
                st.wait()
                st.did(vec.tensor_reduce(keep.comb[:], r4, AX, ALU.add))
                st.wait()
                flat = (x[:].rearrange("p t e -> p (t e)") for x in (keep.comb, keep.comb, g))
                st.did(vec.scalar_tensor_tensor(next(flat), next(flat), 2.0, next(flat), ALU.is_lt, ALU.mult))
                st.wait()

            @block.scalar
            def _(act):
                act.wait_ge(s_w, 48)

                def body(i):
                    for j in range(U):
                        n = U * i + j
                        act.wait_ge(s_tp, n + 1)
                        act.sem_inc(s_go, 1)
                        act.activation(keep.XT[:, :, bass.ds(n * P, P)], tp[j][:].rearrange("p (c n) -> p c n", c=KC),
                                       ACT.Copy).then_inc(s_xT, 1)
                    for h in range(2):
                        q = 2 * i + h
                        act.wait_ge(s_l, q + 1)
                        act.sem_inc(s_go, 1)
                        act.activation(lgT[:, bass.ds(q * GW, GW)], pl[:, 0:GW], ACT.Identity, bias=bg[:]).then_inc(s_lT, 1)
                passes(act, NB, body)
                act.wait_ge(s_v, 2)
                act.activation(g[:], g[:], ACT.Exp).then_inc(s_e, 1)

            @block.tensor
            def _(pe):
                pe.wait_ge(s_w, 48)

                def body(i):
                    for j in range(U):
                        n = U * i + j
                        pe.wait_ge(s_xn, n + 1)
                        need(pe, s_xT, n - U + 1)
                        for c in range(KC):
                            cols = slice(P * c, P * (c + 1))
                            ins = pe.transpose(tp[j][:, cols], xn[:, j, cols], keep.ident[:])
                        ins.then_inc(s_tp, 1)
                    pe.wait_ge(s_xT, U * (i + 1))
                    for h in range(2):
                        q = 2 * i + h
                        need(pe, s_lT, q)
                        for c in range(KC):
                            ins = pe.matmul(pl[:, 0:GW], wg[:, c, :], keep.XT[:, c, bass.ds(q * GW, GW)],
                                            start=c == 0, stop=c == KC - 1)
                        ins.then_inc(s_l, 1)
                passes(pe, NB, body)
                pe.wait_ge(s_lT, 2 * NB)
                for n in range(NT):
                    ins = pe.transpose(pg[:, NX0 * n:NX0 * (n + 1)], lgT[:, P * n:P * (n + 1)], keep.ident[0:NX0, 0:NX0])
                ins.then_inc(s_g, 1)


def experts0(nc, io, keep):
    with Stage(nc, "e0") as s:
        FC = QF // P
        GN = U * P
        HW = GN // 2
        w1, w2 = s.sb("w1", [P, 2, KC, QF]), s.sb("w2", [P, 2, FC, D])
        b1, b2 = s.sb("b1", [P, 2, FC]), s.sb("b2", [P, 2, D])
        hT = s.sb("hT", [P, 2, FC, GN])
        ph = [s.ps(f"ph{k}", [P, D]) for k in range(2 * FC)]
        py = [s.ps(f"py{k}", [P, D]) for k in range(2)]
        s_w = [s.sem(f"weights{k}") for k in range(2)]
        s_h, s_hT, s_y, s_x, s_pre = (s.sem(n) for n in ("hidden", "gelus", "products", "x", "biased"))
        zero = s.sb("zero", [P, 2 * D])
        s_zero, s_z = s.sem("zero"), s.sem("sums_cleared")
        PAIRS, STEPS = NX0 // 2, 2 * NB

        def loop(eng, body):
            body(0)
            with eng.Fori(1, PAIRS) as i:
                body(i)

        with nc.Block() as block:
            @block.sync
            def _(sp):
                def body(i):
                    for r in range(2):
                        e = 2 * i + r
                        need(sp, s_x, (e - 2 + 1) * NT)
                        sp.dma_start(w1[:, r], io["w1"][e].rearrange("(c p) n -> p c n", p=P)).then_inc(s_w[r], 16)
                        sp.dma_start(w2[:, r], io["w2"][e].rearrange("(c p) n -> p c n", p=P)).then_inc(s_w[r], 16)
                        sp.dma_start(b1[:, r], io["b1"][e]).then_inc(s_w[r], 16)
                        sp.dma_start(b2[:, r], io["b2"][e].partition_broadcast(P)).then_inc(s_w[r], 16)
                loop(sp, body)

            @block.gpsimd
            def _(pool):
                pool.memset(zero[:], 0.0).then_inc(s_zero, 1)

            @block.scalar
            def _(act):
                act.wait_ge(s_zero, 1)
                cleared = clear_sums(act, s_z, zero, io["acc1"], D)
                def body(i):
                    for r in range(2):
                        act.wait_ge(s_w[r], 64 * (i + 1))
                        for g in range(NB):
                            q = STEPS * i + NB * r + g
                            par = (NB * r + g) % 2
                            need(act, s_y, U * (q - 1))
                            for k in range(2 * FC):
                                f, h = k // 2, k % 2
                                act.wait_ge(s_h, 2 * FC * q + k + 1)
                                act.activation(hT[:, par, f, HW * h:HW * (h + 1)], ph[k][:, 0:HW], ACT.Gelu_apprx_tanh,
                                               bias=b1[:, r, f:f + 1]).then_inc(s_hT, 1)
                loop(act, body)
                act.wait_ge(s_z, cleared)

            @block.vector
            def _(vec):
                def body(i):
                    for r in range(2):
                        vec.wait_ge(s_w[r], 64 * (i + 1))
                        for g in range(NB):
                            for t in range(U):
                                k = (NB * r + g) * U + t
                                y = STEPS * U * i + k
                                n = U * g + t
                                need(vec, s_x, y - NT + 1)
                                gate = keep.comb[:, n, bass.ds(2 * i + r, 1)]
                                vec.scalar_tensor_tensor(keep.X[:, n, :], b2[:, r, :], gate, keep.X[:, n, :],
                                                         ALU.mult, ALU.add).then_inc(s_pre, 1)
                                vec.wait_ge(s_y, y + 1)
                                vec.wait_ge(s_pre, y + 1)
                                vec.scalar_tensor_tensor(keep.X[:, n, :], py[k % 2][:], gate, keep.X[:, n, :],
                                                         ALU.mult, ALU.add).then_inc(s_x, 1)
                loop(vec, body)

            @block.tensor
            def _(pe):
                def hidden(i, r, g):
                    q = STEPS * i + NB * r + g
                    if g == 0:
                        pe.wait_ge(s_w[r], 64 * (i + 1))
                    for k in range(2 * FC):
                        f, h = k // 2, k % 2
                        need(pe, s_hT, 2 * FC * (q - 1) + k + 1)
                        for c in range(KC):
                            ins = pe.matmul(ph[k][:, 0:HW], w1[:, r, c, P * f:P * (f + 1)],
                                            keep.XT[:, c, GN * g + HW * h:GN * g + HW * (h + 1)], start=c == 0, stop=c == KC - 1)
                        ins.then_inc(s_h, 1)

                def output(i, r, g):
                    last = 2 * NB * i + NB * r + g - 1
                    k0 = (NB * r + g - 1) % STEPS
                    pr = k0 // NB
                    pe.wait_ge(s_hT, 2 * FC * (last + 1))
                    for t in range(U):
                        k = k0 * U + t
                        need(pe, s_x, U * last + t - 2 + 1)
                        for f in range(FC):
                            ins = pe.matmul(py[k % 2][:], hT[:, k0 % 2, f, P * t:P * (t + 1)], w2[:, pr, f, :],
                                            start=f == 0, stop=f == FC - 1)
                        ins.then_inc(s_y, 1)

                def body(i):
                    for r in range(2):
                        for g in range(NB):
                            hidden(i, r, g)
                            if not (isinstance(i, int) and i == 0 and r == 0 and g == 0):
                                output(i, r, g)
                loop(pe, body)
                output(PAIRS, 0, 0)


def tables1(nc, io, keep):
    with Stage(nc, "t1") as s:
        GN, HW = U * P, U * P // 2
        w_pre0, w_pre1, w_nd0, w_nd1 = (s.sb(n, [P, P]) for n in ("w_pre0", "w_pre1", "w_nd0", "w_nd1"))
        w_g1, w_g2 = s.sb("w_g1", [P, 2, 2 * P]), s.sb("w_g2", [P, 2, 2 * P])
        b_g, b_pre0, b_nd0 = s.sb("b_g", [P, 2, 2]), s.sb("b_pre0", [P, 1]), s.sb("b_nd0", [P, P])
        w_s = s.sb("w_s", [P, 2, HID])
        extra = s.sb("extra", [P, 2, D])
        xn = s.sb("xn", [P, U, D])
        xT = s.sb("xT", [P, KC, GN])
        sq, gated = s.sb("sq", [P, 3, GN]), s.sb("gated", [P, 3, GN])
        n1, p0 = s.sb("n1", [P, GN]), s.sb("p0", [P, GN])
        g1, g2 = s.sb("g1", [P, 2, GN]), s.sb("g2", [P, 2, GN])
        srow, drow = s.sb("srow", [P, U, SW]), s.sb("drow", [P, U, DW])
        tp = [s.ps(f"tp{k}", [P, D]) for k in range(2)]
        pr = [s.ps(f"pr{k}", [P, D]) for k in range(2)]
        pg = [s.ps(f"pg{k}", [P, D]) for k in range(4)]
        s_w, s_wab = s.sem("weights"), s.sem("folded")
        s_xn, s_res, s_tp, s_xT, s_p0, s_p0T, s_pr, s_drow, s_prow = (s.sem(n) for n in (
            "normed", "residual", "transposed", "xT", "scalars", "scalarsT", "projections", "destination_rows", "source_rows"))
        s_sq, s_n1, s_g1, s_g1T, s_g2, s_g2T, s_x1, s_nd, s_row = (s.sem(n) for n in (
            "squares", "norms", "hidden", "hiddenT", "gates", "gatesT", "gated", "node_rows", "rows"))
        s_xout, s_rout, s_b = s.sem("xT_out"), s.sem("rows_out"), s.sem("bias_sum")
        s_go = s.sem("go")
        LOADS = 13
        with nc.Block() as block:
            @block.sync
            def _(sp):
                for dst, src in (
                        (w_pre0, io["w_pre0"][:, :]), (w_pre1, io["w_pre1"][:, :]), (w_nd0, io["w_nd0"][:, :]), (w_nd1, io["w_nd1"][:, :]),
                        (w_g1, io["w_g1"].rearrange("(c p) n -> p c n", p=P)), (w_g2, io["w_g2"].rearrange("(c p) n -> p c n", p=P)),
                        (b_g, io["b_g"][:, :, :]), (b_pre0, io["b_pre0"][:, :]), (b_nd0, io["b_nd0"][:, :])):
                    sp.dma_start(dst[:], src).then_inc(s_w, 16)
                sp.dma_start(w_s[:, 0], io["w_s1"][0:P, :]).then_inc(s_w, 16)
                sp.dma_start(w_s[:, 1], io["w_s1"][P:2 * P, :]).then_inc(s_w, 16)
                sp.dma_start(extra[:, 0], io["b_proj"][:, :]).then_inc(s_w, 16)
                sp.dma_start(extra[:, 1], io["b_o0"][:, :]).then_inc(s_w, 16)
                by_s = io["srow"].rearrange("(t p) w -> p t w", p=P)
                by_d = io["drow"].rearrange("(t p) w -> p t w", p=P)

                def body(i):
                    for j in range(U):
                        sp.wait_ge(s_xT, U * i + j + 1)
                        sp.dma_start(io["xhT"][U * i + j].rearrange("p (c n) -> p c n", c=KC), xT[:, :, P * j:P * (j + 1)]).then_inc(s_xout, 16)
                    sp.wait_ge(s_drow, U * (i + 1))
                    sp.dma_start(by_d[:, bass.ds(U * i, U), :], drow[:]).then_inc(s_rout, 16)
                    sp.wait_ge(s_prow, U * (i + 1))
                    sp.wait_ge(s_row, U * (i + 1))
                    sp.dma_start(by_s[:, bass.ds(U * i, U), :], srow[:]).then_inc(s_rout, 16)
                passes(sp, NB, body)
                sp.wait_ge(s_xout, 16 * NT)
                sp.wait_ge(s_rout, 32 * NB)

            @block.gpsimd
            def _(pool):
                pool.wait_ge(s_w, 16 * LOADS)
                pool.tensor_tensor(extra[:, 0, :], extra[:, 0, :], extra[:, 1, :], ALU.add).then_inc(s_b, 1)
                pool.wait_ge(s_b, 1)

                def body(i):
                    for j in range(U):
                        n = U * i + j
                        pool.wait_ge(s_xn, n + 1)
                        pool.tensor_tensor(keep.X[:, n, :], keep.X[:, n, :], xn[:, j, :], ALU.add).then_inc(s_res, 1)
                        pool.wait_ge(s_res, n + 1)
                        pool.sem_inc(s_go, 1)
                        pool.tensor_tensor(keep.X[:, n, :], keep.X[:, n, :], extra[:, 0, :], ALU.add)
                passes(pool, NB, body)

            @block.vector
            def _(vec):
                vec.wait_ge(s_w, 16 * LOADS)
                vec.tensor_tensor(w_s[:, 0, :], w_s[:, 0, :], w_s[:, 1, :], ALU.add).then_inc(s_wab, 1)

                def body(i):
                    for j in range(U):
                        n = U * i + j
                        need(vec, s_tp, n - U + 1)
                        need(vec, s_res, n - U + 1)
                        vec.tensor_scalar(xn[:, j, :], keep.X[:, n, :], keep.mean[:, bass.ds(n, 1)],
                                          keep.rstd[:, bass.ds(n, 1)], ALU.subtract, ALU.mult).then_inc(s_xn, 1)
                    vec.wait_ge(s_xT, U * (i + 1))
                    vec.tensor_tensor(sq[:], xT[:, 1:4, :], xT[:, 1:4, :], ALU.mult).then_inc(s_sq, 1)
                    vec.wait_ge(s_sq, 3 * i + 1)
                    vec.tensor_tensor(sq[:, 0, :], sq[:, 0, :], sq[:, 1, :], ALU.add).then_inc(s_sq, 1)
                    vec.wait_ge(s_sq, 3 * i + 2)
                    vec.tensor_tensor(sq[:, 0, :], sq[:, 0, :], sq[:, 2, :], ALU.add).then_inc(s_sq, 1)
                    need(vec, s_rout, 32 * i)
                    for j in range(U):
                        vec.wait_ge(s_drow, U * i + j + 1)
                        vec.tensor_copy(srow[:, j, 0:3 * P], drow[:, j, 0:3 * P]).then_inc(s_prow, 1)
                    vec.wait_ge(s_g2T, 4 * (i + 1))
                    need(vec, s_nd, U * i)
                    vec.tensor_tensor(gated[:], xT[:, 1:4, :], g2[:, 1, :].unsqueeze(1).broadcast_to([P, 3, GN]),
                                      ALU.mult).then_inc(s_x1, 1)
                    for j in range(U):
                        vec.wait_ge(s_nd, U * i + j + 1)
                        vec.tensor_tensor(srow[:, j, 3 * P:4 * P], pr[j % 2][:, 0:P], b_nd0[:], ALU.add)
                        vec.tensor_copy(srow[:, j, 4 * P:SW], pr[j % 2][:, P:D]).then_inc(s_row, 1)
                passes(vec, NB, body)

            @block.scalar
            def _(act):
                act.wait_ge(s_w, 16 * LOADS)

                def body(i):
                    need(act, s_xout, 16 * U * i)
                    need(act, s_x1, i)
                    for j in range(U):
                        n = U * i + j
                        act.wait_ge(s_tp, n + 1)
                        act.activation(xT[:, :, P * j:P * (j + 1)], tp[j % 2][:].rearrange("p (c n) -> p c n", c=KC),
                                       ACT.Copy).then_inc(s_xT, 1)
                    for h in range(2):
                        act.wait_ge(s_p0, 2 * i + h + 1)
                        act.activation(p0[:, HW * h:HW * (h + 1)], pg[h][:, 0:HW], ACT.Identity, bias=b_pre0[:]).then_inc(s_p0T, 1)
                    act.wait_ge(s_sq, 3 * i + 3)
                    act.activation(n1[:], sq[:, 0, :], ACT.Sqrt, scale=1.0 / 3.0).then_inc(s_n1, 1)
                    need(act, s_rout, 32 * i)
                    for j in range(U):
                        act.wait_ge(s_pr, U * i + j + 1)
                        act.activation(drow[:, j, :], pr[j % 2][:, 0:DW], ACT.Copy).then_inc(s_drow, 1)
                    for k in range(4):
                        f, h = k // 2, k % 2
                        act.wait_ge(s_g1, 4 * i + k + 1)
                        act.activation(g1[:, f, HW * h:HW * (h + 1)], pg[k][:, 0:HW], ACT.Silu,
                                       bias=b_g[:, 0, f:f + 1]).then_inc(s_g1T, 1)
                    for k in range(4):
                        f, h = k // 2, k % 2
                        act.wait_ge(s_g2, 4 * i + k + 1)
                        act.activation(g2[:, f, HW * h:HW * (h + 1)], pg[k][:, 0:HW], ACT.Identity,
                                       bias=b_g[:, 1, f:f + 1]).then_inc(s_g2T, 1)
                passes(act, NB, body)

            @block.tensor
            def _(pe):
                pe.wait_ge(s_w, 16 * LOADS)
                pe.wait_ge(s_wab, 1)

                def body(i):
                    for j in range(U):
                        n = U * i + j
                        pe.wait_ge(s_xn, n + 1)
                        need(pe, s_xT, n if j == 0 else n - 1)
                        for c in range(KC):
                            x = xn[:, j, 0:P] if c == 0 else xn[:, j, P:D].rearrange("p (u c) -> p c u", c=3)[:, c - 1, :]
                            ins = pe.transpose(tp[j % 2][:, P * c:P * (c + 1)], x, keep.ident[:])
                        ins.then_inc(s_tp, 1)
                    pe.wait_ge(s_xT, U * (i + 1))
                    need(pe, s_g2T, 4 * i)
                    for h in range(2):
                        pe.matmul(pg[h][:, 0:HW], w_pre0[:], xT[:, 0, HW * h:HW * (h + 1)], start=True, stop=True).then_inc(s_p0, 1)
                    need(pe, s_row, U * i)
                    pe.wait_ge(s_p0T, 2 * (i + 1))
                    for j in range(U):
                        n = U * i + j
                        if j >= 2:
                            pe.wait_ge(s_drow, n - 1)
                        cols = slice(P * j, P * (j + 1))
                        for c in range(3):
                            pe.matmul(pr[j % 2][:, P * c:P * (c + 1)], xT[:, 1 + c, cols], w_pre1[:], start=True, stop=True)
                        pe.matmul(pr[j % 2][:, 3 * P:DW], p0[:, cols], w_s[:, 0, :], start=True, stop=True).then_inc(s_pr, 1)
                    pe.wait_ge(s_n1, i + 1)
                    for k in range(4):
                        f, h = k // 2, k % 2
                        half = slice(HW * h, HW * (h + 1))
                        pe.matmul(pg[k][:, 0:HW], w_g1[:, 0, P * f:P * (f + 1)], xT[:, 0, half], start=True, stop=False)
                        pe.matmul(pg[k][:, 0:HW], w_g1[:, 1, P * f:P * (f + 1)], n1[:, half], start=False, stop=True).then_inc(s_g1, 1)
                    for k in range(4):
                        f, h = k // 2, k % 2
                        half = slice(HW * h, HW * (h + 1))
                        if k == 0:
                            pe.wait_ge(s_g1T, 4 * (i + 1))
                        pe.matmul(pg[k][:, 0:HW], w_g2[:, 0, P * f:P * (f + 1)], g1[:, 0, half], start=True, stop=False)
                        pe.matmul(pg[k][:, 0:HW], w_g2[:, 1, P * f:P * (f + 1)], g1[:, 1, half], start=False, stop=True).then_inc(s_g2, 1)
                    pe.wait_ge(s_x1, i + 1)
                    pe.wait_ge(s_drow, U * (i + 1))
                    for j in range(U):
                        n = U * i + j
                        if j >= 2:
                            pe.wait_ge(s_row, n - 1)
                        cols = slice(P * j, P * (j + 1))
                        pe.matmul(pr[j % 2][:, 0:P], g2[:, 0, cols], w_nd0[:], start=True, stop=True)
                        for c in range(3):
                            ins = pe.matmul(pr[j % 2][:, P * (c + 1):P * (c + 2)], gated[:, c, cols], w_nd1[:], start=True, stop=True)
                        ins.then_inc(s_nd, 1)
                passes(pe, NB, body)


def mixer1(nc, io, keep):
    with Stage(nc, "x1") as s:
        BANKS = 5
        W = s.sb("w", [P, KC, 3 * D])
        half = s.sb("half", [P, 2])
        ones, zeros = s.sb("ones", [P, 1]), s.sb("zeros", [P, D])
        xT, q, k_, v = (s.sb(n, [P, U, D]) for n in ("xT", "q", "k", "v"))
        acc = [s.ps(f"acc{k}", [P, D]) for k in range(BANKS)]
        pkv, pks = s.ps("pkv", [P, D]), s.ps("pks", [P, D])
        s_w, s_const = s.sem("weights"), s.sem("constants")
        s_x = [s.sem(f"xT_in{j}") for j in range(U)]
        s_qo = [s.sem(f"q_out{j}") for j in range(U)]
        s_mm, s_q, s_k, s_v, s_kv, s_end = (s.sem(n) for n in ("products", "queries", "keys", "values", "kv", "blocks"))
        with nc.Block() as block:
            @block.sync
            def _(sp):
                for k in range(3):
                    sp.dma_start(W[:, :, D * k:D * (k + 1)],
                                 io["w_mix1"][:, D * k:D * (k + 1)].rearrange("(c p) n -> p c n", p=P)).then_inc(s_w, 16)
                sp.dma_start(half[:], io["half"][:, :]).then_inc(s_w, 16)

                def body(i):
                    for j in range(U):
                        n = U * i + j
                        need(sp, s_mm, 3 * (n - U + 1))
                        sp.dma_start(xT[:, j, :], io["xhT"][n]).then_inc(s_x[j], 16)
                passes(sp, NB, body)

            @block.vector
            def _(vec):
                vec.memset(ones[:], 1.0).then_inc(s_const, 1)
                vec.memset(zeros[:], 0.0).then_inc(s_const, 1)

                def body(i):
                    for j in range(U):
                        n = U * i + j
                        last = last_tile(n)
                        vec.wait_ge(s_mm, 3 * n + 1)
                        need(vec, s_qo[j], 16 * i)
                        vec.tensor_scalar(q[:, j, :], acc[3 * j % BANKS][:], 0.0, DH ** -0.5, ALU.max, ALU.add).then_inc(s_q, 1)
                        vec.wait_ge(s_mm, 3 * n + 2)
                        need(vec, s_kv, n - U + 1)
                        ins = vec.tensor_scalar(k_[:, j, :], acc[(3 * j + 1) % BANKS][:], 0.0, DH ** -0.5, ALU.max, ALU.add)
                        if last:
                            ins.then_inc(s_end, 1)
                            vec.wait_ge(s_end, 1)
                            ins = vec.tensor_scalar(k_[:, j, :], k_[:, j, :], keep.valid[:, NT - 1:NT], None, ALU.mult)
                        ins.then_inc(s_k, 1)
                passes(vec, NB, body)
                vec.wait_ge(s_w, 64)
                vec.wait_ge(s_kv, NT)
                for c in range(KC):
                    vec.tensor_tensor(keep.kv[:, c, :].rearrange("p (h d) -> p h d", h=2),
                                      pkv[:, P * c:P * (c + 1)].rearrange("p (h d) -> p h d", h=2),
                                      half[:].unsqueeze(2).broadcast_to([P, 2, DH]), ALU.mult)
                vec.tensor_tensor(keep.ksum[:], pks[:, 0:KC].unsqueeze(2).broadcast_to([P, KC, 2]),
                                  half[:].unsqueeze(1).broadcast_to([P, KC, 2]), ALU.mult).then_inc(s_end, 1)
                vec.wait_ge(s_end, 2)

            @block.scalar
            def _(act):
                def body(i):
                    for j in range(U):
                        n = U * i + j
                        act.wait_ge(s_mm, 3 * n + 3)
                        need(act, s_kv, n - U + 1)
                        act.activation(v[:, j, :], acc[(3 * j + 2) % BANKS][:], ACT.Copy).then_inc(s_v, 1)
                        act.wait_ge(s_q, n + 1)
                        act.dma_start(io["qT"][n], q[:, j, :]).then_inc(s_qo[j], 16)
                passes(act, NB, body)
                for j in range(U):
                    act.wait_ge(s_qo[j], 16 * NB)

            @block.tensor
            def _(pe):
                pe.wait_ge(s_const, 2)
                pe.wait_ge(s_w, 64)
                pe.matmul(pkv[:], zeros[:, 0:P], zeros[:], start=True, stop=False, skip_group_check=True)
                pe.matmul(pks[:, 0:KC], zeros[:, 0:P], zeros[:, 0:KC], start=True, stop=False, skip_group_check=True)

                def products(i, j):
                    n = U * i + j
                    pe.wait_ge(s_x[j], 16 * (i + 1))
                    for w in range(3):
                        m, b = 3 * n + w, (3 * j + w) % BANKS
                        prev = m - BANKS
                        sem = (s_q, s_k, s_v)[(w - BANKS) % 3]
                        need(pe, sem, n - 1 if w < 2 else n)
                        for f in range(KC):
                            for c in range(KC) if w == 0 or f == 0 else ():
                                if w == 0:
                                    ins = pe.matmul(acc[b][:, P * f:P * (f + 1)], W[:, c, P * f:P * (f + 1)],
                                                    xT[:, j, P * c:P * (c + 1)], start=c == 0, stop=c == KC - 1)
                                else:
                                    ins = pe.matmul(acc[b][:], xT[:, j, P * c:P * (c + 1)], W[:, c, D * w:D * (w + 1)],
                                                    start=c == 0, stop=c == KC - 1)
                        ins.then_inc(s_mm, 1)

                def sums(i, j, n):
                    pe.wait_ge(s_v, n + 1)
                    pe.wait_ge(s_k, n + 1)
                    last = last_tile(n)
                    for c in range(KC):
                        cols = slice(P * c, P * (c + 1))
                        pe.matmul(pkv[:, cols], k_[:, j, cols], v[:, j, cols], start=False, stop=last and c == KC - 1,
                                  skip_group_check=True)
                        ins = pe.matmul(pks[:, c:c + 1], k_[:, j, cols], ones[:], start=False,
                                        stop=last and c == KC - 1, skip_group_check=True)
                    ins.then_inc(s_kv, 1)

                def body(i):
                    for j in range(U):
                        n = U * i + j
                        products(i, j)
                        if not (isinstance(n, int) and n == 0):
                            sums(i, (j - 1) % U, n - 1)
                passes(pe, NB, body)
                sums(NB - 1, U - 1, NT - 1)


def edges1(nc, io, keep):
    with Stage(nc, "m1") as s:
        S, R, B = EU, 4, 4
        SD = EH
        GATHER, PAIR = 10, 8
        BW = B * P
        w_c, w_f1, w_2 = s.sb("w_c", [P, HID]), s.sb("w_f1", [HID, HID]), s.sb("w_2", [2 * HID, D])
        sh = s.sb("sh", [P, ET, 4])
        ones = s.sb("ones", [2, P], BF16)
        ig, il = s.sb("ig", [P, 2, 2, EH], I32), s.sb("il", [P, 2, EH], I32)
        attr = s.sb("attr", [HID, 2, EH * P])
        line = s.sb("line", [2, 2, EH * P], BF16)
        srow, drow = s.sb("srow", [P, S, SW]), s.sb("drow", [P, SD, DW])
        ipT = s.sb("ipT", [P, BW])
        soft, hid = s.sb("soft", [2 * HID, BW]), s.sb("hid", [2 * HID, 2, BW])
        w = s.sb("w", [P, 2, D])
        xs, xd = s.sb("xs", [P, 2, D]), s.sb("xd", [P, 2, 3 * P])
        dot, x0w = s.sb("dot", [P, 2, P]), s.sb("x0w", [P, 2, P])
        msg, same, out = s.sb("msg", [P, 2, D]), s.sb("same", [P, 2, B, P]), s.sb("out", [P, R, D])
        pip, ph, pm, pd = s.ps("pip", [P, D]), s.ps("ph", [2 * HID, D]), s.ps("pm", [P, D]), s.ps("pd", [P, D])
        pws, pwf = ([s.ps(f"{n}{k}", [P, D]) for k in range(2)] for n in ("pws", "pwf"))
        s_w, s_pre, s_const = s.sem("weights"), s.sem("prepared"), s.sem("constants")
        s_ig, s_il, s_line, s_attr = ([s.sem(f"{n}{h}") for h in range(2)] for n in ("gather_ix", "lead_ix", "line", "attributes"))
        s_g = [s.sem(f"gathered{k}") for k in range(S)]
        s_add = [s.sem(f"added{k}") for k in range(R)]
        s_go = s.sem("go")
        s_prod, s_ip, s_ipT, s_h, s_soft, s_hid, s_wm, s_wf, s_w2, s_xs, s_st, s_bc, s_same, s_msg, s_seg, s_row = (s.sem(n) for n in (
            "pair_products", "inner", "innerT", "hidden_sums", "soft_steps", "hidden", "weight_products", "factors", "edge_weights", "scaled",
            "steps", "destinations", "same", "messages", "sums", "rows"))
        s_go2, s_go_line = s.sem("go_scalar"), s.sem("go_line")
        DV = 6

        def at(b, k):
            if isinstance(b, int) and not 0 <= EU * b + k < ET:
                return None
            return b + k // EU, k % EU

        with nc.Block() as block:
            @block.sync
            def _(sp):
                sp.dma_start(w_c[:], io["w_s1"][2 * P:3 * P, :]).then_inc(s_w, 16)
                sp.dma_start(w_f1[:], io["w_f1"][:, :]).then_inc(s_w, 16)
                sp.dma_start(w_2[0:HID, :], io["w_s2"][:, :]).then_inc(s_w, 16)
                sp.dma_start(w_2[HID:2 * HID, :], io["w_f2"][:, :]).then_inc(s_w, 16)
                sp.dma_start(sh[:], io["sh"].rearrange("p (t k) -> p t k", k=4)).then_inc(s_w, 16)
                lines = io["src_l"].rearrange("k p t -> k (p t)")

                def body(b):
                    for h in range(2):
                        cols = bass.ds((2 * b + h) * EH * P, EH * P)
                        need(sp, s_prod, EU * (b - 1) + EH * (h + 1))
                        sp.dma_start(ig[:, h, 0, :], io["src_ix"][b, :, EH * h:EH * (h + 1)]).then_inc(s_ig[h], 16)
                        sp.dma_start(ig[:, h, 1, :], io["dst_ix"][b, :, EH * h:EH * (h + 1)]).then_inc(s_ig[h], 16)
                        need(sp, s_h, 4 * (b - 1) + 2 * (h + 1))
                        sp.dma_start(attr[:, h, :], io["attr"][:, cols]).then_inc(s_attr[h], 16)
                        need(sp, s_bc, 4 * (b - 1) + 2 * (h + 1))
                        sp.sem_inc(s_go_line, 1)
                        sp.dma_start(line[:, h, :], lines[:, cols]).then_inc(s_line[h], 16)
                        for r in range(R):
                            need(sp, s_add[r], 16 * (EU // R * (b - 1) + EH // R * (h + 1)))
                        sp.dma_start(il[:, h, :], io["lead_ix1"][:, bass.ds(EU * b + EH * h, EH)]).then_inc(s_il[h], 16)
                passes(sp, EB, body)

            @block.gpsimd
            def _(pool):
                def gather(b, k):
                    t = EU * b + k
                    if k % EH == 0:
                        pool.wait_ge(s_ig[k // EH], 32 * (b + 1))
                    need(pool, s_msg, t - S + 1)
                    need(pool, s_h, 4 * b + k // 4 - 1)
                    pool.sem_inc(s_go, 1)
                    for n, row, table in ((0, drow[:, k % SD, :], io["drow"]), (1, srow[:, k % S, :], io["srow"])):
                        pool.indirect_dma_start(
                            row, None, table,
                            bass.IndirectOffsetOnAxis(ap=ig[:, k // EH, n, k % EH:k % EH + 1], axis=0),
                        ).then_inc(s_g[k % S], 16)

                def scatter(b, k):
                    t = EU * b + k
                    if k % EH == 0:
                        pool.wait_ge(s_il[k // EH], 16 * (b + 1))
                    pool.wait_ge(s_row, t + 1)
                    prev = k - NACC
                    need(pool, s_add[prev % R], 16 * (EU // R * b + prev // R + 1))
                    pool.sem_inc(s_go, 1)
                    pool.indirect_dma_start(
                        io["acc1"][k % NACC], bass.IndirectOffsetOnAxis(ap=il[:, k // EH, k % EH:k % EH + 1], axis=0),
                        out[:, k % R, :], None, compute_op=ALU.add,
                    ).then_inc(s_add[k % R], 16)

                def body(b):
                    for k in range(EU):
                        if there := at(b, k + GATHER):
                            gather(*there)
                        if there := at(b, k - 3):
                            scatter(*there)
                for k in range(GATHER):
                    gather(0, k)
                passes(pool, EB, body)
                scatter(EB - 1, EU - 3)
                scatter(EB - 1, EU - 2)
                scatter(EB - 1, EU - 1)
                for r in range(R):
                    pool.wait_ge(s_add[r], 16 * (ET // R))

            @block.vector
            def _(vec):
                vec.memset(ones[:], 1.0).then_inc(s_const, 1)
                vec.wait_ge(s_w, 80)
                vec.tensor_scalar(w_c[:], w_c[:], 1.0 / 3.0, None, ALU.mult).then_inc(s_pre, 1)
                w_dot = w_2[HID:2 * HID, 3 * P:D]
                vec.tensor_scalar(w_dot, w_dot, 3.0 ** -0.5, None, ALU.mult).then_inc(s_pre, 1)
                vec.wait_ge(s_pre, 2)
                st = Steps(vec, s_st, DV)

                def pair(b, k):
                    vec.wait_ge(s_g[k], 32 * (b + 1))
                    vectors = drow[:, k % SD, 0:3 * P]
                    vec.tensor_tensor(vectors, vectors, srow[:, k % S, 0:3 * P], ALU.mult).then_inc(s_prod, 1)

                def hidden(b, k):
                    q = 4 * b + k // B
                    vec.wait_ge(s_soft, 3 * (q + 1))
                    need(vec, s_wm, B * (q - 1))
                    vec.scalar_tensor_tensor(hid[:, k // B % 2, :], ph[:], 0.0, soft[:], ALU.max, ALU.add).then_inc(s_hid, 1)

                def equals(b, k):
                    q = 4 * b + k // B
                    vec.wait_ge(s_bc, q + 1)
                    need(vec, s_seg, B * (q - 1))
                    vec.tensor_tensor(same[:, k // B % 2], pd[:].rearrange("p (a n) -> p a n", a=B),
                                      keep.src[:, bass.ds(B * q, B)].unsqueeze(2).broadcast_to([P, B, P]),
                                      ALU.is_equal).then_inc(s_same, 1)

                def message(b, k):
                    t, par = EU * b + k, k % 2
                    st.begin(t)
                    ws, msgs = w[:, par, :], msg[:, par, :]
                    x0 = srow[:, k % S, 3 * P:4 * P]

                    def three(x):
                        return x.rearrange("p (c u) -> p c u", c=3)
                    vec.wait_ge(s_xs, t + 1)
                    st.did(vec.tensor_tensor(dot[:, par, :], xd[:, par, 0:P], xd[:, par, P:2 * P], ALU.add))
                    vec.wait_ge(s_wf, t + 1)
                    vec.tensor_tensor(ws, pws[par][:], ws, ALU.mult).then_inc(s_w2, 1)
                    st.wait()
                    st.did(vec.tensor_tensor(dot[:, par, :], dot[:, par, :], xd[:, par, 2 * P:3 * P], ALU.add))
                    vec.wait_ge(s_w2, t + 1)
                    need(vec, s_seg, t - 1)
                    st.did(vec.tensor_tensor(x0w[:, par, :], x0, ws[:, P:2 * P], ALU.mult))
                    st.did(vec.tensor_tensor(three(msgs[:, P:D]), three(xs[:, par, P:D]),
                                             ws[:, 2 * P:3 * P].unsqueeze(1).broadcast_to([P, 3, P]), ALU.mult))
                    st.did(vec.tensor_tensor(msgs[:, 0:P], xs[:, par, 0:P], ws[:, 0:P], ALU.mult))
                    vec.wait_ge(s_st, DV * t + 2)
                    st.did(vec.tensor_tensor(dot[:, par, :], dot[:, par, :], ws[:, 3 * P:D], ALU.mult))
                    vec.wait_ge(s_st, DV * t + 4)
                    for c in range(3):
                        m = msgs[:, P * (c + 1):P * (c + 2)]
                        vec.scalar_tensor_tensor(m, x0w[:, par, :], sh[:, t, 1 + c:2 + c], m, ALU.mult, ALU.add)
                    st.wait()
                    vec.tensor_tensor(msgs[:, 0:P], msgs[:, 0:P], dot[:, par, :], ALU.add).then_inc(s_msg, 1)
                    st.end()

                for k in range(B):
                    pair(0, k)
                equals(0, 0)
                for k in range(B, PAIR):
                    pair(0, k)
                hidden(0, 0)

                def body(b):
                    for k in range(EU):
                        if there := at(b, k + PAIR):
                            pair(*there)
                        if k % B == 1 and (there := at(b, k + 3)):
                            equals(*there)
                        message(b, k)
                        if k % B == 2 and (there := at(b, k + 2)):
                            hidden(*there)
                passes(vec, EB, body)

            @block.scalar
            def _(act):
                act.preload_act_table_set("natural_log_exp_and_others")
                act.wait_ge(s_w, 80)

                def scaled(b, k):
                    t, par = EU * b + k, k % 2
                    act.wait_ge(s_g[k], 32 * (b + 1))
                    need(act, s_msg, t - 1)
                    act.sem_inc(s_go2, 1)
                    act.activation(xs[:, par, :], srow[:, k % S, 3 * P:SW], ACT.Copy, scale=sh[:, t, 0:1])
                    for c in range(3):
                        ins = act.activation(xd[:, par, P * c:P * (c + 1)], srow[:, k % S, P * (4 + c):P * (5 + c)], ACT.Copy,
                                             scale=sh[:, t, 1 + c:2 + c])
                    ins.then_inc(s_xs, 1)

                def factor(b, k):
                    t, par = EU * b + k, k % 2
                    act.wait_ge(s_wm, t + 1)
                    act.activation(w[:, par, :], pwf[par][:], ACT.Copy).then_inc(s_wf, 1)

                def turn(b, k):
                    q = 4 * b + k // B
                    act.wait_ge(s_ip, B * (q + 1))
                    need(act, s_h, q)
                    act.activation(ipT[:], pip[:], ACT.Copy).then_inc(s_ipT, 1)

                def soften(b, k):
                    q = 4 * b + k // B
                    act.wait_ge(s_h, q + 1)
                    need(act, s_hid, q)
                    act.activation(soft[:], ph[:], ACT.Abs).then_inc(s_soft, 1)
                    act.wait_ge(s_soft, 3 * q + 1)
                    act.activation(soft[:], soft[:], ACT.Exp, scale=-1.0).then_inc(s_soft, 1)
                    act.wait_ge(s_soft, 3 * q + 2)
                    act.activation(soft[:], soft[:], ACT.Ln, scale=0.5, bias=0.5).then_inc(s_soft, 1)

                def rows(b, k):
                    t = EU * b + k
                    act.wait_ge(s_seg, t + 1)
                    need(act, s_add[k % R], 16 * (EU // R * b + k // R))
                    act.activation(out[:, k % R, :], pm[:], ACT.Copy).then_inc(s_row, 1)

                turn(0, 0)
                soften(0, 0)
                scaled(0, 0)
                factor(0, 0)

                def body(b):
                    for k in range(EU):
                        if there := at(b, k - 2):
                            rows(*there)
                        if k % B == 1 and (there := at(b, k + 3)):
                            turn(*there)
                        if k % B == 2 and (there := at(b, k + 2)):
                            soften(*there)
                        if there := at(b, k + 1):
                            scaled(*there)
                            factor(*there)
                passes(act, EB, body)
                rows(EB - 1, EU - 2)
                rows(EB - 1, EU - 1)

            @block.tensor
            def _(pe):
                pe.wait_ge(s_const, 1)
                pe.wait_ge(s_pre, 2)

                def inner(b, k):
                    t = EU * b + k
                    pe.wait_ge(s_prod, t + 1)
                    if k % B == 0:
                        need(pe, s_ipT, 4 * b + k // B)
                    for c in range(3):
                        ins = pe.matmul(pip[:, P * (k % B):P * (k % B + 1)], drow[:, k % SD, P * c:P * (c + 1)], keep.ident[:],
                                        start=c == 0, stop=c == 2)
                    ins.then_inc(s_ip, 1)

                def spread(b, k):
                    q = 4 * b + k // B
                    pe.wait_ge(s_line[k // EH], 16 * (b + 1))
                    need(pe, s_same, q)
                    pe.matmul(pd[:], ones[:], line[:, k // EH, BW * (k // B % 2):BW * (k // B % 2 + 1)],
                              start=True, stop=True).then_inc(s_bc, 1)

                def hidden(b, k):
                    q = 4 * b + k // B
                    pe.wait_ge(s_ipT, q + 1)
                    pe.wait_ge(s_attr[k // EH], 16 * (b + 1))
                    need(pe, s_hid, q)
                    pe.matmul(ph[0:HID, :], w_c[:], ipT[:], start=True, stop=False)
                    pe.matmul(ph[HID:2 * HID, :], w_f1[:], attr[:, k // EH, BW * (k // B % 2):BW * (k // B % 2 + 1)],
                              start=True, stop=True)
                    for n in range(B):
                        ins = pe.matmul(ph[0:HID, P * n:P * (n + 1)], drow[:, (k + n) % SD, 3 * P:DW], keep.ident[:],
                                        start=False, stop=n == B - 1)
                    ins.then_inc(s_h, 1)

                def weights(b, k):
                    t, par, cols = EU * b + k, k // B % 2, slice(P * (k % B), P * (k % B + 1))
                    pe.wait_ge(s_hid, 4 * b + k // B + 1)
                    need(pe, s_w2, t - 1)
                    pe.matmul(pws[k % 2][:], hid[0:HID, par, cols], w_2[0:HID, :], start=True, stop=True)
                    pe.matmul(pwf[k % 2][:], hid[HID:2 * HID, par, cols], w_2[HID:2 * HID, :], start=True, stop=True).then_inc(s_wm, 1)

                def sums(b, k):
                    t = EU * b + k
                    pe.wait_ge(s_same, 4 * b + k // B + 1)
                    pe.wait_ge(s_msg, t + 1)
                    need(pe, s_row, t)
                    pe.matmul(pm[:], same[:, k // B % 2, k % B, :], msg[:, k % 2, :], start=True, stop=True).then_inc(s_seg, 1)

                for k in range(B):
                    inner(0, k)
                spread(0, 0)
                hidden(0, 0)
                for k in range(B, PAIR - 1):
                    inner(0, k)
                weights(0, 0)

                def body(b):
                    for k in range(EU):
                        if there := at(b, k + 1):
                            weights(*there)
                        if there := at(b, k - 1):
                            sums(*there)
                        if there := at(b, k + PAIR - 1):
                            inner(*there)
                        if k % B == 0 and (there := at(b, k + B)):
                            spread(*there)
                        if k % B == 1 and (there := at(b, k + 3)):
                            hidden(*there)
                passes(pe, EB, body)
                sums(EB - 1, EU - 1)


def merge1(nc, io, keep):
    with Stage(nc, "g1") as s:
        w_o0, w_o1, w_p = s.sb("w_o0", [P, P]), s.sb("w_o1", [P, P]), s.sb("w_p", [P, KC, D])
        a0, a1, own, q, o, aT, oT = (s.sb(n, [P, U, D]) for n in ("a0", "a1", "own", "q", "o", "aT", "oT"))
        zo = s.sb("zo", [P, H])
        po, pn, tpa, tpo = s.ps("po", [P, D]), s.ps("pn", [P, H]), s.ps("tpa", [P, D]), s.ps("tpo", [P, D])
        pout = [s.ps(f"pout{k}", [P, D]) for k in range(2)]
        s_w = s.sem("weights")
        s_in = [s.sem(f"in{j}") for j in range(U)]
        s_st, s_x0, s_agg, s_o, s_po, s_ta, s_to, s_aT, s_oT, s_mm, s_x = (s.sem(n) for n in (
            "steps", "x_scalars", "edges", "mixed", "attended", "edgesT", "mixedT", "aT", "oT", "products", "x"))
        with nc.Block() as block:
            @block.sync
            def _(sp):
                sp.dma_start(w_o0[:], io["w_o0"][:, :]).then_inc(s_w, 16)
                sp.dma_start(w_o1[:], io["w_o1"][:, :]).then_inc(s_w, 16)
                sp.dma_start(w_p[:], io["w_proj"].rearrange("(c p) n -> p c n", p=P)).then_inc(s_w, 16)

                def body(i):
                    for j in range(U):
                        n = U * i + j
                        need(sp, s_ta, n - U + 1)
                        need(sp, s_po, n - U + 1)
                        rows = bass.ds(n * P, P)
                        sp.dma_start(a0[:, j, :], io["acc1"][0][rows, :]).then_inc(s_in[j], 16)
                        sp.dma_start(a1[:, j, :], io["acc1"][1][rows, :]).then_inc(s_in[j], 16)
                        sp.dma_start(own[:, j, :], io["srow"][rows, 3 * P:SW]).then_inc(s_in[j], 16)
                        sp.dma_start(q[:, j, :], io["qT"][n]).then_inc(s_in[j], 16)
                passes(sp, NB, body)

            @block.vector
            def _(vec):
                st = Steps(vec, s_st, 3)

                def ahead(i, j):
                    n = U * i + j
                    st.begin(n)
                    vec.wait_ge(s_in[j], 64 * (i + 1))
                    st.did(vec.tensor_tensor(a1[:, j, :], a1[:, j, :], own[:, j, :], ALU.add))
                    st.wait()
                    vec.tensor_tensor(a0[:, j, :], a0[:, j, :], a1[:, j, :], ALU.add).then_inc(s_agg, 1)
                    vec.wait_ge(s_po, n + 1)
                    st.did(vec.tensor_scalar(zo[:], pn[:], 1e-6, None, ALU.add))
                    st.wait()
                    st.did(vec.reciprocal(zo[:], zo[:]))
                    st.wait()
                    need(vec, s_to, n - U + 1)
                    vec.tensor_tensor(by_head(o[:, j, :]), by_head(po[:]), over_head(zo[:]), ALU.mult).then_inc(s_o, 1)

                def add(i, j):
                    n = U * i + j
                    vec.wait_ge(s_mm, n + 1)
                    x = keep.X[:, n, :]
                    vec.tensor_tensor(x[:, 0:P], x[:, 0:P], pout[j % 2][:, 0:P], ALU.add).then_inc(s_x0, 1)
                    vectors = x[:, P:D].rearrange("p (u c) -> p c u", c=3)
                    vec.tensor_tensor(vectors, vectors, pout[j % 2][:, P:D].rearrange("p (c u) -> p c u", c=3),
                                      ALU.add).then_inc(s_x, 1)
                    vec.wait_ge(s_x, n + 1)
                    vec.wait_ge(s_x0, n + 1)
                    vec.bn_stats(keep.stats[:, n, :], x)

                ahead(0, 0)

                def body(i):
                    for j in range(U):
                        if not last_tile(U * i + j):
                            ahead(i + (j + 1) // U, (j + 1) % U)
                        add(i, j)
                passes(vec, NB, body)

            @block.scalar
            def _(act):
                def body(i):
                    for j in range(U):
                        n = U * i + j
                        act.wait_ge(s_ta, n + 1)
                        need(act, s_mm, n - U + 1)
                        act.activation(aT[:, j, :], tpa[:], ACT.Copy).then_inc(s_aT, 1)
                        act.wait_ge(s_to, n + 1)
                        act.activation(oT[:, j, :], tpo[:], ACT.Copy).then_inc(s_oT, 1)
                passes(act, NB, body)

            @block.tensor
            def _(pe):
                def edges(i, j):
                    n = U * i + j
                    pe.wait_ge(s_in[j], 64 * (i + 1))
                    need(pe, s_o, n)
                    attend(pe, q[:, j, :], keep.kv, keep.ksum, po, pn).then_inc(s_po, 1)
                    pe.wait_ge(s_agg, n + 1)
                    need(pe, s_aT, n)
                    for c in range(KC):
                        cols = slice(P * c, P * (c + 1))
                        ins = pe.transpose(tpa[:, cols], a0[:, j, cols], keep.ident[:])
                    ins.then_inc(s_ta, 1)

                def mixed(i, j):
                    n = U * i + j
                    pe.wait_ge(s_o, n + 1)
                    need(pe, s_oT, n)
                    for c in range(KC):
                        cols = slice(P * c, P * (c + 1))
                        ins = pe.transpose(tpo[:, cols], o[:, j, cols], keep.ident[:])
                    ins.then_inc(s_to, 1)

                pe.wait_ge(s_w, 48)
                edges(0, 0)
                mixed(0, 0)

                def body(i):
                    for j in range(U):
                        n = U * i + j
                        nxt = (i + (j + 1) // U, (j + 1) % U)
                        if not last_tile(n):
                            edges(*nxt)
                        pe.wait_ge(s_oT, n + 1)
                        need(pe, s_x, n if j == 0 else n - 1)
                        for c in range(KC):
                            pe.matmul(pout[j % 2][:], oT[:, j, P * c:P * (c + 1)], w_p[:, c, :], start=c == 0, stop=False)
                        for c in range(KC):
                            cols = slice(P * c, P * (c + 1))
                            ins = pe.matmul(pout[j % 2][:, cols], aT[:, j, cols], w_o0[:] if c == 0 else w_o1[:],
                                            start=False, stop=c == KC - 1)
                        ins.then_inc(s_mm, 1)
                        if not last_tile(n):
                            mixed(*nxt)
                passes(pe, NB, body)


def route1(nc, io, keep):
    with Stage(nc, "r1") as s:
        xn, xT = s.sb("xn", [P, U, D]), s.sb("xT", [P, U, D])
        ones, zeros = s.sb("ones", [P, 1]), s.sb("zeros", [P, P])
        wg, bg, order = s.sb("wg", [P, KC, NX1]), s.sb("bg", [P, NX1]), s.sb("order", [P, NX1])
        mean, l, m, pick = s.sb("mean", [P, KC]), s.sb("l", [P, NX1]), s.sb("m", [P, 4]), s.sb("pick", [P, 2, NX1])
        tp = [s.ps(f"tp{k}", [P, D]) for k in range(2)]
        pmean, pl = s.ps("pmean", [P, KC]), s.ps("pl", [P, NX1])
        s_w, s_f, s_xn, s_tp, s_xT, s_sum, s_mean, s_l, s_st, s_e, s_const = (s.sem(n) for n in (
            "weights", "valid_factors", "normed", "transposed", "xT", "sums", "mean", "logits", "steps", "exps", "constants"))
        s_out = [s.sem(f"xT_out{j}") for j in range(U)]
        with nc.Block() as block:
            @block.sync
            def _(sp):
                sp.dma_start(wg[:], io["wg1"].rearrange("(c p) n -> p c n", p=P)).then_inc(s_w, 16)
                sp.dma_start(bg[:], io["bg1"][:, :]).then_inc(s_w, 16)
                sp.dma_start(order[:], io["order"][:, :]).then_inc(s_w, 16)

                def body(i):
                    for j in range(U):
                        sp.wait_ge(s_xT, U * i + j + 1)
                        sp.dma_start(io["xhT"][U * i + j], xT[:, j, :]).then_inc(s_out[j], 16)
                passes(sp, NB, body)
                for j in range(U):
                    sp.wait_ge(s_out[j], 16 * NB)

            @block.scalar
            def _(act):
                def body(i):
                    for j in range(U):
                        n = U * i + j
                        act.wait_ge(s_tp, n + 1)
                        need(act, s_out[j], 16 * i)
                        act.activation(xT[:, j, :], tp[j % 2][:], ACT.Copy).then_inc(s_xT, 1)
                passes(act, NB, body)
                act.wait_ge(s_st, 3)
                act.activation(l[:], l[:], ACT.Exp).then_inc(s_e, 1)

            @block.vector
            def _(vec):
                vec.memset(ones[:], 1.0).then_inc(s_const, 1)
                vec.memset(zeros[:], 0.0).then_inc(s_const, 1)
                vec.tensor_tensor(keep.rstd[:], keep.rstd[:], keep.valid[:], ALU.mult).then_inc(s_f, 1)
                vec.wait_ge(s_f, 1)

                def body(i):
                    for j in range(U):
                        n = U * i + j
                        need(vec, s_tp, n - U + 1)
                        vec.tensor_scalar(xn[:, j, :], keep.X[:, n, :], keep.mean[:, bass.ds(n, 1)],
                                          keep.rstd[:, bass.ds(n, 1)], ALU.subtract, ALU.mult).then_inc(s_xn, 1)
                passes(vec, NB, body)
                st = Steps(vec, s_st, 0)
                st.begin(0)
                vec.wait_ge(s_w, 48)
                vec.wait_ge(s_sum, NT)
                vec.tensor_scalar(mean[:], pmean[:], 1.0 / N, None, ALU.mult).then_inc(s_mean, 1)
                vec.wait_ge(s_l, 1)
                st.did(vec.tensor_tensor(l[:], pl[:], bg[:], ALU.add))
                st.wait()
                st.did(vec.tensor_reduce(m[:, 0:1], l[:], AX, ALU.max))
                st.wait()
                st.did(vec.tensor_scalar(l[:], l[:], m[:, 0:1], None, ALU.subtract))
                vec.wait_ge(s_e, 1)
                st.did(vec.tensor_reduce(m[:, 1:2], l[:], AX, ALU.add))
                st.wait()
                st.did(vec.reciprocal(m[:, 1:2], m[:, 1:2]))
                st.wait()
                st.did(vec.tensor_scalar(l[:], l[:], m[:, 1:2], None, ALU.mult))
                st.wait()
                st.did(vec.tensor_reduce(keep.gate[:], l[:], AX, ALU.max))
                st.wait()
                st.did(vec.tensor_scalar(pick[:, 0, :], l[:], keep.gate[:], float(NX1), ALU.is_lt, ALU.mult))
                st.wait()
                st.did(vec.tensor_tensor(pick[:, 1, :], pick[:, 0, :], order[:], ALU.add))
                st.wait()
                st.did(vec.tensor_reduce(m[:, 2:3], pick[:, 1, :], AX, ALU.min))
                st.wait()
                st.did(vec.tensor_copy(keep.expert[:], m[:, 2:3]))
                st.wait()

            @block.tensor
            def _(pe):
                pe.wait_ge(s_const, 2)
                pe.wait_ge(s_w, 48)
                pe.matmul(pmean[:], zeros[:], zeros[:, 0:KC], start=True, stop=False, skip_group_check=True)

                def body(i):
                    for j in range(U):
                        n = U * i + j
                        pe.wait_ge(s_xn, n + 1)
                        need(pe, s_xT, n if j == 0 else n - 1)
                        for c in range(KC):
                            ins = pe.matmul(pmean[:, c:c + 1], xn[:, j, P * c:P * (c + 1)], ones[:], start=False,
                                            stop=last_tile(n) and c == KC - 1, skip_group_check=True)
                        ins.then_inc(s_sum, 1)
                        for c in range(KC):
                            cols = slice(P * c, P * (c + 1))
                            ins = pe.transpose(tp[j % 2][:, cols], xn[:, j, cols], keep.ident[:])
                        ins.then_inc(s_tp, 1)
                passes(pe, NB, body)
                pe.wait_ge(s_mean, 1)
                for c in range(KC):
                    ins = pe.matmul(pl[:], mean[:, c:c + 1].broadcast_to([P, P]), wg[:, c, :], start=c == 0, stop=c == KC - 1)
                ins.then_inc(s_l, 1)


def linear1(nc, io, keep):
    with Stage(nc, "l1") as s:
        W, be = s.sb("w", [P, KC, D]), s.sb("be", [P, D])
        xT, y, out = s.sb("xT", [P, U, D]), s.sb("y", [P, U, D]), s.sb("out", [P, U, D])
        pout = [s.ps(f"pout{k}", [P, D]) for k in range(U)]
        s_w, s_mm, s_y, s_o = s.sem("weights"), s.sem("products"), s.sem("biased"), s.sem("rows")
        s_x = [s.sem(f"xT_in{j}") for j in range(U)]
        s_out = [s.sem(f"out{j}") for j in range(U)]
        with nc.Block() as block:
            @block.sync
            def _(sp):
                e = sp.value_load(keep.expert[0:1, 0:1], min_val=0, max_val=NX1 - 1)
                sp.dma_start(W[:], io["we"][bass.ds(e, 1)].rearrange("a (c p) n -> p (a c) n", p=P)).then_inc(s_w, 16)
                sp.dma_start(be[:], io["be"][bass.ds(e, 1)].rearrange("a n -> (a n)").partition_broadcast(P)).then_inc(s_w, 16)

                def body(i):
                    for j in range(U):
                        n = U * i + j
                        need(sp, s_mm, n - U + 1)
                        sp.dma_start(xT[:, j, :], io["xhT"][n]).then_inc(s_x[j], 16)
                passes(sp, NB, body)

            @block.tensor
            def _(pe):
                pe.wait_ge(s_w, 32)

                def body(i):
                    for j in range(U):
                        n = U * i + j
                        pe.wait_ge(s_x[j], 16 * (i + 1))
                        need(pe, s_y, n - U + 1)
                        for c in range(KC):
                            ins = pe.matmul(pout[j][:], xT[:, j, P * c:P * (c + 1)], W[:, c, :], start=c == 0, stop=c == KC - 1)
                        ins.then_inc(s_mm, 1)
                passes(pe, NB, body)

            @block.vector
            def _(vec):
                vec.wait_ge(s_w, 32)

                def body(i):
                    for j in range(U):
                        n = U * i + j
                        vec.wait_ge(s_mm, n + 1)
                        need(vec, s_o, n - U + 1)
                        vec.tensor_tensor(y[:, j, :], pout[j][:], be[:], ALU.add).then_inc(s_y, 1)
                        vec.wait_ge(s_y, n + 1)
                        need(vec, s_out[j], 16 * i)
                        vec.scalar_tensor_tensor(out[:, j, :], y[:, j, :], keep.gate[:], keep.X[:, n, :],
                                                 ALU.mult, ALU.add).then_inc(s_o, 1)
                passes(vec, NB, body)

            @block.scalar
            def _(act):
                def body(i):
                    for j in range(U):
                        n = U * i + j
                        act.wait_ge(s_o, n + 1)
                        rows = N - P * (NT - 1) if last_tile(n) else P
                        act.dma_start(io["out"][bass.ds(P * n, rows), :], out[0:rows, j, :]).then_inc(s_out[j], 16)
                passes(act, NB, body)
                for j in range(U):
                    act.wait_ge(s_out[j], 16 * NB)


class Kept:
    pass


def program(nc, io, stop=99):
    with Stage(nc, "keep") as s:
        keep = Kept()
        keep.X = s.sb("x", [P, NT, D])
        keep.ident = s.sb("ident", [P, P])
        keep.stats = s.sb("stats", [P, NT, 6])
        keep.mean, keep.rstd, keep.rstd2 = (s.sb(n, [P, NT]) for n in ("mean", "rstd", "rstd2"))
        keep.valid = s.sb("valid", [P, NT])
        keep.dst, keep.src = s.sb("dst", [P, ET]), s.sb("src", [P, ET])
        todo = [stop]

        def run(stage, *more):
            todo[0] -= 1
            if todo[0] >= 0:
                stage(nc, io, keep, *more)

        run(load_consts)
        run(tables0)
        with Stage(nc, "keep0") as s0:
            keep.kv, keep.ksum = s0.sb("kv", [P, KC, P]), s0.sb("ksum", [P, KC, 2])
            with Stage(nc, "keep1") as s1:
                keep.att, keep.count = s1.sb("att", [P, ET, H]), s1.sb("count", [P, ET])
                run(scores0)
                run(weights0)
                run(messages0)
                run(leads1)
            run(merge0)
        run(norm_rows, "n0", False)
        with Stage(nc, "keep2") as s2:
            keep.XT, keep.comb = s2.sb("xt", [P, KC, NP]), s2.sb("comb", [P, NT, NX0])
            run(gates0)
            run(experts0)
        run(norm_rows, "n1", True)
        run(tables1)
        with Stage(nc, "keep3") as s3:
            keep.kv, keep.ksum = s3.sb("kv", [P, KC, P]), s3.sb("ksum", [P, KC, 2])
            run(mixer1)
            run(edges1)
            run(merge1)
        run(norm_rows, "n2", False)
        with Stage(nc, "keep4") as s4:
            keep.gate, keep.expert = s4.sb("gate", [P, 1]), s4.sb("expert", [P, 1], I32)
            run(route1)
            run(linear1)
        return keep


def layouts(a, np):
    f = np.float32
    pad = ET * P - E

    def bc(v):
        return np.broadcast_to(v, (P, v.shape[-1]))

    def cols(v):
        return v.reshape(-1, P).T

    def blocks(v):
        return v.reshape(EB, EU, P).transpose(0, 2, 1)

    src = np.pad(a["src"], (0, pad), mode="edge")
    dst = np.pad(a["dst"], (0, pad), mode="edge")
    dst_to = np.pad(a["dst"], (0, pad), constant_values=NP - 1)
    src_to = np.pad(a["src"], (0, pad), constant_values=NP - 1)
    qkv = a["L0_mix_qkv_w"].T
    order = np.concatenate([np.arange(P), (P + np.arange(D - P).reshape(P, 3).T).reshape(-1)])
    return {
        "x": np.pad(a["x"], ((0, NP - N), (0, 0))),
        "ident": np.eye(P, dtype=f),
        "valid": (np.arange(NP).reshape(NT, P).T < N).astype(f),
        "dst_rows": dst_to.reshape(P, ET),
        "dst_cols": dst_to.reshape(ET, P).T,
        "src_rows": src_to.reshape(P, ET),
        "src_cols": src_to.reshape(ET, P).T,
        "w_att": np.stack([a["L0_gnn_Wq"], a["L0_gnn_Wk"], a["L0_gnn_Wv"]]),
        "b_att": bc(np.concatenate([a["L0_gnn_bq"], a["L0_gnn_bk"], a["L0_gnn_bv"]])),
        "gamma": cols(a["L0_mix_ln_gamma"]),
        "beta": cols(a["L0_mix_ln_beta"]),
        "dst_ix": blocks(dst),
        "src_ix": blocks(src),
        "half": (np.arange(P)[:, None] // DH == np.arange(2)).astype(f),
        "lower": (np.arange(P)[:, None] > np.arange(P)).astype(f),
        "spare": (SPARE + np.arange(P, dtype=f))[:, None],
        "w_mix0": qkv,
        "bq_mix0": cols(a["L0_mix_qkv_b"][:D]),
        "bkv_mix0": bc(a["L0_mix_qkv_b"][D:]),
        "b_res": bc(a["L0_gnn_bff"]),
        "b_res2": bc(a["L0_mix_out_b"]),
        "w_ff": a["L0_gnn_Wff"],
        "w_out0": a["L0_mix_out_w"].T,
        "wg0": a["L0_ffn_Wg"],
        "bg0": a["L0_ffn_bg"][:, None],
        "lower8": bc((np.arange(NX0)[:, None] > np.arange(NX0)).astype(f).reshape(-1)),
        "w1": a["L0_ffn_W1"],
        "b1": a["L0_ffn_b1"].reshape(NX0, QF // P, P).transpose(0, 2, 1),
        "w2": a["L0_ffn_W2"],
        "b2": a["L0_ffn_b2"],
        "w_pre0": a["L1_gnn_W_pre0"],
        "w_pre1": a["L1_gnn_W_pre1"],
        "w_nd0": a["L1_gnn_W_nd0"],
        "w_nd1": a["L1_gnn_W_nd1"],
        "w_g1": a["L1_gnn_W_g1"],
        "w_g2": a["L1_gnn_W_g2"],
        "b_g": np.stack([cols(a["L1_gnn_b_g1"]), cols(a["L1_gnn_b_g2"])], 1),
        "b_pre0": a["L1_gnn_b_pre0"][:, None],
        "b_nd0": bc(a["L1_gnn_b_nd0"]),
        "w_s1": a["L1_gnn_W_s1"],
        "w_s2": a["L1_gnn_W_s2"],
        "w_f1": a["L1_gnn_W_f1"],
        "w_f2": a["L1_gnn_W_f2"],
        "attr": np.pad(a["edge_attr_32"], ((0, pad), (0, 0))).T,
        "sh": np.pad(a["edge_attr_4"], ((0, pad), (0, 0))).reshape(ET, P, 4).transpose(1, 0, 2).reshape(P, ET * 4),
        "w_o0": a["L1_gnn_W_o0"],
        "w_o1": a["L1_gnn_W_o1"],
        "b_o0": bc(np.pad(a["L1_gnn_b_o0"], (0, D - P))),
        "w_mix1": a["L1_mix_W_qkv"].T[order],
        "w_proj": a["L1_mix_W_proj"].T[:, order],
        "b_proj": bc(a["L1_mix_b_proj"]),
        "wg1": a["L1_ffn_Wg"],
        "bg1": bc(a["L1_ffn_bg"]),
        "order": bc(np.arange(NX1, dtype=f)),
        "we": a["L1_ffn_We"],
        "be": a["L1_ffn_be"],
    }


SCRATCH = {
    "xhT": [NT, P, D],
    "qT": [NT, P, D],
    "srow": [NP, SW],
    "drow": [NP, DW],
}


def tensors(nc, arrays):
    io = {name: nc.dram_tensor(f"in_{name}", v.shape, mybir.dt.from_np(v.dtype), kind="ExternalInput").ap()
          for name, v in arrays.items()}
    for name, shape in SCRATCH.items():
        io[name] = nc.dram_tensor(f"mid_{name}", shape, F32, kind="Internal").ap()
    for name, count, shape in (("att_rows", 3, [NP, D]), ("acc0", NACC, [ACCR, ACCW]), ("acc1", NACC, [ACCR, D])):
        io[name] = [nc.dram_tensor(f"mid_{name}{k}", shape, F32, kind="Internal").ap() for k in range(count)]
    for name in ("dst_l", "src_l"):
        io[name] = nc.dram_tensor(f"mid_{name}", [2, P, ET], BF16, kind="Internal").ap()
    for name in ("lead_ix0", "lead_ix1"):
        io[name] = nc.dram_tensor(f"mid_{name}", [P, ET], I32, kind="Internal").ap()
    io["out"] = nc.dram_tensor("out_0", [N, D], F32, kind="ExternalOutput").ap()
    return io


def kernel(**inputs):
    import numpy as np
    import concourse.bacc as bacc
    from concourse.bass_utils import run_bass_kernel_spmd

    given = {name: np.asarray(v) for name, v in inputs.items()}
    arrays = {name: np.ascontiguousarray(v) for name, v in layouts(given, np).items()}
    nc = bacc.Bacc("TRN2", target_bir_lowering=False, num_devices=1)
    program(nc, tensors(nc, arrays))
    r = run_bass_kernel_spmd(nc, [{f"in_{name}": v for name, v in arrays.items()}], core_ids=[0])
    return r.results[0]["out_0"]
```

```python
from contextlib import ExitStack

import concourse.bass as bass
from concourse import mybir

F32 = mybir.dt.float32
I32 = mybir.dt.int32
BF16 = mybir.dt.bfloat16
ALU = mybir.AluOpType
ACT = mybir.ActivationFunctionType
AX = mybir.AxisListType.X
RMAX = bass.bass_isa.ReduceOp.max

P = 128
N = 3125
D = 512
NT = -(-N // P)
NP = NT * P
E = 53125
EU = 16
ET = -(-E // (P * EU)) * EU
EB = ET // EU
EH = EU // 2
U = 5
NB = NT // U
H = 8
DH = D // H
KC = D // P
ACCW = D + H
SPARE = NP
ACCR = NP + P
NACC = 2
QF = 256
NX0 = 8
NX1 = 16
HID = 32
STATS = 7
LEAD_STEPS = 5
DW = 3 * P + HID
SW = 3 * P + D


def need(eng, sem, value):
    if isinstance(value, int) and value <= 0:
        return
    eng.wait_ge(sem, value)


def last_tile(n):
    return isinstance(n, int) and n == NT - 1


def last_pass(b):
    return isinstance(b, int) and b == EB - 1


def passes(eng, count, body):
    body(0)
    if count > 2:
        with eng.Fori(1, count - 1) as i:
            body(i)
    body(count - 1)


class Stage:

    def __init__(self, nc, name):
        self.nc, self.name, self.ctx, self.sems = nc, name, ExitStack(), []

    def __enter__(self):
        self.ctx.__enter__()
        return self

    def __exit__(self, *a):
        if self.sems:
            self.nc.clear_and_free_semaphores(self.sems)
            self.nc.all_engine_barrier()
        return self.ctx.__exit__(*a)

    def sb(self, name, shape, dt=F32):
        return self.ctx.enter_context(self.nc.sbuf_tensor(f"{self.name}_{name}", shape, dt))

    def ps(self, name, shape, dt=F32):
        return self.ctx.enter_context(self.nc.psum_tensor(f"{self.name}_{name}", shape, dt))

    def sem(self, name):
        self.sems.append(self.nc.alloc_semaphore(name=f"{self.name}_{name}"))
        return self.sems[-1]


class Steps:

    def __init__(self, eng, sem, per_pass):
        self.eng, self.sem, self.per_pass, self.base, self.k = eng, sem, per_pass, 0, 0

    def begin(self, i):
        self.base, self.k = i * self.per_pass, 0

    def did(self, ins):
        self.k += 1
        ins.then_inc(self.sem, 1)

    def wait(self):
        self.eng.wait_ge(self.sem, self.base + self.k)

    def end(self):
        assert self.k == self.per_pass, (self.k, self.per_pass)


def norm_factors(vec, s_step, at, keep, tmp, eps=1e-5):
    even, odd = keep.stats[:, :, 1], keep.stats[:, :, 4]
    vec.tensor_tensor(keep.mean[:], even, odd, ALU.add).then_inc(s_step, 1)
    vec.tensor_tensor(tmp[:, 0, :], even, odd, ALU.subtract).then_inc(s_step, 1)
    vec.tensor_tensor(tmp[:, 1, :], keep.stats[:, :, 2], keep.stats[:, :, 5], ALU.add).then_inc(s_step, 1)
    vec.wait_ge(s_step, at + 3)
    vec.tensor_scalar(keep.mean[:], keep.mean[:], 0.5, None, ALU.mult).then_inc(s_step, 1)
    vec.scalar_tensor_tensor(tmp[:, 0, :], tmp[:, 0, :], 0.25, tmp[:, 0, :], ALU.mult, ALU.mult).then_inc(s_step, 1)
    vec.tensor_scalar(tmp[:, 1, :], tmp[:, 1, :], 1.0 / D, eps, ALU.mult, ALU.add).then_inc(s_step, 1)
    vec.wait_ge(s_step, at + 6)
    vec.tensor_tensor(keep.rstd[:], tmp[:, 0, :], tmp[:, 1, :], ALU.add).then_inc(s_step, 1)
    return at + STATS


def lead_rows(vec, s_t, node, count, spare, go, ints):
    vec.tensor_scalar(go[:, 0, :], count[:], 1.0, None, ALU.min).then_inc(s_t, 1)
    vec.tensor_scalar(go[:, 1, :], node[:], -1.0, spare[:], ALU.mult, ALU.add).then_inc(s_t, 1)
    vec.wait_ge(s_t, 2)
    vec.tensor_tensor(go[:, 0, :], go[:, 0, :], go[:, 1, :], ALU.mult).then_inc(s_t, 1)
    vec.wait_ge(s_t, 3)
    vec.tensor_tensor(go[:, 0, :], go[:, 0, :], node[:], ALU.add).then_inc(s_t, 1)
    vec.wait_ge(s_t, 4)
    vec.tensor_copy(ints[:], go[:, 0, :]).then_inc(s_t, 1)


def clear_sums(act, s_z, zero, acc, width):
    for rows in acc:
        rows = rows.rearrange("(p r) w -> p (r w)", p=P)
        for r in range(0, ACCR // P, 2):
            act.dma_start(rows[:, r * width:(r + 2) * width], zero[:, 0:2 * width]).then_inc(s_z, 16)
    return 16 * NACC * (ACCR // P // 2)


def load_consts(nc, io, keep):
    with Stage(nc, "consts") as s:
        ints = s.sb("ints", [P, 4, ET], I32)
        digits, lines = s.sb("digits", [P, 2, 2, ET], I32), s.sb("lines", [P, 2, 2, ET], BF16)
        tmp = s.sb("tmp", [P, 2, NT])
        s_c, s_i, s_f, s_w, s_st, s_v, s_r = (s.sem(n) for n in (
            "consts", "ints", "floats", "row_out", "stats", "steps", "powers"))
        s_x = [s.sem(f"x{b}") for b in range(NB)]
        with nc.Block() as block:
            @block.sync
            def _(sp):
                sp.dma_start(keep.ident[:], io["ident"][:, :]).then_inc(s_c, 16)
                sp.dma_start(keep.valid[:], io["valid"][:, :]).then_inc(s_c, 16)
                for k, ends in enumerate((io["dst_rows"], io["src_rows"], io["dst_cols"], io["src_cols"])):
                    sp.dma_start(ints[:, k, :], ends[:, :]).then_inc(s_i, 16)
                xv = io["x"].rearrange("(t p) f -> p t f", p=P)
                for b in range(NB):
                    sp.dma_start(keep.X[:, U * b:U * (b + 1), :], xv[:, U * b:U * (b + 1), :]).then_inc(s_x[b], 16)
                sp.wait_ge(s_f, 3)
                sp.dma_start(io["dst_l"].rearrange("k p t -> p k t"), lines[:, 0]).then_inc(s_w, 16)
                sp.dma_start(io["src_l"].rearrange("k p t -> p k t"), lines[:, 1]).then_inc(s_w, 16)
                sp.wait_ge(s_c, 32)
                sp.wait_ge(s_w, 32)

            @block.vector
            def _(vec):
                vec.wait_ge(s_i, 64)
                vec.tensor_scalar(digits[:, :, 0, :], ints[:, 0:2, :], -P, None, ALU.bitwise_and).then_inc(s_f, 1)
                vec.tensor_scalar(digits[:, :, 1, :], ints[:, 0:2, :], P - 1, None, ALU.bitwise_and).then_inc(s_f, 1)
                vec.wait_ge(s_f, 2)
                vec.tensor_copy(lines[:], digits[:]).then_inc(s_f, 1)
                vec.tensor_copy(keep.dst[:], ints[:, 2, :])
                vec.tensor_copy(keep.src[:], ints[:, 3, :])
                for n in range(NT):
                    vec.wait_ge(s_x[n // U], 16)
                    ins = vec.bn_stats(keep.stats[:, n, :], keep.X[:, n, :])
                ins.then_inc(s_st, 1)
                vec.wait_ge(s_st, 1)
                at = norm_factors(vec, s_v, 0, keep, tmp)
                vec.wait_ge(s_v, at)
                vec.tensor_scalar(tmp[:, 1, :], keep.rstd[:], 1e-5, None, ALU.subtract).then_inc(s_v, 1)
                vec.wait_ge(s_r, 1)
                vec.reciprocal(keep.rstd[:], keep.rstd[:]).then_inc(s_v, 1)
                vec.wait_ge(s_v, at + 2)
                vec.tensor_tensor(tmp[:, 1, :], tmp[:, 1, :], keep.rstd[:], ALU.mult).then_inc(s_v, 1)
                vec.wait_ge(s_v, at + 3)
                vec.tensor_tensor(tmp[:, 1, :], tmp[:, 1, :], keep.rstd[:], ALU.mult).then_inc(s_v, 1)
                vec.wait_ge(s_v, at + 4)
                vec.tensor_scalar(keep.rstd2[:], tmp[:, 1, :], 1e-5, None, ALU.add).then_inc(s_v, 1)
                vec.wait_ge(s_r, 2)
                vec.reciprocal(keep.rstd2[:], keep.rstd2[:]).then_inc(s_v, 1)

            @block.scalar
            def _(act):
                act.wait_ge(s_v, STATS + 1)
                act.activation(keep.rstd[:], keep.rstd[:], ACT.Sqrt).then_inc(s_r, 1)
                act.wait_ge(s_v, STATS + 5)
                act.activation(keep.rstd2[:], keep.rstd2[:], ACT.Sqrt).then_inc(s_r, 1)


def tables0(nc, io, keep):
    with Stage(nc, "t0") as s:
        W = s.sb("w", [P, KC, 2 * D])
        bias = s.sb("bias", [P, 2, D])
        extra = s.sb("extra", [P, 2, D])
        gamma, beta = s.sb("gamma", [P, KC]), s.sb("beta", [P, KC])
        xn, xh = s.sb("xn", [P, U, D]), s.sb("xh", [P, U, D])
        xnT, xhT = s.sb("xnT", [P, U, D]), s.sb("xhT", [P, U, D])
        rows = s.sb("rows", [P, U, D])
        tpn, tph = s.ps("tpn", [P, D]), s.ps("tph", [P, D])
        acc = [s.ps(f"acc{k}", [P, D]) for k in range(5)]
        s_w, s_b = [s.sem(f"weights{w}") for w in range(2)], s.sem("biases")
        s_gb, s_extra, s_bias = s.sem("norm_biases"), s.sem("output_biases"), s.sem("bias_sum")
        zero = s.sb("zero", [P, 2 * ACCW])
        s_zero, s_z = s.sem("zero"), s.sem("sums_cleared")
        s_go = s.sem("go")
        s_xn, s_xh, s_res, s_tp, s_xT, s_xhT, s_mm, s_rows = (s.sem(n) for n in ("normed", "normed_twice", "residual", "transposed", "xT", "xhT", "products", "rows"))
        s_store = [s.sem(f"rows_out{k}") for k in range(U)]
        s_nstore = [s.sem(f"xnT_out{k}") for k in range(U)]
        s_hstore = [s.sem(f"xhT_out{k}") for k in range(U)]
        with nc.Block() as block:
            @block.sync
            def _(sp):
                sp.dma_start(gamma[:], io["gamma"][:, :]).then_inc(s_gb, 16)
                sp.dma_start(beta[:], io["beta"][:, :]).then_inc(s_gb, 16)
                for k in range(2):
                    sp.dma_start(W[:, :, D * k:D * (k + 1)], io["w_att"][k].rearrange("(c p) n -> p c n", p=P)).then_inc(s_w[k], 16)
                    if k == 0:
                        sp.dma_start(bias[:], io["b_att"][:, 0:2 * D].rearrange("p (k n) -> p k n", k=2)).then_inc(s_b, 16)
                sp.dma_start(extra[:, 0, :], io["b_res"][:, :]).then_inc(s_extra, 16)
                sp.dma_start(extra[:, 1, :], io["b_res2"][:, :]).then_inc(s_extra, 16)

                def body(i):
                    for j in range(U):
                        n = U * i + j
                        sp.wait_ge(s_xT, n + 1)
                        sp.dma_start(io["xnT"][n], xnT[:, j, :]).then_inc(s_nstore[j], 16)
                        sp.wait_ge(s_xhT, n + 1)
                        sp.dma_start(io["xhT"][n], xhT[:, j, :]).then_inc(s_hstore[j], 16)
                        for w in range(2):
                            m, k = 2 * n + w, (2 * j + w) % 5
                            sp.wait_ge(s_rows, m + 1)
                            sp.dma_start(io["att_rows"][w][bass.ds(n * P, P), :], rows[:, k, :]).then_inc(s_store[k], 16)
                passes(sp, NB, body)
                for k in range(U):
                    sp.wait_ge(s_store[k], 16 * 2 * NB)
                    sp.wait_ge(s_nstore[k], 16 * NB)
                    sp.wait_ge(s_hstore[k], 16 * NB)

            @block.vector
            def _(vec):
                def norms(n, j):
                    need(vec, s_tp, 2 * (n - U) + 2)
                    need(vec, s_res, n - U + 1)
                    vec.tensor_scalar(xn[:, j, :], keep.X[:, n, :], keep.mean[:, bass.ds(n, 1)],
                                      keep.rstd[:, bass.ds(n, 1)], ALU.subtract, ALU.mult).then_inc(s_xn, 1)
                    vec.wait_ge(s_xn, n + 1)
                    vec.tensor_scalar(xh[:, j, :], xn[:, j, :], keep.rstd2[:, bass.ds(n, 1)], None,
                                      ALU.mult).then_inc(s_xh, 1)

                norms(0, 0)
                norms(1, 1)
                vec.wait_ge(s_b, 16)

                def body(i):
                    for j in range(U):
                        n = U * i + j
                        if not (isinstance(n, int) and n + 2 >= NT):
                            norms(n + 2, (j + 2) % U)
                        for w in range(2):
                            m, k = 2 * (U * i + j) + w, (2 * j + w) % 5
                            vec.wait_ge(s_mm, m + 1)
                            need(vec, s_store[k], 16 * (2 * i + (2 * j + w) // 5))
                            vec.tensor_tensor(rows[:, k, :], acc[k][:], bias[:, w, :], ALU.add).then_inc(s_rows, 1)
                passes(vec, NB, body)

            @block.gpsimd
            def _(pool):
                pool.memset(zero[:], 0.0).then_inc(s_zero, 1)
                pool.wait_ge(s_extra, 32)
                pool.tensor_tensor(extra[:, 0, :], extra[:, 0, :], extra[:, 1, :], ALU.add).then_inc(s_bias, 1)
                pool.wait_ge(s_bias, 1)

                def body(i):
                    for j in range(U):
                        n = U * i + j
                        pool.wait_ge(s_xn, n + 1)
                        pool.tensor_tensor(keep.X[:, n, :], keep.X[:, n, :], xn[:, j, :], ALU.add).then_inc(s_res, 1)
                        pool.wait_ge(s_res, n + 1)
                        pool.sem_inc(s_go, 1)
                        pool.tensor_tensor(keep.X[:, n, :], keep.X[:, n, :], extra[:, 0, :], ALU.add)
                passes(pool, NB, body)

            @block.scalar
            def _(act):
                act.wait_ge(s_gb, 32)
                act.wait_ge(s_zero, 1)
                cleared = clear_sums(act, s_z, zero, io["acc0"], ACCW)

                def body(i):
                    for j in range(U):
                        n = U * i + j
                        act.wait_ge(s_tp, 2 * n + 1)
                        need(act, s_mm, 2 * (n - U) + 2)
                        need(act, s_nstore[j], 16 * i)
                        act.activation(xnT[:, j, :], tpn[:], ACT.Copy).then_inc(s_xT, 1)
                        act.wait_ge(s_tp, 2 * n + 2)
                        need(act, s_hstore[j], 16 * i)
                        for c in range(KC):
                            cols = slice(P * c, P * (c + 1))
                            ins = act.activation(xhT[:, j, cols], tph[:, cols], ACT.Identity,
                                                 bias=beta[:, c:c + 1], scale=gamma[:, c:c + 1])
                        ins.then_inc(s_xhT, 1)
                passes(act, NB, body)
                act.wait_ge(s_z, cleared)

            @block.tensor
            def _(pe):
                def transposes(n, j):
                    pe.wait_ge(s_xn, n + 1)
                    need(pe, s_xT, n)
                    for c in range(KC):
                        cols = slice(P * c, P * (c + 1))
                        ins = pe.transpose(tpn[:, cols], xn[:, j, cols], keep.ident[:])
                    ins.then_inc(s_tp, 1)
                    pe.wait_ge(s_xh, n + 1)
                    need(pe, s_xhT, n)
                    for c in range(KC):
                        cols = slice(P * c, P * (c + 1))
                        ins = pe.transpose(tph[:, cols], xh[:, j, cols], keep.ident[:])
                    ins.then_inc(s_tp, 1)

                transposes(0, 0)

                def body(i):
                    for j in range(U):
                        n = U * i + j
                        if not last_tile(n):
                            transposes(n + 1, (j + 1) % U)
                        pe.wait_ge(s_xT, n + 1)
                        for w in range(2):
                            m, k = 2 * n + w, (2 * j + w) % 5
                            need(pe, s_rows, m - 5 + 1)
                            if isinstance(n, int) and n == 0:
                                pe.wait_ge(s_w[w], 16)
                            for c in range(KC):
                                ins = pe.matmul(acc[k][:], xnT[:, j, P * c:P * (c + 1)], W[:, c, D * w:D * (w + 1)],
                                                start=c == 0, stop=c == KC - 1)
                            ins.then_inc(s_mm, 1)
                passes(pe, NB, body)


def scores0(nc, io, keep):
    with Stage(nc, "s0") as s:
        S = EH
        W = s.sb("w", [P, KC, 3 * D])
        bq, bkv = s.sb("bq", [P, KC]), s.sb("bkv", [P, 2, D])
        half, lower = s.sb("half", [P, 2]), s.sb("lower", [P, P])
        ones, zeros = s.sb("ones", [P, P]), s.sb("zeros", [P, D])
        ix = s.sb("ix", [P, 2, 2, EH], I32)
        qrow, krow = s.sb("qrow", [P, S, D]), s.sb("krow", [P, S, D])
        line, ones2 = s.sb("line", [2, 2, EH * P], BF16), s.sb("ones2", [2, P], BF16)
        junk = s.sb("junk", [P, P])
        xhT = s.sb("xhT", [P, D])
        w_v, b_v, xnT, rows = s.sb("w_v", [P, KC, D]), s.sb("b_v", [P, D]), s.sb("xnT", [P, D]), s.sb("rows", [P, D])
        y, e, el, v = s.sb("y", [P, 2, D]), s.sb("e", [P, 2, D]), s.sb("el", [P, 2, D]), s.sb("v", [P, D])
        pq, pk, pv, pkv, pks, prow = (s.ps(n, [P, D]) for n in ("pq", "pk", "pv", "pkv", "pks", "prow"))
        s_wv, s_xn, s_vm, s_row, s_rout = (s.sem(n) for n in (
            "value_weights", "xnT_in", "value_products", "value_rows", "value_rows_out"))
        pd = [s.ps(f"pd{k}", [P, D]) for k in range(2)]
        s_w, s_b, s_const = s.sem("weights"), s.sem("biases"), s.sem("constants")
        s_ix = [s.sem(f"indices{h}") for h in range(2)]
        s_line = [s.sem(f"line{h}") for h in range(2)]
        s_g = [s.sem(f"gathered{k}") for k in range(S)]
        s_prod, s_att, s_cnt, s_bc = s.sem("edge_products"), s.sem("scores"), s.sem("counts"), s.sem("destinations")
        s_x, s_mm, s_y, s_e, s_el, s_v, s_kv, s_q = (s.sem(n) for n in (
            "xhT_in", "products", "sums", "exps", "elu", "values", "kv", "q_out"))
        s_end = s.sem("blocks")
        s_go = s.sem("go")
        with nc.Block() as block:
            @block.sync
            def _(sp):
                lines = io["dst_l"].rearrange("k p t -> k (p t)")

                def node_tile(b):
                    need(sp, s_mm, 3 * b)
                    sp.dma_start(xhT[:], io["xhT"][b]).then_inc(s_x, 16)
                    need(sp, s_vm, b)
                    sp.dma_start(xnT[:], io["xnT"][b]).then_inc(s_xn, 16)

                def body(b):
                    first = isinstance(b, int) and b == 0
                    if not first and not last_pass(b):
                        node_tile(b)
                    for h in range(2):
                        need(sp, s_att, EU * (b - 1) + EH * (h + 1))
                        sp.dma_start(ix[:, h, 0, :], io["dst_ix"][b, :, EH * h:EH * (h + 1)]).then_inc(s_ix[h], 16)
                        sp.dma_start(ix[:, h, 1, :], io["src_ix"][b, :, EH * h:EH * (h + 1)]).then_inc(s_ix[h], 16)
                        need(sp, s_bc, 4 * (b - 1) + 2 * (h + 1))
                        sp.dma_start(line[:, h, :], lines[:, bass.ds((2 * b + h) * EH * P, EH * P)]).then_inc(s_line[h], 16)
                    if first:
                        node_tile(b)
                passes(sp, EB, body)

            @block.gpsimd
            def _(pool):
                def body(b):
                    for k in range(EU):
                        t = EU * b + k
                        if k % EH == 0:
                            pool.wait_ge(s_ix[k // EH], 32 * (b + 1))
                        need(pool, s_att, t - S + 1)
                        pool.sem_inc(s_go, 1)
                        for w, rows in ((0, qrow), (1, krow)):
                            pool.indirect_dma_start(
                                rows[:, k % S, :], None, io["att_rows"][w],
                                bass.IndirectOffsetOnAxis(ap=ix[:, k // EH, w, k % EH:k % EH + 1], axis=0),
                            ).then_inc(s_g[k % S], 16)
                passes(pool, EB, body)

            @block.vector
            def _(vec):
                vec.memset(ones[:], 1.0).then_inc(s_const, 1)
                vec.memset(ones2[:], 1.0).then_inc(s_const, 1)
                vec.memset(zeros[:], 0.0).then_inc(s_const, 1)
                vec.wait_ge(s_b, 64)

                def edge(b, k):
                    t = EU * b + k
                    vec.wait_ge(s_g[k % S], 32 * (2 * b + k // S + 1))
                    vec.tensor_tensor(qrow[:, k % S, :], qrow[:, k % S, :], krow[:, k % S, :], ALU.mult).then_inc(s_prod, 1)
                    if k % 4 == 0:
                        vec.wait_ge(s_bc, 4 * b + k // 4 + 1)
                    need(vec, s_cnt, t)
                    vec.scalar_tensor_tensor(junk[:], pd[k // 4 % 2][:, P * (k % 4):P * (k % 4 + 1)],
                                             keep.dst[:, bass.ds(t, 1)], lower[:], ALU.is_equal, ALU.mult,
                                             accum_out=keep.count[:, bass.ds(t, 1)]).then_inc(s_cnt, 1)
                    vec.wait_ge(s_prod, t + 1)
                    vec.tensor_reduce(keep.att[:, t, :], qrow[:, k % S, :].rearrange("p (h d) -> p h d", h=H),
                                      AX, ALU.add).then_inc(s_att, 1)

                def mix_sums(b):
                    vec.wait_ge(s_mm, 3 * b + 1)
                    need(vec, s_el, 2 * b - 1)
                    vec.tensor_tensor(y[:, 0, :].rearrange("p (c n) -> p c n", c=KC),
                                      pq[:].rearrange("p (c n) -> p c n", c=KC),
                                      bq[:].unsqueeze(2).broadcast_to([P, KC, P]), ALU.add).then_inc(s_y, 1)
                    vec.wait_ge(s_mm, 3 * b + 2)
                    vec.tensor_tensor(y[:, 1, :], pk[:], bkv[:, 0, :], ALU.add).then_inc(s_y, 1)

                def mix_values(b):
                    vec.wait_ge(s_mm, 3 * b + 3)
                    need(vec, s_kv, b)
                    vec.tensor_tensor(v[:], pv[:], bkv[:, 1, :], ALU.add).then_inc(s_v, 1)

                def value_rows(b):
                    vec.wait_ge(s_vm, b + 1)
                    if isinstance(b, int) and b == 0:
                        vec.wait_ge(s_wv, 32)
                    need(vec, s_rout, 16 * b)
                    vec.tensor_tensor(rows[:], prow[:], b_v[:], ALU.add).then_inc(s_row, 1)

                def mix_elu(b, last):
                    vec.wait_ge(s_e, 4 * b + 2)
                    need(vec, s_q, 16 * b)
                    vec.scalar_tensor_tensor(el[:, 0, :], y[:, 0, :], 0.0, e[:, 0, :], ALU.max, ALU.add).then_inc(s_el, 1)
                    vec.wait_ge(s_e, 4 * b + 4)
                    ins = vec.scalar_tensor_tensor(el[:, 1, :], y[:, 1, :], 0.0, e[:, 1, :], ALU.max, ALU.add)
                    if last:
                        ins.then_inc(s_end, 1)
                        vec.wait_ge(s_end, 1)
                        ins = vec.tensor_scalar(el[:, 1, :], el[:, 1, :], keep.valid[:, NT - 1:NT], None, ALU.mult)
                    ins.then_inc(s_el, 1)

                def body(b):
                    last = isinstance(b, int) and b == NT - 1
                    for k in range(EU):
                        if k == 8 and not last_pass(b):
                            mix_sums(b)
                        if k == 12 and not last_pass(b):
                            mix_values(b)
                            mix_elu(b, last)
                        if k == 15 and not last_pass(b):
                            value_rows(b)
                        edge(b, k)
                body(0)
                with vec.Fori(1, NT - 1) as b:
                    body(b)
                body(NT - 1)
                body(EB - 1)
                vec.wait_ge(s_kv, NT)
                for c in range(KC):
                    vec.tensor_tensor(keep.kv[:, c, :].rearrange("p (h d) -> p h d", h=2),
                                      pkv[:, P * c:P * (c + 1)].rearrange("p (h d) -> p h d", h=2),
                                      half[:].unsqueeze(2).broadcast_to([P, 2, DH]), ALU.mult)
                vec.tensor_tensor(keep.ksum[:], pks[:, 0:KC].unsqueeze(2).broadcast_to([P, KC, 2]),
                                  half[:].unsqueeze(1).broadcast_to([P, KC, 2]), ALU.mult).then_inc(s_end, 1)
                vec.wait_ge(s_end, 2)

            @block.scalar
            def _(act):
                act.dma_start(bq[:], io["bq_mix0"][:, :]).then_inc(s_b, 16)
                act.dma_start(bkv[:], io["bkv_mix0"].rearrange("p (k n) -> p k n", k=2)).then_inc(s_b, 16)
                act.dma_start(half[:], io["half"][:, :]).then_inc(s_b, 16)
                act.dma_start(lower[:], io["lower"][:, :]).then_inc(s_b, 16)
                for k in range(3):
                    act.dma_start(W[:, :, D * k:D * (k + 1)],
                                  io["w_mix0"][:, D * k:D * (k + 1)].rearrange("(c p) n -> p c n", p=P)).then_inc(s_w, 16)
                act.dma_start(w_v[:], io["w_att"][2].rearrange("(c p) n -> p c n", p=P)).then_inc(s_wv, 16)
                act.dma_start(b_v[:], io["b_att"][:, 2 * D:3 * D]).then_inc(s_wv, 16)

                def body(b):
                    for k in range(2):
                        act.wait_ge(s_y, 2 * b + k + 1)
                        need(act, s_el, 2 * (b - 1) + k + 1)
                        act.activation(e[:, k, :], y[:, k, :], ACT.Relu, scale=-1.0).then_inc(s_e, 1)
                        act.wait_ge(s_e, 4 * b + 2 * k + 1)
                        act.activation(e[:, k, :], e[:, k, :], ACT.Exp, scale=-1.0).then_inc(s_e, 1)
                    act.wait_ge(s_el, 2 * b + 1)
                    act.dma_start(io["qT"][b], el[:, 0, :]).then_inc(s_q, 16)
                    act.wait_ge(s_row, b + 1)
                    act.dma_start(io["att_rows"][2][bass.ds(b * P, P), :], rows[:]).then_inc(s_rout, 16)
                passes(act, NT, body)
                act.wait_ge(s_rout, 16 * NT)
                act.wait_ge(s_q, 16 * NT)

            @block.tensor
            def _(pe):
                pe.wait_ge(s_const, 3)
                pe.matmul(pkv[:], zeros[:, 0:P], zeros[:], start=True, stop=False, skip_group_check=True)
                pe.matmul(pks[:, 0:KC], zeros[:, 0:P], zeros[:, 0:KC], start=True, stop=False, skip_group_check=True)

                def spread(b, q):
                    pe.wait_ge(s_line[q // 2], 16 * (b + 1))
                    need(pe, s_cnt, EU * b + 4 * (q - 2) + 4)
                    pe.matmul(pd[q % 2][:], ones2[:], line[:, q // 2, D * (q % 2):D * (q % 2 + 1)],
                              start=True, stop=True).then_inc(s_bc, 1)

                def mix_qk(b):
                    if isinstance(b, int) and b == 0:
                        pe.wait_ge(s_w, 48)
                        pe.wait_ge(s_wv, 32)
                    pe.wait_ge(s_x, 16 * (b + 1))
                    need(pe, s_y, 2 * b - 1)
                    for f in range(KC):
                        for c in range(KC):
                            ins = pe.matmul(pq[:, P * f:P * (f + 1)], W[:, c, P * f:P * (f + 1)],
                                            xhT[:, P * c:P * (c + 1)], start=c == 0, stop=c == KC - 1)
                    ins.then_inc(s_mm, 1)
                    row_product(1, pk, s_y, 2 * b)

                def row_product(w, acc, s_read, count):
                    need(pe, s_read, count)
                    for c in range(KC):
                        ins = pe.matmul(acc[:], xhT[:, P * c:P * (c + 1)], W[:, c, D * w:D * (w + 1)],
                                        start=c == 0, stop=c == KC - 1)
                    ins.then_inc(s_mm, 1)

                def values(b):
                    pe.wait_ge(s_xn, 16 * (b + 1))
                    need(pe, s_row, b)
                    for c in range(KC):
                        ins = pe.matmul(prow[:], xnT[:, P * c:P * (c + 1)], w_v[:, c, :], start=c == 0, stop=c == KC - 1)
                    ins.then_inc(s_vm, 1)

                def sums(b, last):
                    pe.wait_ge(s_v, b + 1)
                    pe.wait_ge(s_el, 2 * b + 2)
                    for c in range(KC):
                        cols = slice(P * c, P * (c + 1))
                        pe.matmul(pkv[:, cols], el[:, 1, cols], v[:, cols], start=False, stop=last and c == KC - 1,
                                  skip_group_check=True)
                        ins = pe.matmul(pks[:, c:c + 1], el[:, 1, cols], ones[:, 0:1], start=False,
                                        stop=last and c == KC - 1, skip_group_check=True)
                    ins.then_inc(s_kv, 1)

                def body(b):
                    spread(b, 0)
                    spread(b, 1)
                    if not (isinstance(b, int) and b == 0):
                        sums(b - 1, last_pass(b))
                    if not last_pass(b):
                        mix_qk(b)
                    spread(b, 2)
                    if not last_pass(b):
                        row_product(2, pv, s_v, b)
                        values(b)
                    spread(b, 3)
                body(0)
                with pe.Fori(1, NT - 1) as b:
                    body(b)
                body(NT - 1)
                body(EB - 1)


def weights0(nc, io, keep):
    with Stage(nc, "w0") as s:
        m = s.sb("m", [P, 3])
        spare = s.sb("spare", [P, 1])
        go = s.sb("go", [P, 2, ET])
        ints = s.sb("ints", [P, ET], I32)
        s_in, s_m, s_all, s_b, s_exp, s_t, s_out = (s.sem(n) for n in ("spare", "max", "max_all", "shift", "exps", "steps", "out"))
        with nc.Block() as block:
            @block.sync
            def _(sp):
                sp.dma_start(spare[:], io["spare"][:, :]).then_inc(s_in, 16)
                sp.wait_ge(s_t, LEAD_STEPS)
                sp.dma_start(io["lead_ix0"][:, :], ints[:]).then_inc(s_out, 16)
                sp.wait_ge(s_out, 16)

            @block.gpsimd
            def _(pool):
                pool.wait_ge(s_m, 1)
                pool.partition_all_reduce(m[:, 1:2], m[:, 0:1], P, RMAX).then_inc(s_all, 1)

            @block.scalar
            def _(act):
                act.wait_ge(s_b, 1)
                flat = keep.att[:].rearrange("p t h -> p (t h)")
                act.activation(flat, flat, ACT.Exp, bias=m[:, 2:3], scale=DH ** -0.5).then_inc(s_exp, 1)

            @block.vector
            def _(vec):
                vec.reduce_max(m[:, 0:1], keep.att[:].rearrange("p t h -> p (t h)"), AX).then_inc(s_m, 1)
                vec.wait_ge(s_in, 16)
                lead_rows(vec, s_t, keep.dst, keep.count, spare, go, ints)
                vec.wait_ge(s_all, 1)
                vec.tensor_scalar(m[:, 2:3], m[:, 1:2], -DH ** -0.5, 3.0, ALU.mult, ALU.add).then_inc(s_b, 1)


def messages0(nc, io, keep):
    with Stage(nc, "m0") as s:
        S, LEAD, LAG, R = EH, 4, 3, 4
        ones = s.sb("ones", [2, P], BF16)
        ix, il = s.sb("ix", [P, 2, EH], I32), s.sb("il", [P, 2, EH], I32)
        vrow = s.sb("vrow", [P, S, D])
        line, sline = s.sb("line", [2, 2, EH * P], BF16), s.sb("sline", [2, 2, EH * P], BF16)
        lower, junk = s.sb("lower", [P, P]), s.sb("junk", [P, P])
        same = s.sb("same", [P, R, P])
        out = s.sb("out", [P, R, ACCW])
        w_out, q, o, oT, zo = (s.sb(n, shape) for n, shape in (
            ("w_out", [P, KC, D]), ("q", [P, D]), ("o", [P, D]), ("oT", [P, D]), ("zo", [P, H])))
        pd, psrc = s.ps("pd", [P, D]), s.ps("psrc", [P, D])
        pm = [s.ps(f"pm{k}", [P, D]) for k in range(2)]
        pw, po, pn, pout = s.ps("pw", [P, D]), s.ps("po", [P, D]), s.ps("pn", [P, D]), s.ps("pout", [P, D])
        s_wo, s_qin, s_po, s_z, s_o, s_to, s_oT, s_out, s_x = (s.sem(n) for n in (
            "mixer_weights", "queries_in", "attended", "normalizers", "mixed", "mixedT", "oT", "mixer_output", "x"))
        s_const, s_low, s_cnt, s_bs = s.sem("constants"), s.sem("lower"), s.sem("counts"), s.sem("sources")
        s_go = s.sem("go")
        s_ix = [s.sem(f"gather_ix{h}") for h in range(2)]
        s_il = [s.sem(f"lead_ix{h}") for h in range(2)]
        s_line = [s.sem(f"line{h}") for h in range(2)]
        s_g = [s.sem(f"gathered{k}") for k in range(S)]
        s_add = [s.sem(f"added{k}") for k in range(R)]
        s_msg, s_same, s_bc, s_mm, s_row = (s.sem(n) for n in ("messages", "same", "destinations", "products", "rows"))
        with nc.Block() as block:
            @block.sync
            def _(sp):
                lines = io["dst_l"].rearrange("k p t -> k (p t)")
                slines = io["src_l"].rearrange("k p t -> k (p t)")
                sp.dma_start(lower[:], io["lower"][:, :]).then_inc(s_low, 16)

                def body(b):
                    if not last_pass(b):
                        need(sp, s_po, b)
                        sp.dma_start(q[:], io["qT"][b]).then_inc(s_qin, 16)
                    for h in range(2):
                        need(sp, s_msg, EU * (b - 1) + EH * (h + 1))
                        sp.dma_start(ix[:, h, :], io["src_ix"][b, :, EH * h:EH * (h + 1)]).then_inc(s_ix[h], 16)
                        need(sp, s_bs, 4 * (b - 1) + 2 * (h + 1))
                        cols = bass.ds((2 * b + h) * EH * P, EH * P)
                        sp.dma_start(line[:, h, :], lines[:, cols]).then_inc(s_line[h], 16)
                        sp.dma_start(sline[:, h, :], slines[:, cols]).then_inc(s_line[h], 16)
                        for r in range(R):
                            need(sp, s_add[r], 16 * ((EU * (b - 1) + EH * (h + 1)) // R) if isinstance(b, int)
                                 else 16 * (EU // R * (b - 1) + EH // R * (h + 1)))
                        sp.dma_start(il[:, h, :], io["lead_ix0"][:, bass.ds(EU * b + EH * h, EH)]).then_inc(s_il[h], 16)
                passes(sp, EB, body)

            @block.gpsimd
            def _(pool):
                def gather(b, k):
                    b, k = b + k // EU, k % EU
                    t = EU * b + k
                    if k % EH == 0:
                        pool.wait_ge(s_ix[k // EH], 16 * (b + 1))
                    need(pool, s_mm, t - S + 1)
                    pool.sem_inc(s_go, 1)
                    pool.indirect_dma_start(
                        vrow[:, k % S, :], None, io["att_rows"][2],
                        bass.IndirectOffsetOnAxis(ap=ix[:, k // EH, k % EH:k % EH + 1], axis=0),
                    ).then_inc(s_g[k % S], 16)

                def scatter(b, k):
                    if k % EH == 0:
                        pool.wait_ge(s_il[k // EH], 16 * (b + 1))
                    pool.wait_ge(s_row, EU * b + k + 1)
                    prev = k - NACC
                    need(pool, s_add[prev % R], 16 * (EU // R * b + prev // R + 1))
                    pool.sem_inc(s_go, 1)
                    pool.indirect_dma_start(
                        io["acc0"][k % NACC], bass.IndirectOffsetOnAxis(ap=il[:, k // EH, k % EH:k % EH + 1], axis=0),
                        out[:, k % R, :], None, compute_op=ALU.add,
                    ).then_inc(s_add[k % R], 16)

                def body(b):
                    for k in range(EU):
                        if not (last_pass(b) and k + LEAD >= EU):
                            gather(b, k + LEAD)
                        if k >= LAG:
                            scatter(b, k - LAG)
                        elif not (isinstance(b, int) and b == 0):
                            scatter(b - 1, EU + k - LAG)
                for k in range(LEAD):
                    gather(0, k)
                passes(pool, EB, body)
                for k in range(EU - LAG, EU):
                    scatter(EB - 1, k)
                for r in range(R):
                    pool.wait_ge(s_add[r], 16 * (ET // R))

            @block.vector
            def _(vec):
                vec.memset(ones[:], 1.0).then_inc(s_const, 1)
                vec.wait_ge(s_low, 16)

                def norm_mixed(b):
                    vec.wait_ge(s_po, b + 1)
                    vec.tensor_scalar(zo[:], pn[:, 0:H], 1e-8, None, ALU.add).then_inc(s_z, 1)
                    vec.wait_ge(s_z, 2 * b + 1)
                    vec.reciprocal(zo[:], zo[:]).then_inc(s_z, 1)
                    vec.wait_ge(s_z, 2 * b + 2)
                    need(vec, s_to, b)
                    vec.tensor_tensor(by_head(o[:]), by_head(po[:]), over_head(zo[:]), ALU.mult).then_inc(s_o, 1)

                def add_mixed(b):
                    vec.wait_ge(s_out, b + 1)
                    vec.tensor_tensor(keep.X[:, b, :], keep.X[:, b, :], pout[:], ALU.add).then_inc(s_x, 1)

                def body(b):
                    for k in range(EU):
                        t = EU * b + k
                        if k == 4 and not last_pass(b):
                            norm_mixed(b)
                        if k == 15 and not last_pass(b):
                            add_mixed(b)
                        if k % 4 == 0:
                            vec.wait_ge(s_bc, 4 * b + k // 4 + 1)
                        need(vec, s_mm, t - R + 1)
                        vec.tensor_scalar(same[:, k % R, :], pd[:, P * (k % 4):P * (k % 4 + 1)],
                                          keep.dst[:, bass.ds(t, 1)], None, ALU.is_equal).then_inc(s_same, 1)
                        if k % 4 == 0:
                            vec.wait_ge(s_bs, 4 * b + k // 4 + 1)
                        need(vec, s_cnt, t)
                        vec.scalar_tensor_tensor(junk[:], psrc[:, P * (k % 4):P * (k % 4 + 1)],
                                                 keep.src[:, bass.ds(t, 1)], lower[:], ALU.is_equal, ALU.mult,
                                                 accum_out=keep.count[:, bass.ds(t, 1)]).then_inc(s_cnt, 1)
                        vec.wait_ge(s_g[k % S], 16 * (2 * b + k // S + 1))
                        rows = vrow[:, k % S, :].rearrange("p (h d) -> p h d", h=H)
                        vec.tensor_tensor(rows, rows, keep.att[:, t, :].unsqueeze(2).broadcast_to([P, H, DH]),
                                          ALU.mult).then_inc(s_msg, 1)
                passes(vec, EB, body)

            @block.tensor
            def _(pe):
                pe.wait_ge(s_const, 1)

                def spread(b, q):
                    pe.wait_ge(s_line[q // 2], 32 * (b + 1))
                    need(pe, s_same, EU * b + 4 * q)
                    pe.matmul(pd[:], ones[:], line[:, q // 2, D * (q % 2):D * (q % 2 + 1)],
                              start=True, stop=True).then_inc(s_bc, 1)
                    need(pe, s_cnt, EU * b + 4 * q)
                    pe.matmul(psrc[:], ones[:], sline[:, q // 2, D * (q % 2):D * (q % 2 + 1)],
                              start=True, stop=True).then_inc(s_bs, 1)

                spread(0, 0)

                def body(b):
                    for k in range(EU):
                        t = EU * b + k
                        if k == 2 and not last_pass(b):
                            pe.wait_ge(s_qin, 16 * (b + 1))
                            if isinstance(b, int) and b == 0:
                                pe.wait_ge(s_wo, 16)
                            need(pe, s_oT, b)
                            attend(pe, q, keep.kv, keep.ksum, po, pn).then_inc(s_po, 1)
                        if k == 6 and not last_pass(b):
                            pe.wait_ge(s_o, b + 1)
                            for c in range(KC):
                                ins = pe.transpose(po[:, P * c:P * (c + 1)], o[:, P * c:P * (c + 1)], keep.ident[:])
                            ins.then_inc(s_to, 1)
                        if k in range(10, 10 + KC) and not last_pass(b):
                            c = k - 10
                            if c == 0:
                                pe.wait_ge(s_oT, b + 1)
                                need(pe, s_x, b)
                            ins = pe.matmul(pout[:], oT[:, P * c:P * (c + 1)], w_out[:, c, :], start=c == 0, stop=c == KC - 1)
                            if c == KC - 1:
                                ins.then_inc(s_out, 1)
                        pe.wait_ge(s_msg, t + 1)
                        need(pe, s_row, t - 1)
                        pe.matmul(pm[k % 2][:], same[:, k % R, :], vrow[:, k % S, :], start=True, stop=True)
                        need(pe, s_row, t)
                        pe.matmul(pw[:, 0:H], same[:, k % R, :], keep.att[:, t, :], start=True, stop=True).then_inc(s_mm, 1)
                        if k % 4 == 3 and not (last_pass(b) and k + 1 == EU):
                            spread(b + (k + 1) // EU, (k // 4 + 1) % 4)
                passes(pe, EB, body)

            @block.scalar
            def _(act):
                act.dma_start(w_out[:], io["w_out0"].rearrange("(c p) n -> p c n", p=P)).then_inc(s_wo, 16)

                def body(b):
                    for k in range(EU):
                        t = EU * b + k
                        act.wait_ge(s_mm, t + 1)
                        need(act, s_add[k % R], 16 * (EU // R * b + k // R))
                        act.activation(out[:, k % R, 0:D], pm[k % 2][:], ACT.Copy)
                        act.activation(out[:, k % R, D:ACCW], pw[:, 0:H], ACT.Copy).then_inc(s_row, 1)
                        if k == 8 and not last_pass(b):
                            act.wait_ge(s_to, b + 1)
                            need(act, s_out, b)
                            act.activation(oT[:], po[:], ACT.Copy).then_inc(s_oT, 1)
                passes(act, EB, body)


def leads1(nc, io, keep):
    with Stage(nc, "w1") as s:
        spare = s.sb("spare", [P, 1])
        go = s.sb("go", [P, 2, ET])
        ints = s.sb("ints", [P, ET], I32)
        s_in, s_t, s_out = s.sem("spare"), s.sem("steps"), s.sem("out")
        with nc.Block() as block:
            @block.sync
            def _(sp):
                sp.dma_start(spare[:], io["spare"][:, :]).then_inc(s_in, 16)
                sp.wait_ge(s_t, LEAD_STEPS)
                sp.dma_start(io["lead_ix1"][:, :], ints[:]).then_inc(s_out, 16)
                sp.wait_ge(s_out, 16)

            @block.vector
            def _(vec):
                vec.wait_ge(s_in, 16)
                lead_rows(vec, s_t, keep.src, keep.count, spare, go, ints)


def attend(pe, q, kv, ksum, po, pn):
    for c in range(KC):
        cols = slice(P * c, P * (c + 1))
        pe.matmul(po[:, cols], q[:, cols], kv[:, c, :], start=True, stop=True)
    for c in range(KC):
        ins = pe.matmul(pn[:, 2 * c:2 * c + 2], q[:, P * c:P * (c + 1)], ksum[:, c, :], start=True, stop=True)
    return ins


def by_head(x):
    return x.rearrange("p (h d) -> p h d", h=H)


def over_head(x):
    return x.unsqueeze(2).broadcast_to([P, H, DH])


def merge0(nc, io, keep):
    with Stage(nc, "g0") as s:
        W = s.sb("w", [P, KC, D])
        a0, a1 = s.sb("a0", [P, U, ACCW]), s.sb("a1", [P, U, ACCW])
        aT, z = s.sb("aT", [P, U, D]), s.sb("z", [P, 2, H])
        tp, pout = ([s.ps(f"{n}{k}", [P, D]) for k in range(2)] for n in ("tp", "pout"))
        s_w = s.sem("weights")
        s_in = [s.sem(f"in{j}") for j in range(U)]
        s_st, s_agg, s_ta, s_aT, s_mm, s_x = (s.sem(n) for n in (
            "steps", "edges", "edgesT", "aT", "products", "x"))
        with nc.Block() as block:
            @block.sync
            def _(sp):
                def body(i):
                    for j in range(U):
                        n = U * i + j
                        need(sp, s_ta, n - U + 1)
                        rows = bass.ds(n * P, P)
                        sp.dma_start(a0[:, j, :], io["acc0"][0][rows, :]).then_inc(s_in[j], 16)
                        sp.dma_start(a1[:, j, :], io["acc0"][1][rows, :]).then_inc(s_in[j], 16)
                passes(sp, NB, body)

            @block.vector
            def _(vec):
                st = Steps(vec, s_st, 3)

                def norm_edges(i, j):
                    n = U * i + j
                    st.begin(n)
                    vec.wait_ge(s_in[j], 32 * (i + 1))
                    st.did(vec.tensor_tensor(a0[:, j, :], a0[:, j, :], a1[:, j, :], ALU.add))
                    st.wait()
                    den = a0[:, j, D:ACCW]
                    st.did(vec.scalar_tensor_tensor(z[:, 0, :], den, 0.0, den, ALU.is_equal, ALU.add))
                    st.wait()
                    st.did(vec.reciprocal(z[:, 1, :], z[:, 0, :]))
                    st.wait()
                    vec.tensor_tensor(by_head(a0[:, j, 0:D]), by_head(a0[:, j, 0:D]), over_head(z[:, 1, :]),
                                      ALU.mult).then_inc(s_agg, 1)

                def add(i, j):
                    n = U * i + j
                    vec.wait_ge(s_mm, n + 1)
                    vec.tensor_tensor(keep.X[:, n, :], keep.X[:, n, :], pout[j % 2][:], ALU.add).then_inc(s_x, 1)
                    vec.wait_ge(s_x, n + 1)
                    vec.bn_stats(keep.stats[:, n, :], keep.X[:, n, :])

                norm_edges(0, 0)
                norm_edges(0, 1)

                def body(i):
                    for j in range(U):
                        n = U * i + j
                        if not (isinstance(n, int) and n + 2 >= NT):
                            norm_edges(i + (j + 2) // U, (j + 2) % U)
                        add(i, j)
                passes(vec, NB, body)

            @block.scalar
            def _(act):
                act.dma_start(W[:], io["w_ff"].rearrange("(c p) n -> p c n", p=P)).then_inc(s_w, 16)

                def body(i):
                    for j in range(U):
                        n = U * i + j
                        act.wait_ge(s_ta, n + 1)
                        need(act, s_mm, n - U + 1)
                        act.activation(aT[:, j, :], tp[j % 2][:], ACT.Copy).then_inc(s_aT, 1)
                passes(act, NB, body)

            @block.tensor
            def _(pe):
                def edges(i, j):
                    n = U * i + j
                    pe.wait_ge(s_agg, n + 1)
                    need(pe, s_aT, n if j == 0 else n - 1)
                    for c in range(KC):
                        cols = slice(P * c, P * (c + 1))
                        ins = pe.transpose(tp[j % 2][:, cols], a0[:, j, cols], keep.ident[:])
                    ins.then_inc(s_ta, 1)

                edges(0, 0)
                pe.wait_ge(s_w, 16)

                def body(i):
                    for j in range(U):
                        n = U * i + j
                        if not last_tile(n):
                            edges(i + (j + 1) // U, (j + 1) % U)
                        pe.wait_ge(s_aT, n + 1)
                        need(pe, s_x, n if j == 0 else n - 1)
                        for c in range(KC):
                            ins = pe.matmul(pout[j % 2][:], aT[:, j, P * c:P * (c + 1)], W[:, c, :], start=c == 0, stop=c == KC - 1)
                        ins.then_inc(s_mm, 1)
                passes(pe, NB, body)


def norm_rows(nc, io, keep, name):
    with Stage(nc, name) as s:
        tmp = s.sb("tmp", [P, 2, NT])
        s_v, s_r = s.sem("steps"), s.sem("roots")
        with nc.Block() as block:
            @block.vector
            def _(vec):
                at = norm_factors(vec, s_v, 0, keep, tmp)
                vec.wait_ge(s_r, 1)
                vec.reciprocal(keep.rstd[:], keep.rstd[:]).then_inc(s_v, 1)
                vec.wait_ge(s_v, at + 1)

            @block.scalar
            def _(act):
                act.wait_ge(s_v, STATS)
                act.activation(keep.rstd[:], keep.rstd[:], ACT.Sqrt).then_inc(s_r, 1)


def gates0(nc, io, keep):
    with Stage(nc, "r0") as s:
        xn = s.sb("xn", [P, U, D])
        wg, bg, lower8 = s.sb("wg", [P, KC, NX0]), s.sb("bg", [NX0, 1]), s.sb("lower8", [P, NX0 * NX0])
        lgT = s.sb("lgT", [NX0, NP])
        g = s.sb("g", [P, NT, NX0])
        m = s.sb("m", [P, NT])
        rank, eq = s.sb("rank", [P, NT, NX0 * NX0]), s.sb("eq", [P, NT, NX0 * NX0])
        tp = [s.ps(f"tp{k}", [P, D]) for k in range(5)]
        pl = s.ps("pl", [NX0, D])
        pg = s.ps("pg", [P, NT * NX0])
        GW = 640 // 2
        s_w, s_xn, s_tp, s_xT, s_l, s_lT, s_g, s_e, s_v = (s.sem(n) for n in (
            "weights", "normed", "transposed", "xT", "logits", "logitsT", "turned", "exps", "steps"))
        s_go = s.sem("go")
        with nc.Block() as block:
            @block.sync
            def _(sp):
                sp.dma_start(wg[:], io["wg0"].rearrange("(c p) n -> p c n", p=P)).then_inc(s_w, 16)
                sp.dma_start(bg[:], io["bg0"][:, :]).then_inc(s_w, 16)
                sp.dma_start(lower8[:], io["lower8"][:, :]).then_inc(s_w, 16)
                sp.wait_ge(s_w, 48)

            @block.vector
            def _(vec):
                def body(i):
                    for j in range(U):
                        n = U * i + j
                        need(vec, s_tp, n - U + 1)
                        vec.tensor_scalar(xn[:, j, :], keep.X[:, n, :], keep.mean[:, bass.ds(n, 1)],
                                          keep.rstd[:, bass.ds(n, 1)], ALU.subtract, ALU.mult).then_inc(s_xn, 1)
                passes(vec, NB, body)
                st = Steps(vec, s_v, 0)
                st.begin(0)

                def over(x):
                    return x.unsqueeze(2).broadcast_to([P, NT, NX0])
                vec.wait_ge(s_w, 48)
                vec.wait_ge(s_g, 1)
                logits = pg[:].rearrange("p (t e) -> p t e", e=NX0)
                st.did(vec.tensor_reduce(m[:], logits, AX, ALU.max))
                st.wait()
                st.did(vec.tensor_tensor(g[:], logits, over(m[:]), ALU.subtract))
                vec.wait_ge(s_e, 1)
                st.did(vec.tensor_reduce(m[:], g[:], AX, ALU.add))
                st.wait()
                st.did(vec.reciprocal(m[:], m[:]))
                st.wait()
                st.did(vec.tensor_tensor(g[:], g[:], over(m[:]), ALU.mult))
                st.wait()
                wide = [P, NT, NX0, NX0]
                r4, e4 = (x[:].rearrange("p t (a b) -> p t a b", b=NX0) for x in (rank, eq))
                mine, other = g[:].unsqueeze(3).broadcast_to(wide), g[:].unsqueeze(2).broadcast_to(wide)
                st.did(vec.tensor_tensor(r4, other, mine, ALU.is_gt))
                st.did(vec.tensor_tensor(e4, other, mine, ALU.is_equal))
                st.wait()
                st.did(vec.tensor_tensor(eq[:], eq[:], lower8[:].unsqueeze(1).broadcast_to([P, NT, NX0 * NX0]), ALU.mult))
                st.wait()
                st.did(vec.tensor_tensor(rank[:], rank[:], eq[:], ALU.add))
                st.wait()
                st.did(vec.tensor_reduce(keep.comb[:], r4, AX, ALU.add))
                st.wait()
                flat = (x[:].rearrange("p t e -> p (t e)") for x in (keep.comb, keep.comb, g))
                st.did(vec.scalar_tensor_tensor(next(flat), next(flat), 2.0, next(flat), ALU.is_lt, ALU.mult))
                st.wait()

            @block.scalar
            def _(act):
                act.wait_ge(s_w, 48)

                def body(i):
                    for j in range(U):
                        n = U * i + j
                        act.wait_ge(s_tp, n + 1)
                        act.sem_inc(s_go, 1)
                        act.activation(keep.XT[:, :, bass.ds(n * P, P)], tp[j][:].rearrange("p (c n) -> p c n", c=KC),
                                       ACT.Copy).then_inc(s_xT, 1)
                    for h in range(2):
                        q = 2 * i + h
                        act.wait_ge(s_l, q + 1)
                        act.sem_inc(s_go, 1)
                        act.activation(lgT[:, bass.ds(q * GW, GW)], pl[:, 0:GW], ACT.Identity, bias=bg[:]).then_inc(s_lT, 1)
                passes(act, NB, body)
                act.wait_ge(s_v, 2)
                act.activation(g[:], g[:], ACT.Exp).then_inc(s_e, 1)

            @block.tensor
            def _(pe):
                pe.wait_ge(s_w, 48)

                def body(i):
                    for j in range(U):
                        n = U * i + j
                        pe.wait_ge(s_xn, n + 1)
                        need(pe, s_xT, n - U + 1)
                        for c in range(KC):
                            cols = slice(P * c, P * (c + 1))
                            ins = pe.transpose(tp[j][:, cols], xn[:, j, cols], keep.ident[:])
                        ins.then_inc(s_tp, 1)
                    pe.wait_ge(s_xT, U * (i + 1))
                    for h in range(2):
                        q = 2 * i + h
                        need(pe, s_lT, q)
                        for c in range(KC):
                            ins = pe.matmul(pl[:, 0:GW], wg[:, c, :], keep.XT[:, c, bass.ds(q * GW, GW)],
                                            start=c == 0, stop=c == KC - 1)
                        ins.then_inc(s_l, 1)
                passes(pe, NB, body)
                pe.wait_ge(s_lT, 2 * NB)
                for n in range(NT):
                    ins = pe.transpose(pg[:, NX0 * n:NX0 * (n + 1)], lgT[:, P * n:P * (n + 1)], keep.ident[0:NX0, 0:NX0])
                ins.then_inc(s_g, 1)


def experts0(nc, io, keep):
    with Stage(nc, "e0") as s:
        FC = QF // P
        GN = U * P
        HW = GN // 2
        w1, w2 = s.sb("w1", [P, 2, KC, QF]), s.sb("w2", [P, 2, FC, D])
        b1, b2 = s.sb("b1", [P, 2, FC]), s.sb("b2", [P, 2, D])
        hT = s.sb("hT", [P, 2, FC, GN])
        ph = [s.ps(f"ph{k}", [P, D]) for k in range(2 * FC)]
        py = [s.ps(f"py{k}", [P, D]) for k in range(2)]
        s_w = [s.sem(f"weights{k}") for k in range(2)]
        s_h, s_hT, s_y, s_x, s_pre = (s.sem(n) for n in ("hidden", "gelus", "products", "x", "biased"))
        zero = s.sb("zero", [P, 2 * D])
        s_zero, s_z = s.sem("zero"), s.sem("sums_cleared")
        PAIRS, STEPS = NX0 // 2, 2 * NB

        def loop(eng, body):
            body(0)
            with eng.Fori(1, PAIRS) as i:
                body(i)

        with nc.Block() as block:
            @block.sync
            def _(sp):
                def body(i):
                    for r in range(2):
                        e = 2 * i + r
                        need(sp, s_x, (e - 2 + 1) * NT)
                        sp.dma_start(w1[:, r], io["w1"][e].rearrange("(c p) n -> p c n", p=P)).then_inc(s_w[r], 16)
                        sp.dma_start(w2[:, r], io["w2"][e].rearrange("(c p) n -> p c n", p=P)).then_inc(s_w[r], 16)
                        sp.dma_start(b1[:, r], io["b1"][e]).then_inc(s_w[r], 16)
                        sp.dma_start(b2[:, r], io["b2"][e].partition_broadcast(P)).then_inc(s_w[r], 16)
                loop(sp, body)

            @block.gpsimd
            def _(pool):
                pool.memset(zero[:], 0.0).then_inc(s_zero, 1)

            @block.scalar
            def _(act):
                act.wait_ge(s_zero, 1)
                cleared = clear_sums(act, s_z, zero, io["acc1"], D)
                def body(i):
                    for r in range(2):
                        act.wait_ge(s_w[r], 64 * (i + 1))
                        for g in range(NB):
                            q = STEPS * i + NB * r + g
                            par = (NB * r + g) % 2
                            need(act, s_y, U * (q - 1))
                            for k in range(2 * FC):
                                f, h = k // 2, k % 2
                                act.wait_ge(s_h, 2 * FC * q + k + 1)
                                act.activation(hT[:, par, f, HW * h:HW * (h + 1)], ph[k][:, 0:HW], ACT.Gelu_apprx_tanh,
                                               bias=b1[:, r, f:f + 1]).then_inc(s_hT, 1)
                loop(act, body)
                act.wait_ge(s_z, cleared)

            @block.vector
            def _(vec):
                def body(i):
                    for r in range(2):
                        vec.wait_ge(s_w[r], 64 * (i + 1))
                        for g in range(NB):
                            for t in range(U):
                                k = (NB * r + g) * U + t
                                y = STEPS * U * i + k
                                n = U * g + t
                                need(vec, s_x, y - NT + 1)
                                gate = keep.comb[:, n, bass.ds(2 * i + r, 1)]
                                vec.scalar_tensor_tensor(keep.X[:, n, :], b2[:, r, :], gate, keep.X[:, n, :],
                                                         ALU.mult, ALU.add).then_inc(s_pre, 1)
                                vec.wait_ge(s_y, y + 1)
                                vec.wait_ge(s_pre, y + 1)
                                vec.scalar_tensor_tensor(keep.X[:, n, :], py[k % 2][:], gate, keep.X[:, n, :],
                                                         ALU.mult, ALU.add).then_inc(s_x, 1)
                                if isinstance(i, int) and i == PAIRS - 1 and r == 1:
                                    vec.wait_ge(s_x, y + 1)
                                    vec.bn_stats(keep.stats[:, n, :], keep.X[:, n, :])
                passes(vec, PAIRS, body)

            @block.tensor
            def _(pe):
                def hidden(i, r, g):
                    q = STEPS * i + NB * r + g
                    if g == 0:
                        pe.wait_ge(s_w[r], 64 * (i + 1))
                    for k in range(2 * FC):
                        f, h = k // 2, k % 2
                        need(pe, s_hT, 2 * FC * (q - 1) + k + 1)
                        for c in range(KC):
                            ins = pe.matmul(ph[k][:, 0:HW], w1[:, r, c, P * f:P * (f + 1)],
                                            keep.XT[:, c, GN * g + HW * h:GN * g + HW * (h + 1)], start=c == 0, stop=c == KC - 1)
                        ins.then_inc(s_h, 1)

                def output(i, r, g):
                    last = 2 * NB * i + NB * r + g - 1
                    k0 = (NB * r + g - 1) % STEPS
                    pr = k0 // NB
                    pe.wait_ge(s_hT, 2 * FC * (last + 1))
                    for t in range(U):
                        k = k0 * U + t
                        need(pe, s_x, U * last + t - 2 + 1)
                        for f in range(FC):
                            ins = pe.matmul(py[k % 2][:], hT[:, k0 % 2, f, P * t:P * (t + 1)], w2[:, pr, f, :],
                                            start=f == 0, stop=f == FC - 1)
                        ins.then_inc(s_y, 1)

                def body(i):
                    for r in range(2):
                        for g in range(NB):
                            hidden(i, r, g)
                            if not (isinstance(i, int) and i == 0 and r == 0 and g == 0):
                                output(i, r, g)
                loop(pe, body)
                output(PAIRS, 0, 0)


def tables1(nc, io, keep):
    with Stage(nc, "t1") as s:
        GN, HW = U * P, U * P // 2
        w_pre0, w_pre1, w_nd0, w_nd1 = (s.sb(n, [P, P]) for n in ("w_pre0", "w_pre1", "w_nd0", "w_nd1"))
        w_g1, w_g2 = s.sb("w_g1", [P, 2, 2 * P]), s.sb("w_g2", [P, 2, 2 * P])
        b_g, b_pre0, b_nd0 = s.sb("b_g", [P, 2, 2]), s.sb("b_pre0", [P, 1]), s.sb("b_nd0", [P, P])
        w_s = s.sb("w_s", [P, 2, HID])
        xn = s.sb("xn", [P, U, D])
        xT = s.sb("xT", [P, KC, GN])
        sq, gated = s.sb("sq", [P, 3, GN]), s.sb("gated", [P, 3, GN])
        n1, p0 = s.sb("n1", [P, GN]), s.sb("p0", [P, GN])
        g1, g2 = s.sb("g1", [P, 2, GN]), s.sb("g2", [P, 2, GN])
        srow, drow = s.sb("srow", [P, U, SW]), s.sb("drow", [P, U, DW])
        tp = [s.ps(f"tp{k}", [P, D]) for k in range(2)]
        pr = [s.ps(f"pr{k}", [P, D]) for k in range(2)]
        pg = [s.ps(f"pg{k}", [P, D]) for k in range(4)]
        s_w, s_wab = s.sem("weights"), s.sem("folded")
        s_xn, s_res, s_tp, s_xT, s_p0, s_p0T, s_pr, s_drow, s_prow = (s.sem(n) for n in (
            "normed", "residual", "transposed", "xT", "scalars", "scalarsT", "projections", "destination_rows", "source_rows"))
        s_sq, s_n1, s_g1, s_g1T, s_g2, s_g2T, s_x1, s_nd, s_row = (s.sem(n) for n in (
            "squares", "norms", "hidden", "hiddenT", "gates", "gatesT", "gated", "node_rows", "rows"))
        s_xout, s_rout = s.sem("xT_out"), s.sem("rows_out")
        LOADS = 11
        with nc.Block() as block:
            @block.sync
            def _(sp):
                sp.dma_start(w_s[:, 0], io["w_s1"][0:P, :]).then_inc(s_w, 16)
                sp.dma_start(w_s[:, 1], io["w_s1"][P:2 * P, :]).then_inc(s_w, 16)
                for dst, src in ((w_pre0, io["w_pre0"][:, :]), (w_pre1, io["w_pre1"][:, :]), (b_pre0, io["b_pre0"][:, :]),
                                 (w_g1, io["w_g1"].rearrange("(c p) n -> p c n", p=P))):
                    sp.dma_start(dst[:], src).then_inc(s_w, 16)
                by_s = io["srow"].rearrange("(t p) w -> p t w", p=P)
                by_d = io["drow"].rearrange("(t p) w -> p t w", p=P)

                def body(i):
                    for j in range(U):
                        sp.wait_ge(s_xT, U * i + j + 1)
                        sp.dma_start(io["xhT"][U * i + j].rearrange("p (c n) -> p c n", c=KC), xT[:, :, P * j:P * (j + 1)]).then_inc(s_xout, 16)
                    sp.wait_ge(s_drow, U * (i + 1))
                    sp.dma_start(by_d[:, bass.ds(U * i, U), :], drow[:]).then_inc(s_rout, 16)
                    sp.wait_ge(s_prow, U * (i + 1))
                    sp.wait_ge(s_row, U * (i + 1))
                    sp.dma_start(by_s[:, bass.ds(U * i, U), :], srow[:]).then_inc(s_rout, 16)
                passes(sp, NB, body)
                sp.wait_ge(s_xout, 16 * NT)
                sp.wait_ge(s_rout, 32 * NB)

            @block.gpsimd
            def _(pool):
                def body(i):
                    for j in range(U):
                        n = U * i + j
                        pool.wait_ge(s_xn, n + 1)
                        pool.tensor_tensor(keep.X[:, n, :], keep.X[:, n, :], xn[:, j, :], ALU.add).then_inc(s_res, 1)
                passes(pool, NB, body)

            @block.vector
            def _(vec):
                def body(i):
                    for j in range(U):
                        n = U * i + j
                        need(vec, s_tp, n - U + 1)
                        need(vec, s_res, n - U + 1)
                        vec.tensor_scalar(xn[:, j, :], keep.X[:, n, :], keep.mean[:, bass.ds(n, 1)],
                                          keep.rstd[:, bass.ds(n, 1)], ALU.subtract, ALU.mult).then_inc(s_xn, 1)
                    if isinstance(i, int) and i == 0:
                        vec.wait_ge(s_w, 16 * LOADS)
                        vec.tensor_tensor(w_s[:, 0, :], w_s[:, 0, :], w_s[:, 1, :], ALU.add).then_inc(s_wab, 1)
                    vec.wait_ge(s_xT, U * (i + 1))
                    vec.tensor_tensor(sq[:], xT[:, 1:4, :], xT[:, 1:4, :], ALU.mult).then_inc(s_sq, 1)
                    vec.wait_ge(s_sq, 3 * i + 1)
                    vec.tensor_tensor(sq[:, 0, :], sq[:, 0, :], sq[:, 1, :], ALU.add).then_inc(s_sq, 1)
                    vec.wait_ge(s_sq, 3 * i + 2)
                    vec.tensor_tensor(sq[:, 0, :], sq[:, 0, :], sq[:, 2, :], ALU.add).then_inc(s_sq, 1)
                    need(vec, s_rout, 32 * i)
                    for j in range(U):
                        vec.wait_ge(s_drow, U * i + j + 1)
                        vec.tensor_copy(srow[:, j, 0:3 * P], drow[:, j, 0:3 * P]).then_inc(s_prow, 1)
                    vec.wait_ge(s_g2T, 4 * (i + 1))
                    need(vec, s_nd, U * i)
                    vec.tensor_tensor(gated[:], xT[:, 1:4, :], g2[:, 1, :].unsqueeze(1).broadcast_to([P, 3, GN]),
                                      ALU.mult).then_inc(s_x1, 1)
                    for j in range(U):
                        vec.wait_ge(s_nd, U * i + j + 1)
                        vec.tensor_tensor(srow[:, j, 3 * P:4 * P], pr[j % 2][:, 0:P], b_nd0[:], ALU.add)
                        vec.tensor_copy(srow[:, j, 4 * P:SW], pr[j % 2][:, P:D]).then_inc(s_row, 1)
                passes(vec, NB, body)

            @block.scalar
            def _(act):
                for dst, src in ((b_g[:], io["b_g"][:, :, :]), (b_nd0[:], io["b_nd0"][:, :]),
                                 (w_g2[:], io["w_g2"].rearrange("(c p) n -> p c n", p=P)),
                                 (w_nd0[:], io["w_nd0"][:, :]), (w_nd1[:], io["w_nd1"][:, :])):
                    act.dma_start(dst, src).then_inc(s_w, 16)
                act.wait_ge(s_w, 16 * LOADS)

                def body(i):
                    need(act, s_xout, 16 * U * i)
                    need(act, s_x1, i)
                    for j in range(U):
                        n = U * i + j
                        act.wait_ge(s_tp, n + 1)
                        act.activation(xT[:, :, P * j:P * (j + 1)], tp[j % 2][:].rearrange("p (c n) -> p c n", c=KC),
                                       ACT.Copy).then_inc(s_xT, 1)
                    for h in range(2):
                        act.wait_ge(s_p0, 2 * i + h + 1)
                        act.activation(p0[:, HW * h:HW * (h + 1)], pg[h][:, 0:HW], ACT.Identity, bias=b_pre0[:]).then_inc(s_p0T, 1)
                    act.wait_ge(s_sq, 3 * i + 3)
                    act.activation(n1[:], sq[:, 0, :], ACT.Sqrt, scale=1.0 / 3.0).then_inc(s_n1, 1)
                    need(act, s_rout, 32 * i)
                    for j in range(U):
                        act.wait_ge(s_pr, U * i + j + 1)
                        act.activation(drow[:, j, :], pr[j % 2][:, 0:DW], ACT.Copy).then_inc(s_drow, 1)
                    for k in range(4):
                        f, h = k // 2, k % 2
                        act.wait_ge(s_g1, 4 * i + k + 1)
                        act.activation(g1[:, f, HW * h:HW * (h + 1)], pg[k][:, 0:HW], ACT.Silu,
                                       bias=b_g[:, 0, f:f + 1]).then_inc(s_g1T, 1)
                    for k in range(4):
                        f, h = k // 2, k % 2
                        act.wait_ge(s_g2, 4 * i + k + 1)
                        act.activation(g2[:, f, HW * h:HW * (h + 1)], pg[k][:, 0:HW], ACT.Identity,
                                       bias=b_g[:, 1, f:f + 1]).then_inc(s_g2T, 1)
                passes(act, NB, body)

            @block.tensor
            def _(pe):
                def body(i):
                    for j in range(U):
                        n = U * i + j
                        pe.wait_ge(s_xn, n + 1)
                        need(pe, s_xT, n if j == 0 else n - 1)
                        for c in range(KC):
                            x = xn[:, j, 0:P] if c == 0 else xn[:, j, P:D].rearrange("p (u c) -> p c u", c=3)[:, c - 1, :]
                            ins = pe.transpose(tp[j % 2][:, P * c:P * (c + 1)], x, keep.ident[:])
                        ins.then_inc(s_tp, 1)
                    pe.wait_ge(s_xT, U * (i + 1))
                    if isinstance(i, int) and i == 0:
                        pe.wait_ge(s_wab, 1)
                    need(pe, s_g2T, 4 * i)
                    for h in range(2):
                        pe.matmul(pg[h][:, 0:HW], w_pre0[:], xT[:, 0, HW * h:HW * (h + 1)], start=True, stop=True).then_inc(s_p0, 1)
                    need(pe, s_row, U * i)
                    pe.wait_ge(s_p0T, 2 * (i + 1))
                    for j in range(U):
                        n = U * i + j
                        if j >= 2:
                            pe.wait_ge(s_drow, n - 1)
                        cols = slice(P * j, P * (j + 1))
                        for c in range(3):
                            pe.matmul(pr[j % 2][:, P * c:P * (c + 1)], xT[:, 1 + c, cols], w_pre1[:], start=True, stop=True)
                        pe.matmul(pr[j % 2][:, 3 * P:DW], p0[:, cols], w_s[:, 0, :], start=True, stop=True).then_inc(s_pr, 1)
                    pe.wait_ge(s_n1, i + 1)
                    for k in range(4):
                        f, h = k // 2, k % 2
                        half = slice(HW * h, HW * (h + 1))
                        pe.matmul(pg[k][:, 0:HW], w_g1[:, 0, P * f:P * (f + 1)], xT[:, 0, half], start=True, stop=False)
                        pe.matmul(pg[k][:, 0:HW], w_g1[:, 1, P * f:P * (f + 1)], n1[:, half], start=False, stop=True).then_inc(s_g1, 1)
                    for k in range(4):
                        f, h = k // 2, k % 2
                        half = slice(HW * h, HW * (h + 1))
                        if k == 0:
                            pe.wait_ge(s_g1T, 4 * (i + 1))
                        pe.matmul(pg[k][:, 0:HW], w_g2[:, 0, P * f:P * (f + 1)], g1[:, 0, half], start=True, stop=False)
                        pe.matmul(pg[k][:, 0:HW], w_g2[:, 1, P * f:P * (f + 1)], g1[:, 1, half], start=False, stop=True).then_inc(s_g2, 1)
                    pe.wait_ge(s_x1, i + 1)
                    pe.wait_ge(s_drow, U * (i + 1))
                    for j in range(U):
                        n = U * i + j
                        if j >= 2:
                            pe.wait_ge(s_row, n - 1)
                        cols = slice(P * j, P * (j + 1))
                        pe.matmul(pr[j % 2][:, 0:P], g2[:, 0, cols], w_nd0[:], start=True, stop=True)
                        for c in range(3):
                            ins = pe.matmul(pr[j % 2][:, P * (c + 1):P * (c + 2)], gated[:, c, cols], w_nd1[:], start=True, stop=True)
                        ins.then_inc(s_nd, 1)
                passes(pe, NB, body)


def mixer1(nc, io, keep):
    with Stage(nc, "x1") as s:
        BANKS = 5
        W = s.sb("w", [P, KC, 3 * D])
        half = s.sb("half", [P, 2])
        ones, zeros = s.sb("ones", [P, 1]), s.sb("zeros", [P, D])
        extra = s.sb("extra", [P, 2, D])
        xT, q, k_, v = (s.sb(n, [P, U, D]) for n in ("xT", "q", "k", "v"))
        acc = [s.ps(f"acc{k}", [P, D]) for k in range(BANKS)]
        pkv, pks = s.ps("pkv", [P, D]), s.ps("pks", [P, D])
        s_w, s_half, s_const = [s.sem(f"weights{w}") for w in range(3)], s.sem("half"), s.sem("constants")
        s_extra, s_bias = s.sem("output_biases"), s.sem("bias_sum")
        s_x = [s.sem(f"xT_in{j}") for j in range(U)]
        s_qo = [s.sem(f"q_out{j}") for j in range(U)]
        s_mm, s_q, s_k, s_v, s_kv, s_end = (s.sem(n) for n in ("products", "queries", "keys", "values", "kv", "blocks"))
        with nc.Block() as block:
            @block.sync
            def _(sp):
                sp.dma_start(half[:], io["half"][:, :]).then_inc(s_half, 16)

                def body(i):
                    for j in range(U):
                        n = U * i + j
                        need(sp, s_mm, 3 * (n - U + 1))
                        sp.dma_start(xT[:, j, :], io["xhT"][n]).then_inc(s_x[j], 16)
                passes(sp, NB, body)

            @block.gpsimd
            def _(pool):
                pool.dma_start(extra[:, 0], io["b_proj"][:, :]).then_inc(s_extra, 16)
                pool.dma_start(extra[:, 1], io["b_o0"][:, :]).then_inc(s_extra, 16)
                pool.wait_ge(s_extra, 32)
                pool.tensor_tensor(extra[:, 0, :], extra[:, 0, :], extra[:, 1, :], ALU.add).then_inc(s_bias, 1)
                pool.wait_ge(s_bias, 1)
                with pool.Fori(0, NT) as n:
                    pool.tensor_tensor(keep.X[:, n, :], keep.X[:, n, :], extra[:, 0, :], ALU.add)

            @block.vector
            def _(vec):
                vec.memset(ones[:], 1.0).then_inc(s_const, 1)
                vec.memset(zeros[:], 0.0).then_inc(s_const, 1)

                def body(i):
                    for j in range(U):
                        n = U * i + j
                        last = last_tile(n)
                        vec.wait_ge(s_mm, 3 * n + 1)
                        need(vec, s_qo[j], 16 * i)
                        vec.tensor_scalar(q[:, j, :], acc[3 * j % BANKS][:], 0.0, DH ** -0.5, ALU.max, ALU.add).then_inc(s_q, 1)
                        vec.wait_ge(s_mm, 3 * n + 2)
                        need(vec, s_kv, n - U + 1)
                        ins = vec.tensor_scalar(k_[:, j, :], acc[(3 * j + 1) % BANKS][:], 0.0, DH ** -0.5, ALU.max, ALU.add)
                        if last:
                            ins.then_inc(s_end, 1)
                            vec.wait_ge(s_end, 1)
                            ins = vec.tensor_scalar(k_[:, j, :], k_[:, j, :], keep.valid[:, NT - 1:NT], None, ALU.mult)
                        ins.then_inc(s_k, 1)
                passes(vec, NB, body)
                vec.wait_ge(s_half, 16)
                vec.wait_ge(s_kv, NT)
                for c in range(KC):
                    vec.tensor_tensor(keep.kv[:, c, :].rearrange("p (h d) -> p h d", h=2),
                                      pkv[:, P * c:P * (c + 1)].rearrange("p (h d) -> p h d", h=2),
                                      half[:].unsqueeze(2).broadcast_to([P, 2, DH]), ALU.mult)
                vec.tensor_tensor(keep.ksum[:], pks[:, 0:KC].unsqueeze(2).broadcast_to([P, KC, 2]),
                                  half[:].unsqueeze(1).broadcast_to([P, KC, 2]), ALU.mult).then_inc(s_end, 1)
                vec.wait_ge(s_end, 2)

            @block.scalar
            def _(act):
                for k in range(3):
                    act.dma_start(W[:, :, D * k:D * (k + 1)],
                                  io["w_mix1"][:, D * k:D * (k + 1)].rearrange("(c p) n -> p c n", p=P)).then_inc(s_w[k], 16)
                def body(i):
                    for j in range(U):
                        n = U * i + j
                        act.wait_ge(s_mm, 3 * n + 3)
                        need(act, s_kv, n - U + 1)
                        act.activation(v[:, j, :], acc[(3 * j + 2) % BANKS][:], ACT.Copy).then_inc(s_v, 1)
                        act.wait_ge(s_q, n + 1)
                        act.dma_start(io["qT"][n], q[:, j, :]).then_inc(s_qo[j], 16)
                passes(act, NB, body)
                for j in range(U):
                    act.wait_ge(s_qo[j], 16 * NB)

            @block.tensor
            def _(pe):
                pe.wait_ge(s_const, 2)
                pe.matmul(pkv[:], zeros[:, 0:P], zeros[:], start=True, stop=False, skip_group_check=True)
                pe.matmul(pks[:, 0:KC], zeros[:, 0:P], zeros[:, 0:KC], start=True, stop=False, skip_group_check=True)

                def products(i, j):
                    n = U * i + j
                    pe.wait_ge(s_x[j], 16 * (i + 1))
                    for w in range(3):
                        b = (3 * j + w) % BANKS
                        sem = (s_q, s_k, s_v)[(w - BANKS) % 3]
                        need(pe, sem, n - 1 if w < 2 else n)
                        if isinstance(n, int) and n == 0:
                            pe.wait_ge(s_w[w], 16)
                        for f in range(KC):
                            for c in range(KC) if w == 0 or f == 0 else ():
                                if w == 0:
                                    ins = pe.matmul(acc[b][:, P * f:P * (f + 1)], W[:, c, P * f:P * (f + 1)],
                                                    xT[:, j, P * c:P * (c + 1)], start=c == 0, stop=c == KC - 1)
                                else:
                                    ins = pe.matmul(acc[b][:], xT[:, j, P * c:P * (c + 1)], W[:, c, D * w:D * (w + 1)],
                                                    start=c == 0, stop=c == KC - 1)
                        ins.then_inc(s_mm, 1)

                def sums(i, j, n):
                    pe.wait_ge(s_v, n + 1)
                    pe.wait_ge(s_k, n + 1)
                    last = last_tile(n)
                    for c in range(KC):
                        cols = slice(P * c, P * (c + 1))
                        pe.matmul(pkv[:, cols], k_[:, j, cols], v[:, j, cols], start=False, stop=last and c == KC - 1,
                                  skip_group_check=True)
                        ins = pe.matmul(pks[:, c:c + 1], k_[:, j, cols], ones[:], start=False,
                                        stop=last and c == KC - 1, skip_group_check=True)
                    ins.then_inc(s_kv, 1)

                def body(i):
                    for j in range(U):
                        n = U * i + j
                        products(i, j)
                        if not (isinstance(n, int) and n == 0):
                            sums(i, (j - 1) % U, n - 1)
                passes(pe, NB, body)
                sums(NB - 1, U - 1, NT - 1)


def edges1(nc, io, keep):
    with Stage(nc, "m1") as s:
        S, R, B = EU, 4, 4
        SD = EH
        GATHER, PAIR = 10, 8
        BW = B * P
        w_c, w_f1, w_2 = s.sb("w_c", [P, HID]), s.sb("w_f1", [HID, HID]), s.sb("w_2", [2 * HID, D])
        sh = s.sb("sh", [P, ET, 4])
        ones = s.sb("ones", [2, P], BF16)
        ig, il = s.sb("ig", [P, 2, 2, EH], I32), s.sb("il", [P, 2, EH], I32)
        attr = s.sb("attr", [HID, 2, EH * P])
        line = s.sb("line", [2, 2, EH * P], BF16)
        srow, drow = s.sb("srow", [P, S, SW]), s.sb("drow", [P, SD, DW])
        ipT = s.sb("ipT", [P, BW])
        soft, hid = s.sb("soft", [2 * HID, BW]), s.sb("hid", [2 * HID, 2, BW])
        w = s.sb("w", [P, 2, D])
        xs, xd = s.sb("xs", [P, 2, D]), s.sb("xd", [P, 2, 3 * P])
        dot, x0w = s.sb("dot", [P, 2, P]), s.sb("x0w", [P, 2, P])
        msg, same, out = s.sb("msg", [P, 2, D]), s.sb("same", [P, 2, B, P]), s.sb("out", [P, R, D])
        pip, ph, pm, pd = s.ps("pip", [P, D]), s.ps("ph", [2 * HID, D]), s.ps("pm", [P, D]), s.ps("pd", [P, D])
        pws, pwf = ([s.ps(f"{n}{k}", [P, D]) for k in range(2)] for n in ("pws", "pwf"))
        s_w, s_pre, s_const = s.sem("weights"), s.sem("prepared"), s.sem("constants")
        s_ig, s_il, s_line, s_attr = ([s.sem(f"{n}{h}") for h in range(2)] for n in ("gather_ix", "lead_ix", "line", "attributes"))
        s_g = [s.sem(f"gathered{k}") for k in range(S)]
        s_add = [s.sem(f"added{k}") for k in range(R)]
        s_go = s.sem("go")
        s_prod, s_ip, s_ipT, s_h, s_soft, s_hid, s_wm, s_wf, s_w2, s_xs, s_st, s_bc, s_same, s_msg, s_seg, s_row = (s.sem(n) for n in (
            "pair_products", "inner", "innerT", "hidden_sums", "soft_steps", "hidden", "weight_products", "factors", "edge_weights", "scaled",
            "steps", "destinations", "same", "messages", "sums", "rows"))
        s_go2, s_go_line = s.sem("go_scalar"), s.sem("go_line")
        DV = 6

        def at(b, k):
            if isinstance(b, int) and not 0 <= EU * b + k < ET:
                return None
            return b + k // EU, k % EU

        with nc.Block() as block:
            @block.sync
            def _(sp):
                lines = io["src_l"].rearrange("k p t -> k (p t)")

                def body(b):
                    for h in range(2):
                        cols = bass.ds((2 * b + h) * EH * P, EH * P)
                        need(sp, s_prod, EU * (b - 1) + EH * (h + 1))
                        sp.dma_start(ig[:, h, 0, :], io["src_ix"][b, :, EH * h:EH * (h + 1)]).then_inc(s_ig[h], 16)
                        sp.dma_start(ig[:, h, 1, :], io["dst_ix"][b, :, EH * h:EH * (h + 1)]).then_inc(s_ig[h], 16)
                        need(sp, s_h, 4 * (b - 1) + 2 * (h + 1))
                        sp.dma_start(attr[:, h, :], io["attr"][:, cols]).then_inc(s_attr[h], 16)
                        need(sp, s_bc, 4 * (b - 1) + 2 * (h + 1))
                        sp.sem_inc(s_go_line, 1)
                        sp.dma_start(line[:, h, :], lines[:, cols]).then_inc(s_line[h], 16)
                        for r in range(R):
                            need(sp, s_add[r], 16 * (EU // R * (b - 1) + EH // R * (h + 1)))
                        sp.dma_start(il[:, h, :], io["lead_ix1"][:, bass.ds(EU * b + EH * h, EH)]).then_inc(s_il[h], 16)
                passes(sp, EB, body)

            @block.gpsimd
            def _(pool):
                def gather(b, k):
                    t = EU * b + k
                    if k % EH == 0:
                        pool.wait_ge(s_ig[k // EH], 32 * (b + 1))
                    need(pool, s_msg, t - S + 1)
                    need(pool, s_h, 4 * b + k // 4 - 1)
                    pool.sem_inc(s_go, 1)
                    for n, row, table in ((0, drow[:, k % SD, :], io["drow"]), (1, srow[:, k % S, :], io["srow"])):
                        pool.indirect_dma_start(
                            row, None, table,
                            bass.IndirectOffsetOnAxis(ap=ig[:, k // EH, n, k % EH:k % EH + 1], axis=0),
                        ).then_inc(s_g[k % S], 16)

                def scatter(b, k):
                    t = EU * b + k
                    if k % EH == 0:
                        pool.wait_ge(s_il[k // EH], 16 * (b + 1))
                    pool.wait_ge(s_row, t + 1)
                    prev = k - NACC
                    need(pool, s_add[prev % R], 16 * (EU // R * b + prev // R + 1))
                    pool.sem_inc(s_go, 1)
                    pool.indirect_dma_start(
                        io["acc1"][k % NACC], bass.IndirectOffsetOnAxis(ap=il[:, k // EH, k % EH:k % EH + 1], axis=0),
                        out[:, k % R, :], None, compute_op=ALU.add,
                    ).then_inc(s_add[k % R], 16)

                def body(b):
                    for k in range(EU):
                        if there := at(b, k + GATHER):
                            gather(*there)
                        if there := at(b, k - 3):
                            scatter(*there)
                for k in range(GATHER):
                    gather(0, k)
                passes(pool, EB, body)
                scatter(EB - 1, EU - 3)
                scatter(EB - 1, EU - 2)
                scatter(EB - 1, EU - 1)
                for r in range(R):
                    pool.wait_ge(s_add[r], 16 * (ET // R))

            @block.vector
            def _(vec):
                vec.memset(ones[:], 1.0).then_inc(s_const, 1)
                vec.wait_ge(s_w, 80)
                vec.tensor_scalar(w_c[:], w_c[:], 1.0 / 3.0, None, ALU.mult).then_inc(s_pre, 1)
                w_dot = w_2[HID:2 * HID, 3 * P:D]
                vec.tensor_scalar(w_dot, w_dot, 3.0 ** -0.5, None, ALU.mult).then_inc(s_pre, 1)
                vec.wait_ge(s_pre, 2)
                st = Steps(vec, s_st, DV)

                def pair(b, k):
                    vec.wait_ge(s_g[k], 32 * (b + 1))
                    vectors = drow[:, k % SD, 0:3 * P]
                    vec.tensor_tensor(vectors, vectors, srow[:, k % S, 0:3 * P], ALU.mult).then_inc(s_prod, 1)

                def hidden(b, k):
                    q = 4 * b + k // B
                    vec.wait_ge(s_soft, 3 * (q + 1))
                    need(vec, s_wm, B * (q - 1))
                    vec.scalar_tensor_tensor(hid[:, k // B % 2, :], ph[:], 0.0, soft[:], ALU.max, ALU.add).then_inc(s_hid, 1)

                def equals(b, k):
                    q = 4 * b + k // B
                    vec.wait_ge(s_bc, q + 1)
                    need(vec, s_seg, B * (q - 1))
                    vec.tensor_tensor(same[:, k // B % 2], pd[:].rearrange("p (a n) -> p a n", a=B),
                                      keep.src[:, bass.ds(B * q, B)].unsqueeze(2).broadcast_to([P, B, P]),
                                      ALU.is_equal).then_inc(s_same, 1)

                def message(b, k):
                    t, par = EU * b + k, k % 2
                    st.begin(t)
                    ws, msgs = w[:, par, :], msg[:, par, :]
                    x0 = srow[:, k % S, 3 * P:4 * P]

                    def three(x):
                        return x.rearrange("p (c u) -> p c u", c=3)
                    vec.wait_ge(s_xs, t + 1)
                    st.did(vec.tensor_tensor(dot[:, par, :], xd[:, par, 0:P], xd[:, par, P:2 * P], ALU.add))
                    vec.wait_ge(s_wf, t + 1)
                    vec.tensor_tensor(ws, pws[par][:], ws, ALU.mult).then_inc(s_w2, 1)
                    st.wait()
                    st.did(vec.tensor_tensor(dot[:, par, :], dot[:, par, :], xd[:, par, 2 * P:3 * P], ALU.add))
                    vec.wait_ge(s_w2, t + 1)
                    need(vec, s_seg, t - 1)
                    st.did(vec.tensor_tensor(x0w[:, par, :], x0, ws[:, P:2 * P], ALU.mult))
                    st.did(vec.tensor_tensor(three(msgs[:, P:D]), three(xs[:, par, P:D]),
                                             ws[:, 2 * P:3 * P].unsqueeze(1).broadcast_to([P, 3, P]), ALU.mult))
                    st.did(vec.tensor_tensor(msgs[:, 0:P], xs[:, par, 0:P], ws[:, 0:P], ALU.mult))
                    vec.wait_ge(s_st, DV * t + 2)
                    st.did(vec.tensor_tensor(dot[:, par, :], dot[:, par, :], ws[:, 3 * P:D], ALU.mult))
                    vec.wait_ge(s_st, DV * t + 4)
                    for c in range(3):
                        m = msgs[:, P * (c + 1):P * (c + 2)]
                        vec.scalar_tensor_tensor(m, x0w[:, par, :], sh[:, t, 1 + c:2 + c], m, ALU.mult, ALU.add)
                    st.wait()
                    vec.tensor_tensor(msgs[:, 0:P], msgs[:, 0:P], dot[:, par, :], ALU.add).then_inc(s_msg, 1)
                    st.end()

                for k in range(B):
                    pair(0, k)
                equals(0, 0)
                for k in range(B, PAIR):
                    pair(0, k)
                hidden(0, 0)

                def body(b):
                    for k in range(EU):
                        if there := at(b, k + PAIR):
                            pair(*there)
                        if k % B == 1 and (there := at(b, k + 3)):
                            equals(*there)
                        message(b, k)
                        if k % B == 2 and (there := at(b, k + 2)):
                            hidden(*there)
                passes(vec, EB, body)

            @block.scalar
            def _(act):
                act.dma_start(w_c[:], io["w_s1"][2 * P:3 * P, :]).then_inc(s_w, 16)
                act.dma_start(w_f1[:], io["w_f1"][:, :]).then_inc(s_w, 16)
                act.dma_start(w_2[0:HID, :], io["w_s2"][:, :]).then_inc(s_w, 16)
                act.dma_start(w_2[HID:2 * HID, :], io["w_f2"][:, :]).then_inc(s_w, 16)
                act.dma_start(sh[:], io["sh"].rearrange("p (t k) -> p t k", k=4)).then_inc(s_w, 16)
                act.preload_act_table_set("natural_log_exp_and_others")
                act.wait_ge(s_w, 80)

                def scaled(b, k):
                    t, par = EU * b + k, k % 2
                    act.wait_ge(s_g[k], 32 * (b + 1))
                    need(act, s_msg, t - 1)
                    act.sem_inc(s_go2, 1)
                    act.activation(xs[:, par, :], srow[:, k % S, 3 * P:SW], ACT.Copy, scale=sh[:, t, 0:1])
                    for c in range(3):
                        ins = act.activation(xd[:, par, P * c:P * (c + 1)], srow[:, k % S, P * (4 + c):P * (5 + c)], ACT.Copy,
                                             scale=sh[:, t, 1 + c:2 + c])
                    ins.then_inc(s_xs, 1)

                def factor(b, k):
                    t, par = EU * b + k, k % 2
                    act.wait_ge(s_wm, t + 1)
                    act.activation(w[:, par, :], pwf[par][:], ACT.Copy).then_inc(s_wf, 1)

                def turn(b, k):
                    q = 4 * b + k // B
                    act.wait_ge(s_ip, B * (q + 1))
                    need(act, s_h, q)
                    act.activation(ipT[:], pip[:], ACT.Copy).then_inc(s_ipT, 1)

                def soften(b, k):
                    q = 4 * b + k // B
                    act.wait_ge(s_h, q + 1)
                    need(act, s_hid, q)
                    act.activation(soft[:], ph[:], ACT.Abs).then_inc(s_soft, 1)
                    act.wait_ge(s_soft, 3 * q + 1)
                    act.activation(soft[:], soft[:], ACT.Exp, scale=-1.0).then_inc(s_soft, 1)
                    act.wait_ge(s_soft, 3 * q + 2)
                    act.activation(soft[:], soft[:], ACT.Ln, scale=0.5, bias=0.5).then_inc(s_soft, 1)

                def rows(b, k):
                    t = EU * b + k
                    act.wait_ge(s_seg, t + 1)
                    need(act, s_add[k % R], 16 * (EU // R * b + k // R))
                    act.activation(out[:, k % R, :], pm[:], ACT.Copy).then_inc(s_row, 1)

                turn(0, 0)
                soften(0, 0)
                scaled(0, 0)
                factor(0, 0)

                def body(b):
                    for k in range(EU):
                        if there := at(b, k - 2):
                            rows(*there)
                        if k % B == 1 and (there := at(b, k + 3)):
                            turn(*there)
                        if k % B == 2 and (there := at(b, k + 2)):
                            soften(*there)
                        if there := at(b, k + 1):
                            scaled(*there)
                            factor(*there)
                passes(act, EB, body)
                rows(EB - 1, EU - 2)
                rows(EB - 1, EU - 1)

            @block.tensor
            def _(pe):
                pe.wait_ge(s_const, 1)
                pe.wait_ge(s_pre, 2)

                def inner(b, k):
                    t = EU * b + k
                    pe.wait_ge(s_prod, t + 1)
                    if k % B == 0:
                        need(pe, s_ipT, 4 * b + k // B)
                    for c in range(3):
                        ins = pe.matmul(pip[:, P * (k % B):P * (k % B + 1)], drow[:, k % SD, P * c:P * (c + 1)], keep.ident[:],
                                        start=c == 0, stop=c == 2)
                    ins.then_inc(s_ip, 1)

                def spread(b, k):
                    q = 4 * b + k // B
                    pe.wait_ge(s_line[k // EH], 16 * (b + 1))
                    need(pe, s_same, q)
                    pe.matmul(pd[:], ones[:], line[:, k // EH, BW * (k // B % 2):BW * (k // B % 2 + 1)],
                              start=True, stop=True).then_inc(s_bc, 1)

                def hidden(b, k):
                    q = 4 * b + k // B
                    pe.wait_ge(s_ipT, q + 1)
                    pe.wait_ge(s_attr[k // EH], 16 * (b + 1))
                    need(pe, s_hid, q)
                    pe.matmul(ph[0:HID, :], w_c[:], ipT[:], start=True, stop=False)
                    pe.matmul(ph[HID:2 * HID, :], w_f1[:], attr[:, k // EH, BW * (k // B % 2):BW * (k // B % 2 + 1)],
                              start=True, stop=True)
                    for n in range(B):
                        ins = pe.matmul(ph[0:HID, P * n:P * (n + 1)], drow[:, (k + n) % SD, 3 * P:DW], keep.ident[:],
                                        start=False, stop=n == B - 1)
                    ins.then_inc(s_h, 1)

                def weights(b, k):
                    t, par, cols = EU * b + k, k // B % 2, slice(P * (k % B), P * (k % B + 1))
                    pe.wait_ge(s_hid, 4 * b + k // B + 1)
                    need(pe, s_w2, t - 1)
                    pe.matmul(pws[k % 2][:], hid[0:HID, par, cols], w_2[0:HID, :], start=True, stop=True)
                    pe.matmul(pwf[k % 2][:], hid[HID:2 * HID, par, cols], w_2[HID:2 * HID, :], start=True, stop=True).then_inc(s_wm, 1)

                def sums(b, k):
                    t = EU * b + k
                    pe.wait_ge(s_same, 4 * b + k // B + 1)
                    pe.wait_ge(s_msg, t + 1)
                    need(pe, s_row, t)
                    pe.matmul(pm[:], same[:, k // B % 2, k % B, :], msg[:, k % 2, :], start=True, stop=True).then_inc(s_seg, 1)

                for k in range(B):
                    inner(0, k)
                spread(0, 0)
                hidden(0, 0)
                for k in range(B, PAIR - 1):
                    inner(0, k)
                weights(0, 0)

                def body(b):
                    for k in range(EU):
                        if there := at(b, k + 1):
                            weights(*there)
                        if there := at(b, k - 1):
                            sums(*there)
                        if there := at(b, k + PAIR - 1):
                            inner(*there)
                        if k % B == 0 and (there := at(b, k + B)):
                            spread(*there)
                        if k % B == 1 and (there := at(b, k + 3)):
                            hidden(*there)
                passes(pe, EB, body)
                sums(EB - 1, EU - 1)


def merge1(nc, io, keep):
    with Stage(nc, "g1") as s:
        w_o0, w_o1, w_p = s.sb("w_o0", [P, P]), s.sb("w_o1", [P, P]), s.sb("w_p", [P, KC, D])
        a0, a1, own, q, o, aT, oT = (s.sb(n, [P, U, D]) for n in ("a0", "a1", "own", "q", "o", "aT", "oT"))
        zo = s.sb("zo", [P, H])
        po, pn, tpa, tpo = s.ps("po", [P, D]), s.ps("pn", [P, H]), s.ps("tpa", [P, D]), s.ps("tpo", [P, D])
        pout = [s.ps(f"pout{k}", [P, D]) for k in range(2)]
        s_w = s.sem("weights")
        s_in = [s.sem(f"in{j}") for j in range(U)]
        s_st, s_own, s_x0, s_agg, s_o, s_po, s_ta, s_to, s_aT, s_oT, s_mm, s_x = (s.sem(n) for n in (
            "steps", "with_own", "x_scalars", "edges", "mixed", "attended", "edgesT", "mixedT", "aT", "oT", "products", "x"))
        with nc.Block() as block:
            @block.sync
            def _(sp):
                def body(i):
                    for j in range(U):
                        n = U * i + j
                        need(sp, s_ta, n - U + 1)
                        need(sp, s_po, n - U + 1)
                        rows = bass.ds(n * P, P)
                        sp.dma_start(a0[:, j, :], io["acc1"][0][rows, :]).then_inc(s_in[j], 16)
                        sp.dma_start(a1[:, j, :], io["acc1"][1][rows, :]).then_inc(s_in[j], 16)
                        sp.dma_start(own[:, j, :], io["srow"][rows, 3 * P:SW]).then_inc(s_in[j], 16)
                        sp.dma_start(q[:, j, :], io["qT"][n]).then_inc(s_in[j], 16)
                passes(sp, NB, body)

            @block.vector
            def _(vec):
                st = Steps(vec, s_st, 2)

                def sum_edges(i, j):
                    n = U * i + j
                    vec.wait_ge(s_in[j], 64 * (i + 1))
                    vec.tensor_tensor(a1[:, j, :], a1[:, j, :], own[:, j, :], ALU.add).then_inc(s_own, 1)
                    vec.wait_ge(s_own, n + 1)
                    vec.tensor_tensor(a0[:, j, :], a0[:, j, :], a1[:, j, :], ALU.add).then_inc(s_agg, 1)

                def norm_mixed(i, j):
                    n = U * i + j
                    st.begin(n)
                    vec.wait_ge(s_po, n + 1)
                    st.did(vec.tensor_scalar(zo[:], pn[:], 1e-6, None, ALU.add))
                    st.wait()
                    st.did(vec.reciprocal(zo[:], zo[:]))
                    st.wait()
                    need(vec, s_to, n - U + 1)
                    vec.tensor_tensor(by_head(o[:, j, :]), by_head(po[:]), over_head(zo[:]), ALU.mult).then_inc(s_o, 1)

                def add(i, j):
                    n = U * i + j
                    vec.wait_ge(s_mm, n + 1)
                    x = keep.X[:, n, :]
                    vec.tensor_tensor(x[:, 0:P], x[:, 0:P], pout[j % 2][:, 0:P], ALU.add).then_inc(s_x0, 1)
                    vectors = x[:, P:D].rearrange("p (u c) -> p c u", c=3)
                    vec.tensor_tensor(vectors, vectors, pout[j % 2][:, P:D].rearrange("p (c u) -> p c u", c=3),
                                      ALU.add).then_inc(s_x, 1)
                    vec.wait_ge(s_x, n + 1)
                    vec.wait_ge(s_x0, n + 1)
                    vec.bn_stats(keep.stats[:, n, :], x)

                sum_edges(0, 0)
                sum_edges(0, 1)
                norm_mixed(0, 0)

                def body(i):
                    for j in range(U):
                        n = U * i + j
                        if not (isinstance(n, int) and n + 2 >= NT):
                            sum_edges(i + (j + 2) // U, (j + 2) % U)
                        if not last_tile(n):
                            norm_mixed(i + (j + 1) // U, (j + 1) % U)
                        add(i, j)
                passes(vec, NB, body)

            @block.scalar
            def _(act):
                act.dma_start(w_o0[:], io["w_o0"][:, :]).then_inc(s_w, 16)
                act.dma_start(w_o1[:], io["w_o1"][:, :]).then_inc(s_w, 16)
                act.dma_start(w_p[:], io["w_proj"].rearrange("(c p) n -> p c n", p=P)).then_inc(s_w, 16)

                def body(i):
                    for j in range(U):
                        n = U * i + j
                        act.wait_ge(s_ta, n + 1)
                        need(act, s_mm, n - U + 1)
                        act.activation(aT[:, j, :], tpa[:], ACT.Copy).then_inc(s_aT, 1)
                        act.wait_ge(s_to, n + 1)
                        act.activation(oT[:, j, :], tpo[:], ACT.Copy).then_inc(s_oT, 1)
                passes(act, NB, body)

            @block.tensor
            def _(pe):
                def edges(i, j):
                    n = U * i + j
                    pe.wait_ge(s_in[j], 64 * (i + 1))
                    need(pe, s_o, n)
                    attend(pe, q[:, j, :], keep.kv, keep.ksum, po, pn).then_inc(s_po, 1)
                    pe.wait_ge(s_agg, n + 1)
                    need(pe, s_aT, n)
                    for c in range(KC):
                        cols = slice(P * c, P * (c + 1))
                        ins = pe.transpose(tpa[:, cols], a0[:, j, cols], keep.ident[:])
                    ins.then_inc(s_ta, 1)

                def mixed(i, j):
                    n = U * i + j
                    pe.wait_ge(s_o, n + 1)
                    need(pe, s_oT, n)
                    for c in range(KC):
                        cols = slice(P * c, P * (c + 1))
                        ins = pe.transpose(tpo[:, cols], o[:, j, cols], keep.ident[:])
                    ins.then_inc(s_to, 1)

                edges(0, 0)
                mixed(0, 0)
                pe.wait_ge(s_w, 48)

                def body(i):
                    for j in range(U):
                        n = U * i + j
                        nxt = (i + (j + 1) // U, (j + 1) % U)
                        if not last_tile(n):
                            edges(*nxt)
                        pe.wait_ge(s_oT, n + 1)
                        need(pe, s_x, n if j == 0 else n - 1)
                        for c in range(KC):
                            pe.matmul(pout[j % 2][:], oT[:, j, P * c:P * (c + 1)], w_p[:, c, :], start=c == 0, stop=False)
                        for c in range(KC):
                            cols = slice(P * c, P * (c + 1))
                            ins = pe.matmul(pout[j % 2][:, cols], aT[:, j, cols], w_o0[:] if c == 0 else w_o1[:],
                                            start=False, stop=c == KC - 1)
                        ins.then_inc(s_mm, 1)
                        if not last_tile(n):
                            mixed(*nxt)
                passes(pe, NB, body)


def route1(nc, io, keep):
    with Stage(nc, "r1") as s:
        xn, xT = s.sb("xn", [P, U, D]), s.sb("xT", [P, U, D])
        sums = s.sb("sums", [P, NT, KC])
        wg, bg, order = s.sb("wg", [P, KC, NX1]), s.sb("bg", [P, NX1]), s.sb("order", [P, NX1])
        mean, l, m, pick = s.sb("mean", [P, KC]), s.sb("l", [P, NX1]), s.sb("m", [P, 4]), s.sb("pick", [P, 2, NX1])
        tp = [s.ps(f"tp{k}", [P, D]) for k in range(2)]
        pl = s.ps("pl", [P, NX1])
        s_w, s_f, s_xn, s_tp, s_xT, s_sum, s_mean, s_l, s_st, s_e = (s.sem(n) for n in (
            "weights", "valid_factors", "normed", "transposed", "xT", "sums", "mean", "logits", "steps", "exps"))
        s_out = [s.sem(f"xT_out{j}") for j in range(U)]
        with nc.Block() as block:
            @block.sync
            def _(sp):
                sp.dma_start(wg[:], io["wg1"].rearrange("(c p) n -> p c n", p=P)).then_inc(s_w, 16)
                sp.dma_start(bg[:], io["bg1"][:, :]).then_inc(s_w, 16)
                sp.dma_start(order[:], io["order"][:, :]).then_inc(s_w, 16)

                def body(i):
                    for j in range(U):
                        sp.wait_ge(s_xT, U * i + j + 1)
                        sp.dma_start(io["xhT"][U * i + j], xT[:, j, :]).then_inc(s_out[j], 16)
                passes(sp, NB, body)
                for j in range(U):
                    sp.wait_ge(s_out[j], 16 * NB)

            @block.scalar
            def _(act):
                def body(i):
                    for j in range(U):
                        n = U * i + j
                        act.wait_ge(s_tp, n + 1)
                        need(act, s_out[j], 16 * i)
                        need(act, s_sum, n - U + 1)
                        act.activation(xT[:, j, :], tp[j % 2][:], ACT.Copy).then_inc(s_xT, 1)
                passes(act, NB, body)
                act.wait_ge(s_st, 4)
                act.activation(l[:], l[:], ACT.Exp).then_inc(s_e, 1)

            @block.vector
            def _(vec):
                vec.tensor_tensor(keep.rstd[:], keep.rstd[:], keep.valid[:], ALU.mult).then_inc(s_f, 1)
                vec.wait_ge(s_f, 1)

                def body(i):
                    for j in range(U):
                        n = U * i + j
                        need(vec, s_tp, n - U + 1)
                        vec.tensor_scalar(xn[:, j, :], keep.X[:, n, :], keep.mean[:, bass.ds(n, 1)],
                                          keep.rstd[:, bass.ds(n, 1)], ALU.subtract, ALU.mult).then_inc(s_xn, 1)
                    for j in range(U):
                        n = U * i + j
                        vec.wait_ge(s_xT, n + 1)
                        vec.tensor_reduce(sums[:, n, :], xT[:, j, :].rearrange("p (c n) -> p c n", c=KC), AX, ALU.add).then_inc(s_sum, 1)
                passes(vec, NB, body)
                st = Steps(vec, s_st, 0)
                st.begin(0)
                vec.wait_ge(s_w, 48)
                vec.wait_ge(s_sum, NT)
                st.did(vec.tensor_reduce(mean[:], sums[:].rearrange("p t c -> p c t"), AX, ALU.add))
                st.wait()
                vec.tensor_scalar(mean[:], mean[:], 1.0 / N, None, ALU.mult).then_inc(s_mean, 1)
                vec.wait_ge(s_l, 1)
                st.did(vec.tensor_tensor(l[:], pl[:], bg[:], ALU.add))
                st.wait()
                st.did(vec.tensor_reduce(m[:, 0:1], l[:], AX, ALU.max))
                st.wait()
                st.did(vec.tensor_scalar(l[:], l[:], m[:, 0:1], None, ALU.subtract))
                vec.wait_ge(s_e, 1)
                st.did(vec.tensor_reduce(m[:, 1:2], l[:], AX, ALU.add))
                st.wait()
                st.did(vec.reciprocal(m[:, 1:2], m[:, 1:2]))
                st.wait()
                st.did(vec.tensor_scalar(l[:], l[:], m[:, 1:2], None, ALU.mult))
                st.wait()
                st.did(vec.tensor_reduce(keep.gate[:], l[:], AX, ALU.max))
                st.wait()
                st.did(vec.tensor_scalar(pick[:, 0, :], l[:], keep.gate[:], float(NX1), ALU.is_lt, ALU.mult))
                st.wait()
                st.did(vec.tensor_tensor(pick[:, 1, :], pick[:, 0, :], order[:], ALU.add))
                st.wait()
                st.did(vec.tensor_reduce(m[:, 2:3], pick[:, 1, :], AX, ALU.min))
                st.wait()
                st.did(vec.tensor_copy(keep.expert[:], m[:, 2:3]))
                st.wait()

            @block.tensor
            def _(pe):
                def body(i):
                    for j in range(U):
                        n = U * i + j
                        pe.wait_ge(s_xn, n + 1)
                        need(pe, s_xT, n if j == 0 else n - 1)
                        for c in range(KC):
                            cols = slice(P * c, P * (c + 1))
                            ins = pe.transpose(tp[j % 2][:, cols], xn[:, j, cols], keep.ident[:])
                        ins.then_inc(s_tp, 1)
                passes(pe, NB, body)
                pe.wait_ge(s_w, 48)
                pe.wait_ge(s_mean, 1)
                for c in range(KC):
                    ins = pe.matmul(pl[:], mean[:, c:c + 1].broadcast_to([P, P]), wg[:, c, :], start=c == 0, stop=c == KC - 1)
                ins.then_inc(s_l, 1)


def linear1(nc, io, keep):
    with Stage(nc, "l1") as s:
        W, be = s.sb("w", [P, KC, D]), s.sb("be", [P, D])
        xT, y, out = s.sb("xT", [P, U, D]), s.sb("y", [P, U, D]), s.sb("out", [P, U, D])
        pout = [s.ps(f"pout{k}", [P, D]) for k in range(U)]
        s_w, s_mm, s_y, s_o = s.sem("weights"), s.sem("products"), s.sem("biased"), s.sem("rows")
        s_x = [s.sem(f"xT_in{j}") for j in range(U)]
        s_out = [s.sem(f"out{j}") for j in range(U)]
        with nc.Block() as block:
            @block.sync
            def _(sp):
                e = sp.value_load(keep.expert[0:1, 0:1], min_val=0, max_val=NX1 - 1)
                sp.dma_start(W[:], io["we"][bass.ds(e, 1)].rearrange("a (c p) n -> p (a c) n", p=P)).then_inc(s_w, 16)
                sp.dma_start(be[:], io["be"][bass.ds(e, 1)].rearrange("a n -> (a n)").partition_broadcast(P)).then_inc(s_w, 16)

                def body(i):
                    for j in range(U):
                        n = U * i + j
                        need(sp, s_mm, n - U + 1)
                        sp.dma_start(xT[:, j, :], io["xhT"][n]).then_inc(s_x[j], 16)
                passes(sp, NB, body)

            @block.tensor
            def _(pe):
                pe.wait_ge(s_w, 32)

                def body(i):
                    for j in range(U):
                        n = U * i + j
                        pe.wait_ge(s_x[j], 16 * (i + 1))
                        need(pe, s_y, n - U + 1)
                        for c in range(KC):
                            ins = pe.matmul(pout[j][:], xT[:, j, P * c:P * (c + 1)], W[:, c, :], start=c == 0, stop=c == KC - 1)
                        ins.then_inc(s_mm, 1)
                passes(pe, NB, body)

            @block.vector
            def _(vec):
                vec.wait_ge(s_w, 32)

                def body(i):
                    for j in range(U):
                        n = U * i + j
                        vec.wait_ge(s_mm, n + 1)
                        need(vec, s_o, n - U + 1)
                        vec.tensor_tensor(y[:, j, :], pout[j][:], be[:], ALU.add).then_inc(s_y, 1)
                        vec.wait_ge(s_y, n + 1)
                        need(vec, s_out[j], 16 * i)
                        vec.scalar_tensor_tensor(out[:, j, :], y[:, j, :], keep.gate[:], keep.X[:, n, :],
                                                 ALU.mult, ALU.add).then_inc(s_o, 1)
                passes(vec, NB, body)

            @block.scalar
            def _(act):
                def body(i):
                    for j in range(U):
                        n = U * i + j
                        act.wait_ge(s_o, n + 1)
                        rows = N - P * (NT - 1) if last_tile(n) else P
                        act.dma_start(io["out"][bass.ds(P * n, rows), :], out[0:rows, j, :]).then_inc(s_out[j], 16)
                passes(act, NB, body)
                for j in range(U):
                    act.wait_ge(s_out[j], 16 * NB)


class Kept:
    pass


def program(nc, io, stop=99):
    with Stage(nc, "keep") as s:
        keep = Kept()
        keep.X = s.sb("x", [P, NT, D])
        keep.ident = s.sb("ident", [P, P])
        keep.stats = s.sb("stats", [P, NT, 6])
        keep.mean, keep.rstd, keep.rstd2 = (s.sb(n, [P, NT]) for n in ("mean", "rstd", "rstd2"))
        keep.valid = s.sb("valid", [P, NT])
        keep.dst, keep.src = s.sb("dst", [P, ET]), s.sb("src", [P, ET])
        todo = [stop]

        def run(stage, *more):
            todo[0] -= 1
            if todo[0] >= 0:
                stage(nc, io, keep, *more)

        run(load_consts)
        run(tables0)
        with Stage(nc, "keep0") as s0:
            keep.kv, keep.ksum = s0.sb("kv", [P, KC, P]), s0.sb("ksum", [P, KC, 2])
            with Stage(nc, "keep1") as s1:
                keep.att, keep.count = s1.sb("att", [P, ET, H]), s1.sb("count", [P, ET])
                run(scores0)
                run(weights0)
                run(messages0)
                run(leads1)
            run(merge0)
        run(norm_rows, "n0")
        with Stage(nc, "keep2") as s2:
            keep.XT, keep.comb = s2.sb("xt", [P, KC, NP]), s2.sb("comb", [P, NT, NX0])
            run(gates0)
            run(experts0)
        run(norm_rows, "n1")
        run(tables1)
        with Stage(nc, "keep3") as s3:
            keep.kv, keep.ksum = s3.sb("kv", [P, KC, P]), s3.sb("ksum", [P, KC, 2])
            run(mixer1)
            run(edges1)
            run(merge1)
        run(norm_rows, "n2")
        with Stage(nc, "keep4") as s4:
            keep.gate, keep.expert = s4.sb("gate", [P, 1]), s4.sb("expert", [P, 1], I32)
            run(route1)
            run(linear1)
        return keep


def layouts(a, np):
    f = np.float32
    pad = ET * P - E

    def bc(v):
        return np.broadcast_to(v, (P, v.shape[-1]))

    def cols(v):
        return v.reshape(-1, P).T

    def blocks(v):
        return v.reshape(EB, EU, P).transpose(0, 2, 1)

    src = np.pad(a["src"], (0, pad), mode="edge")
    dst = np.pad(a["dst"], (0, pad), mode="edge")
    dst_to = np.pad(a["dst"], (0, pad), constant_values=NP - 1)
    src_to = np.pad(a["src"], (0, pad), constant_values=NP - 1)
    qkv = a["L0_mix_qkv_w"].T
    order = np.concatenate([np.arange(P), (P + np.arange(D - P).reshape(P, 3).T).reshape(-1)])
    return {
        "x": np.pad(a["x"], ((0, NP - N), (0, 0))),
        "ident": np.eye(P, dtype=f),
        "valid": (np.arange(NP).reshape(NT, P).T < N).astype(f),
        "dst_rows": dst_to.reshape(P, ET),
        "dst_cols": dst_to.reshape(ET, P).T,
        "src_rows": src_to.reshape(P, ET),
        "src_cols": src_to.reshape(ET, P).T,
        "w_att": np.stack([a["L0_gnn_Wq"], a["L0_gnn_Wk"], a["L0_gnn_Wv"]]),
        "b_att": bc(np.concatenate([a["L0_gnn_bq"], a["L0_gnn_bk"], a["L0_gnn_bv"]])),
        "gamma": cols(a["L0_mix_ln_gamma"]),
        "beta": cols(a["L0_mix_ln_beta"]),
        "dst_ix": blocks(dst),
        "src_ix": blocks(src),
        "half": (np.arange(P)[:, None] // DH == np.arange(2)).astype(f),
        "lower": (np.arange(P)[:, None] > np.arange(P)).astype(f),
        "spare": (SPARE + np.arange(P, dtype=f))[:, None],
        "w_mix0": qkv,
        "bq_mix0": cols(a["L0_mix_qkv_b"][:D]),
        "bkv_mix0": bc(a["L0_mix_qkv_b"][D:]),
        "b_res": bc(a["L0_gnn_bff"]),
        "b_res2": bc(a["L0_mix_out_b"]),
        "w_ff": a["L0_gnn_Wff"],
        "w_out0": a["L0_mix_out_w"].T,
        "wg0": a["L0_ffn_Wg"],
        "bg0": a["L0_ffn_bg"][:, None],
        "lower8": bc((np.arange(NX0)[:, None] > np.arange(NX0)).astype(f).reshape(-1)),
        "w1": a["L0_ffn_W1"],
        "b1": a["L0_ffn_b1"].reshape(NX0, QF // P, P).transpose(0, 2, 1),
        "w2": a["L0_ffn_W2"],
        "b2": a["L0_ffn_b2"],
        "w_pre0": a["L1_gnn_W_pre0"],
        "w_pre1": a["L1_gnn_W_pre1"],
        "w_nd0": a["L1_gnn_W_nd0"],
        "w_nd1": a["L1_gnn_W_nd1"],
        "w_g1": a["L1_gnn_W_g1"],
        "w_g2": a["L1_gnn_W_g2"],
        "b_g": np.stack([cols(a["L1_gnn_b_g1"]), cols(a["L1_gnn_b_g2"])], 1),
        "b_pre0": a["L1_gnn_b_pre0"][:, None],
        "b_nd0": bc(a["L1_gnn_b_nd0"]),
        "w_s1": a["L1_gnn_W_s1"],
        "w_s2": a["L1_gnn_W_s2"],
        "w_f1": a["L1_gnn_W_f1"],
        "w_f2": a["L1_gnn_W_f2"],
        "attr": np.pad(a["edge_attr_32"], ((0, pad), (0, 0))).T,
        "sh": np.pad(a["edge_attr_4"], ((0, pad), (0, 0))).reshape(ET, P, 4).transpose(1, 0, 2).reshape(P, ET * 4),
        "w_o0": a["L1_gnn_W_o0"],
        "w_o1": a["L1_gnn_W_o1"],
        "b_o0": bc(np.pad(a["L1_gnn_b_o0"], (0, D - P))),
        "w_mix1": a["L1_mix_W_qkv"].T[order],
        "w_proj": a["L1_mix_W_proj"].T[:, order],
        "b_proj": bc(a["L1_mix_b_proj"]),
        "wg1": a["L1_ffn_Wg"],
        "bg1": bc(a["L1_ffn_bg"]),
        "order": bc(np.arange(NX1, dtype=f)),
        "we": a["L1_ffn_We"],
        "be": a["L1_ffn_be"],
    }


SCRATCH = {
    "xhT": [NT, P, D],
    "xnT": [NT, P, D],
    "qT": [NT, P, D],
    "srow": [NP, SW],
    "drow": [NP, DW],
}


def tensors(nc, arrays):
    io = {name: nc.dram_tensor(f"in_{name}", v.shape, mybir.dt.from_np(v.dtype), kind="ExternalInput").ap()
          for name, v in arrays.items()}
    for name, shape in SCRATCH.items():
        io[name] = nc.dram_tensor(f"mid_{name}", shape, F32, kind="Internal").ap()
    for name, count, shape in (("att_rows", 3, [NP, D]), ("acc0", NACC, [ACCR, ACCW]), ("acc1", NACC, [ACCR, D])):
        io[name] = [nc.dram_tensor(f"mid_{name}{k}", shape, F32, kind="Internal").ap() for k in range(count)]
    for name in ("dst_l", "src_l"):
        io[name] = nc.dram_tensor(f"mid_{name}", [2, P, ET], BF16, kind="Internal").ap()
    for name in ("lead_ix0", "lead_ix1"):
        io[name] = nc.dram_tensor(f"mid_{name}", [P, ET], I32, kind="Internal").ap()
    io["out"] = nc.dram_tensor("out_0", [N, D], F32, kind="ExternalOutput").ap()
    return io


def kernel(**inputs):
    import numpy as np
    import concourse.bacc as bacc
    from concourse.bass_utils import run_bass_kernel_spmd

    given = {name: np.asarray(v) for name, v in inputs.items()}
    arrays = {name: np.ascontiguousarray(v) for name, v in layouts(given, np).items()}
    nc = bacc.Bacc("TRN2", target_bir_lowering=False, num_devices=1)
    program(nc, tensors(nc, arrays))
    r = run_bass_kernel_spmd(nc, [{f"in_{name}": v for name, v in arrays.items()}], core_ids=[0])
    return r.results[0]["out_0"]
```
